# Optimizing a Trainium2 kernel written in Bass

```python
import numpy as np
import jax
import jax.numpy as jnp

def _softmax(x, axis=-1):
    return jax.nn.softmax(x, axis=axis)

def _gelu(x):
    return jax.nn.gelu(x, approximate=True)

def _silu(x):
    return jax.nn.silu(x)

def _sigmoid(x):
    return jax.nn.sigmoid(x)

def _layernorm(x, axis=-1, eps=1e-05):
    m = jnp.mean(x, axis=axis, keepdims=True)
    v = jnp.var(x, axis=axis, keepdims=True)
    return (x - m) / jnp.sqrt(v + eps)

def _scatter_add(tgt, idx, src, axis=0):
    return tgt.at[idx].add(src)

def _segment_sum(src, seg, n):
    return jax.ops.segment_sum(src, seg, n)
kernel_name = 'mk_prb_d1_jaxref_r8_ecc571'

def setup_inputs(seed: int=0):
    np.random.seed(seed)
    _w = jnp.asarray

    def _L0_attn_setup():
        import jax, jax.numpy as jnp
        import numpy as np
        import math
        N_HEAD = 16
        V_HEAD = 32
        NOPE = 32
        ROPE_D = 64
        KEEP = 32
        EPS = 1e-06

        def _freqs(T, dim=ROPE_D, theta=10000.0):
            f = 1.0 / theta ** (jnp.arange(0, dim, 2, dtype=jnp.float32) / dim)
            t = jnp.arange(T, dtype=jnp.float32)
            a = jnp.outer(t, f)
            return (jnp.cos(a), jnp.sin(a))

        def _rope(x, cos, sin):
            S = x.shape[-2]
            c = cos[:S][None, None]
            s = sin[:S][None, None]
            x1, x2 = jnp.split(x, 2, axis=-1)
            return jnp.concatenate([x1 * c - x2 * s, x1 * s + x2 * c], axis=-1)

        def _rms(x, g, eps=EPS):
            return x * jax.lax.rsqrt(jnp.mean(x * x, axis=-1, keepdims=True) + eps) * g

        def _attn(q, k, v, causal):
            scale = 1.0 / math.sqrt(q.shape[-1])
            s = jnp.einsum('bhqd,bhkd->bhqk', q, k) * scale
            if causal:
                Tq, Tk = (s.shape[-2], s.shape[-1])
                mask = jnp.tril(jnp.ones((Tq, Tk), dtype=bool))
                s = jnp.where(mask, s, jnp.finfo(s.dtype).min)
            return jnp.einsum('bhqk,bhkd->bhqd', jax.nn.softmax(s, axis=-1), v)

        def _forward(x, w_cq, g_qnorm, w_dq_nope, w_dq_rope, w_ckv, g_kvnorm, w_dk_nope, w_dv, w_krope, w_imp, w_selk, w_selv, w_wink, w_winv, w_gate, w_proj):
            B, T, C = x.shape
            cos, sin = _freqs(T)
            nq = _rms(x @ w_cq, g_qnorm)
            q_nope = (nq @ w_dq_nope).reshape(B, T, N_HEAD, NOPE).transpose(0, 2, 1, 3)
            q_rope = (nq @ w_dq_rope).reshape(B, T, N_HEAD, ROPE_D).transpose(0, 2, 1, 3)
            q_rope = _rope(q_rope, cos, sin)
            q = jnp.concatenate([q_nope, q_rope], axis=-1)
            gate = jax.nn.softmax((x @ w_gate).mean(axis=1), axis=-1)
            ckv = _rms(x @ w_ckv, g_kvnorm)
            k_nope = (ckv @ w_dk_nope).reshape(B, T, N_HEAD, NOPE).transpose(0, 2, 1, 3)
            v1 = (ckv @ w_dv).reshape(B, T, N_HEAD, V_HEAD).transpose(0, 2, 1, 3)
            k_rope = (x @ w_krope).reshape(B, T, 1, ROPE_D).transpose(0, 2, 1, 3) / N_HEAD
            k_rope = _rope(k_rope, cos, sin)
            k1 = jnp.concatenate([k_nope, jnp.broadcast_to(k_rope, (B, N_HEAD, T, ROPE_D))], axis=-1)
            scores = (x @ w_imp)[..., 0]
            _, idx = jax.lax.top_k(scores, KEEP)
            idx = jnp.sort(idx, axis=1)
            sel = jnp.take_along_axis(x, idx[:, :, None], axis=1)
            ks = (sel @ w_selk).reshape(B, KEEP, N_HEAD, NOPE + ROPE_D).transpose(0, 2, 1, 3)
            vs = (sel @ w_selv).reshape(B, KEEP, N_HEAD, V_HEAD).transpose(0, 2, 1, 3)
            ks = jnp.concatenate([ks[..., :NOPE], _rope(ks[..., NOPE:], cos, sin)], axis=-1)
            kw = (x @ w_wink).reshape(B, T, N_HEAD, NOPE + ROPE_D).transpose(0, 2, 1, 3)
            vw = (x @ w_winv).reshape(B, T, N_HEAD, V_HEAD).transpose(0, 2, 1, 3)
            kw = jnp.concatenate([kw[..., :NOPE], _rope(kw[..., NOPE:], cos, sin)], axis=-1)
            a1 = _attn(q, k1, v1, causal=True)
            a2 = _attn(q, ks, vs, causal=False)
            a3 = _attn(q, kw, vw, causal=True)
            g = gate[:, :, None, None, None]
            out = g[:, 0] * a1 + g[:, 1] * a2 + g[:, 2] * a3
            out = out.transpose(0, 2, 1, 3).reshape(B, T, N_HEAD * V_HEAD)
            return out @ w_proj
        key = jax.random.key(seed)
        ks = jax.random.split(key, 20)
        B, T, C = (2, 128, 128)
        q_lora, kv_lora = (96, 32)
        std = 0.02

        def w(k, shape):
            return jax.random.normal(k, shape, dtype=jnp.float32) * std
        return {'x': jax.random.normal(ks[0], (B, T, C), dtype=jnp.float32), 'w_cq': w(ks[1], (C, q_lora)), 'g_qnorm': jnp.ones((q_lora,), jnp.float32), 'w_dq_nope': w(ks[2], (q_lora, N_HEAD * NOPE)), 'w_dq_rope': w(ks[3], (q_lora, N_HEAD * ROPE_D)), 'w_ckv': w(ks[4], (C, kv_lora)), 'g_kvnorm': jnp.ones((kv_lora,), jnp.float32), 'w_dk_nope': w(ks[5], (kv_lora, N_HEAD * NOPE)), 'w_dv': w(ks[6], (kv_lora, N_HEAD * V_HEAD)), 'w_krope': w(ks[7], (C, ROPE_D)), 'w_imp': w(ks[8], (C, 1)), 'w_selk': w(ks[9], (C, N_HEAD * (NOPE + ROPE_D))), 'w_selv': w(ks[10], (C, N_HEAD * V_HEAD)), 'w_wink': w(ks[11], (C, N_HEAD * (NOPE + ROPE_D))), 'w_winv': w(ks[12], (C, N_HEAD * V_HEAD)), 'w_gate': w(ks[13], (C, 3)), 'w_proj': w(ks[14], (N_HEAD * V_HEAD, C))}
    _L0_attn_in = _L0_attn_setup()

    def _L0_ffn_setup():
        import jax, jax.numpy as jnp
        import numpy as np
        D_MODEL = 128
        HIDDEN = 256
        N_EXPERTS = 8
        TOP_K = 2
        BATCH = 2
        SEQ = 256
        key = jax.random.key(seed)
        ks = jax.random.split(key, 9)
        s = 0.02
        return {'x': jax.random.normal(ks[0], (BATCH, SEQ, D_MODEL), dtype=jnp.float32), 'w_router': jax.random.normal(ks[1], (D_MODEL, N_EXPERTS), dtype=jnp.float32) * s, 'w1': jax.random.normal(ks[2], (N_EXPERTS, D_MODEL, HIDDEN), dtype=jnp.float32) * s, 'w3': jax.random.normal(ks[3], (N_EXPERTS, D_MODEL, HIDDEN), dtype=jnp.float32) * s, 'w2': jax.random.normal(ks[4], (N_EXPERTS, HIDDEN, D_MODEL), dtype=jnp.float32) * s, 'sw1': jax.random.normal(ks[5], (D_MODEL, HIDDEN), dtype=jnp.float32) * s, 'sw3': jax.random.normal(ks[6], (D_MODEL, HIDDEN), dtype=jnp.float32) * s, 'sw2': jax.random.normal(ks[7], (HIDDEN, D_MODEL), dtype=jnp.float32) * s}
    _L0_ffn_in = _L0_ffn_setup()
    _d = {'L0_attn_x': _L0_attn_in['x'], 'L0_attn_w_cq': _L0_attn_in['w_cq'], 'L0_attn_g_qnorm': _L0_attn_in['g_qnorm'], 'L0_attn_w_dq_nope': _L0_attn_in['w_dq_nope'], 'L0_attn_w_dq_rope': _L0_attn_in['w_dq_rope'], 'L0_attn_w_ckv': _L0_attn_in['w_ckv'], 'L0_attn_g_kvnorm': _L0_attn_in['g_kvnorm'], 'L0_attn_w_dk_nope': _L0_attn_in['w_dk_nope'], 'L0_attn_w_dv': _L0_attn_in['w_dv'], 'L0_attn_w_krope': _L0_attn_in['w_krope'], 'L0_attn_w_imp': _L0_attn_in['w_imp'], 'L0_attn_w_selk': _L0_attn_in['w_selk'], 'L0_attn_w_selv': _L0_attn_in['w_selv'], 'L0_attn_w_wink': _L0_attn_in['w_wink'], 'L0_attn_w_winv': _L0_attn_in['w_winv'], 'L0_attn_w_gate': _L0_attn_in['w_gate'], 'L0_attn_w_proj': _L0_attn_in['w_proj'], 'L0_ffn_w_router': _L0_ffn_in['w_router'], 'L0_ffn_w1': _L0_ffn_in['w1'], 'L0_ffn_w3': _L0_ffn_in['w3'], 'L0_ffn_w2': _L0_ffn_in['w2'], 'L0_ffn_sw1': _L0_ffn_in['sw1'], 'L0_ffn_sw3': _L0_ffn_in['sw3'], 'L0_ffn_sw2': _L0_ffn_in['sw2']}
    _x0 = _d['L0_attn_x']
    _d['L0_attn_x'] = jax.random.normal(jax.random.fold_in(jax.random.key(seed), 1), (16, 256, 128), dtype=_x0.dtype)
    del _x0
    return _d

def reference(L0_attn_x, L0_attn_w_cq, L0_attn_g_qnorm, L0_attn_w_dq_nope, L0_attn_w_dq_rope, L0_attn_w_ckv, L0_attn_g_kvnorm, L0_attn_w_dk_nope, L0_attn_w_dv, L0_attn_w_krope, L0_attn_w_imp, L0_attn_w_selk, L0_attn_w_selv, L0_attn_w_wink, L0_attn_w_winv, L0_attn_w_gate, L0_attn_w_proj, L0_ffn_w_router, L0_ffn_w1, L0_ffn_w3, L0_ffn_w2, L0_ffn_sw1, L0_ffn_sw3, L0_ffn_sw2):

    def _L0_attn_ref(x, w_cq, g_qnorm, w_dq_nope, w_dq_rope, w_ckv, g_kvnorm, w_dk_nope, w_dv, w_krope, w_imp, w_selk, w_selv, w_wink, w_winv, w_gate, w_proj):
        import jax, jax.numpy as jnp
        import numpy as np
        import math
        N_HEAD = 16
        V_HEAD = 32
        NOPE = 32
        ROPE_D = 64
        KEEP = 32
        EPS = 1e-06

        def _freqs(T, dim=ROPE_D, theta=10000.0):
            f = 1.0 / theta ** (jnp.arange(0, dim, 2, dtype=jnp.float32) / dim)
            t = jnp.arange(T, dtype=jnp.float32)
            a = jnp.outer(t, f)
            return (jnp.cos(a), jnp.sin(a))

        def _rope(x, cos, sin):
            S = x.shape[-2]
            c = cos[:S][None, None]
            s = sin[:S][None, None]
            x1, x2 = jnp.split(x, 2, axis=-1)
            return jnp.concatenate([x1 * c - x2 * s, x1 * s + x2 * c], axis=-1)

        def _rms(x, g, eps=EPS):
            return x * jax.lax.rsqrt(jnp.mean(x * x, axis=-1, keepdims=True) + eps) * g

        def _attn(q, k, v, causal):
            scale = 1.0 / math.sqrt(q.shape[-1])
            s = jnp.einsum('bhqd,bhkd->bhqk', q, k) * scale
            if causal:
                Tq, Tk = (s.shape[-2], s.shape[-1])
                mask = jnp.tril(jnp.ones((Tq, Tk), dtype=bool))
                s = jnp.where(mask, s, jnp.finfo(s.dtype).min)
            return jnp.einsum('bhqk,bhkd->bhqd', jax.nn.softmax(s, axis=-1), v)

        def _forward(x, w_cq, g_qnorm, w_dq_nope, w_dq_rope, w_ckv, g_kvnorm, w_dk_nope, w_dv, w_krope, w_imp, w_selk, w_selv, w_wink, w_winv, w_gate, w_proj):
            B, T, C = x.shape
            cos, sin = _freqs(T)
            nq = _rms(x @ w_cq, g_qnorm)
            q_nope = (nq @ w_dq_nope).reshape(B, T, N_HEAD, NOPE).transpose(0, 2, 1, 3)
            q_rope = (nq @ w_dq_rope).reshape(B, T, N_HEAD, ROPE_D).transpose(0, 2, 1, 3)
            q_rope = _rope(q_rope, cos, sin)
            q = jnp.concatenate([q_nope, q_rope], axis=-1)
            gate = jax.nn.softmax((x @ w_gate).mean(axis=1), axis=-1)
            ckv = _rms(x @ w_ckv, g_kvnorm)
            k_nope = (ckv @ w_dk_nope).reshape(B, T, N_HEAD, NOPE).transpose(0, 2, 1, 3)
            v1 = (ckv @ w_dv).reshape(B, T, N_HEAD, V_HEAD).transpose(0, 2, 1, 3)
            k_rope = (x @ w_krope).reshape(B, T, 1, ROPE_D).transpose(0, 2, 1, 3) / N_HEAD
            k_rope = _rope(k_rope, cos, sin)
            k1 = jnp.concatenate([k_nope, jnp.broadcast_to(k_rope, (B, N_HEAD, T, ROPE_D))], axis=-1)
            scores = (x @ w_imp)[..., 0]
            _, idx = jax.lax.top_k(scores, KEEP)
            idx = jnp.sort(idx, axis=1)
            sel = jnp.take_along_axis(x, idx[:, :, None], axis=1)
            ks = (sel @ w_selk).reshape(B, KEEP, N_HEAD, NOPE + ROPE_D).transpose(0, 2, 1, 3)
            vs = (sel @ w_selv).reshape(B, KEEP, N_HEAD, V_HEAD).transpose(0, 2, 1, 3)
            ks = jnp.concatenate([ks[..., :NOPE], _rope(ks[..., NOPE:], cos, sin)], axis=-1)
            kw = (x @ w_wink).reshape(B, T, N_HEAD, NOPE + ROPE_D).transpose(0, 2, 1, 3)
            vw = (x @ w_winv).reshape(B, T, N_HEAD, V_HEAD).transpose(0, 2, 1, 3)
            kw = jnp.concatenate([kw[..., :NOPE], _rope(kw[..., NOPE:], cos, sin)], axis=-1)
            a1 = _attn(q, k1, v1, causal=True)
            a2 = _attn(q, ks, vs, causal=False)
            a3 = _attn(q, kw, vw, causal=True)
            g = gate[:, :, None, None, None]
            out = g[:, 0] * a1 + g[:, 1] * a2 + g[:, 2] * a3
            out = out.transpose(0, 2, 1, 3).reshape(B, T, N_HEAD * V_HEAD)
            return out @ w_proj
        return _forward(x, w_cq, g_qnorm, w_dq_nope, w_dq_rope, w_ckv, g_kvnorm, w_dk_nope, w_dv, w_krope, w_imp, w_selk, w_selv, w_wink, w_winv, w_gate, w_proj)

    def _L0_ffn_ref(x, w_router, w1, w3, w2, sw1, sw3, sw2):
        import jax, jax.numpy as jnp
        import numpy as np
        D_MODEL = 128
        HIDDEN = 256
        N_EXPERTS = 8
        TOP_K = 2
        BATCH = 2
        SEQ = 256
        b, s, d = x.shape
        xf = x.reshape(b * s, d)
        probs = jax.nn.softmax(xf @ w_router, axis=-1)
        top_vals, top_idx = jax.lax.top_k(probs, TOP_K)
        gates = top_vals / jnp.sum(top_vals, axis=-1, keepdims=True)
        onehot = jax.nn.one_hot(top_idx, N_EXPERTS, dtype=xf.dtype)
        cw = jnp.einsum('tk,tke->te', gates, onehot)
        h1 = jnp.einsum('td,edh->eth', xf, w1)
        h3 = jnp.einsum('td,edh->eth', xf, w3)
        y = jnp.einsum('eth,ehd->etd', jax.nn.silu(h1) * h3, w2)
        out = jnp.einsum('etd,te->td', y, cw)
        out = out + jax.nn.silu(xf @ sw1) * (xf @ sw3) @ sw2
        return out.reshape(b, s, d)
    x = L0_attn_x
    xn = _layernorm(x, axis=-1)
    x = x + _L0_attn_ref(xn, L0_attn_w_cq, L0_attn_g_qnorm, L0_attn_w_dq_nope, L0_attn_w_dq_rope, L0_attn_w_ckv, L0_attn_g_kvnorm, L0_attn_w_dk_nope, L0_attn_w_dv, L0_attn_w_krope, L0_attn_w_imp, L0_attn_w_selk, L0_attn_w_selv, L0_attn_w_wink, L0_attn_w_winv, L0_attn_w_gate, L0_attn_w_proj) + _L0_ffn_ref(xn, L0_ffn_w_router, L0_ffn_w1, L0_ffn_w3, L0_ffn_w2, L0_ffn_sw1, L0_ffn_sw3, L0_ffn_sw2)
    return x

_drawn_inputs = setup_inputs


def setup_inputs(seed=0):
    import zlib

    import numpy as np

    out = dict(_drawn_inputs(seed))
    spreads = {'L0_attn_g_qnorm': (1.0, 0.6), 'L0_attn_g_kvnorm': (1.0, 0.6)}
    factors = {'L0_attn_w_cq': 8.0,
     'L0_attn_w_dq_nope': 8.0,
     'L0_attn_w_dq_rope': 8.0,
     'L0_attn_w_ckv': 8.0,
     'L0_attn_w_dk_nope': 8.0,
     'L0_attn_w_dv': 8.0,
     'L0_attn_w_krope': 64.0,
     'L0_attn_w_imp': 7.527,
     'L0_attn_w_selk': 8.0,
     'L0_attn_w_selv': 7.104,
     'L0_attn_w_wink': 8.0,
     'L0_attn_w_winv': 8.0,
     'L0_attn_w_gate': 8.0,
     'L0_attn_w_proj': 5.743,
     'L0_ffn_w_router': 8.0,
     'L0_ffn_w1': 8.0,
     'L0_ffn_w3': 8.0,
     'L0_ffn_w2': 8.0,
     'L0_ffn_sw1': 6.903,
     'L0_ffn_sw3': 6.815,
     'L0_ffn_sw2': 6.825}
    for name, (base, spread) in spreads.items():
        noise = np.random.default_rng([zlib.crc32(name.encode()), seed]).standard_normal(out[name].shape)
        drawn = base * np.exp(spread * noise) if base else spread * noise
        out[name] = jnp.asarray(drawn.astype(out[name].dtype))
    for name, factor in factors.items():
        out[name] = (out[name] * factor).astype(out[name].dtype)
    return out
```

```python
from contextlib import ExitStack

import concourse.bass as bass
from concourse import mybir

F32 = mybir.dt.float32
F32R = mybir.dt.float32r
BF16 = mybir.dt.bfloat16
ALU = mybir.AluOpType
ACT = mybir.ActivationFunctionType
X = mybir.AxisListType.X

B, T, C = 16, 256, 128
P = 128
NT = T // P
H, HG = 16, 4
G = H // HG
NOPE, ROPE, VH = 32, 64, 32
HALF = ROPE // 2
D = NOPE + ROPE
QL, KL = 96, 32
KEEP = 32
QC = HG * D
GC = QC + HG * VH
E1 = 9
NE = E1 - 1
HID = 256
HC = HID // P
BT = 4
NBLK = B * T // (BT * P)
BTOK = BT * P
SPB = B // (BTOK // T) and BTOK // T
A_CKV, A_KR, A_IMP, A_GATE, A_ROUT = QL, QL + KL, QL + KL + ROPE, QL + KL + ROPE + 1, QL + KL + ROPE + 4
A_N = A_ROUT + NE
EPS_LN, EPS_RMS = 1e-5, 1e-6
SCALE = float(D) ** -0.5
NEG = -1e30
BR1, BR3, BR2 = 0, 1, 2

CONST_COLS = {}


def _layout():
    at = 0
    for name, n in [("ident", P), ("cos", NT * ROPE), ("sin", NT * ROPE), ("scos", ROPE), ("ssin", ROPE),
                    ("mask", T), ("mrow", 3), ("iota", KEEP), ("tri", NE * NE), ("block", P),
                    ("mean", P), ("ones", VH), ("eps", 2)]:
        CONST_COLS[name] = (at, n)
        at += n
    return at


NCONST = _layout()


def constants(np):
    c = np.zeros((P, NCONST), np.float32)

    def put(name, a):
        at, n = CONST_COLS[name]
        c[:, at:at + n] = np.asarray(a, np.float32).reshape(P, n)

    inv = (np.float32(1.0) / np.float32(10000.0) ** (np.arange(0, ROPE, 2, dtype=np.float32) / np.float32(ROPE))).astype(np.float32)
    ang = np.outer(np.arange(T, dtype=np.float32), inv).astype(np.float32)
    cos, sin = np.cos(ang), np.sin(ang)
    two_c, two_s = np.concatenate([cos, cos], 1), np.concatenate([-sin, sin], 1)
    p = np.arange(P)
    put("ident", np.eye(P))
    put("cos", two_c.reshape(NT, P, ROPE).transpose(1, 0, 2))
    put("sin", two_s.reshape(NT, P, ROPE).transpose(1, 0, 2))
    put("scos", two_c[p % KEEP])
    put("ssin", two_s[p % KEEP])
    put("mask", np.where(np.arange(T)[None, :] <= p[:, None] + T - P, 0.0, NEG))
    put("mrow", np.where(p[:, None] == D + np.arange(3)[None, :], -1.0, 0.0))
    put("iota", np.broadcast_to(np.arange(1, KEEP + 1), (P, KEEP)))
    e = np.arange(NE)
    put("tri", np.broadcast_to((e[None, :] < e[:, None]).reshape(1, -1), (P, NE * NE)))
    put("block", (p[:, None] // KEEP == p[None, :] // VH))
    put("mean", np.full((P, P), 1.0 / T))
    put("ones", np.ones((P, VH)))
    put("eps", np.broadcast_to([EPS_LN, EPS_RMS], (P, 2)))
    return c


def wait_alone(eng, semaphore, value, passed):
    eng.wait_ge(semaphore, value)
    eng.sem_inc(passed, 1)


def layer_kernel(nc, a, out):
    ctx = ExitStack()
    with ctx:
        def sem(name):
            return ctx.enter_context(nc.semaphore(name))

        def keep(name, shape, dt=F32):
            return ctx.enter_context(nc.sbuf_tensor(name, shape, dt))

        dram = lambda name, shape: nc.dram_tensor(name, shape, F32, kind="Internal").ap()
        xt_d = dram("xt_d", (B, C, 2, T))
        nt_d = dram("nt_d", (B, P, 2, T))
        kr_d = dram("kr_d", (B, ROPE, T))
        res_d = dram("res_d", (B * T, C))
        ks_d = dram("ks_d", (B, P, H * KEEP))
        vs_d = dram("vs_d", (B, KEEP, H * VH))

        const = keep("const", [P, NCONST])
        misc = keep("misc", [P, B * NT, 4])
        xn_all = keep("xn_all", [P, B * NT, C])
        gates = keep("gates", [P, B, 3])

        def cst(name):
            at, n = CONST_COLS[name]
            return const[:, at:at + n]

        const_in = sem("const_in")
        mixture(nc, ctx, a, sem, cst, const, const_in, misc, xn_all, xt_d, nt_d, kr_d, res_d)
        select(nc, a, sem, cst, misc, xn_all, gates, ks_d, vs_d)
        attend(nc, a, sem, cst, gates, xt_d, nt_d, kr_d, res_d, ks_d, vs_d, out)


def mixture(nc, octx, a, sem, cst, const, const_in, misc, xn_all, xt_d, nt_d, kr_d, res_d):
    ctx = ExitStack()
    with ctx:
        def sb(name, shape, dt=F32):
            return ctx.enter_context(nc.sbuf_tensor(name, shape, dt))

        def ps(name, shape, dt=F32):
            return ctx.enter_context(nc.psum_tensor(name, shape, dt))

        w13_raw = sb("w13_raw", [P, 2, 2, HID])
        w13 = sb("w13", [P, 2, E1, 2, HID], F32R)
        w2 = sb("w2", [P, E1, HC, C])
        wa = sb("wa", [P, A_N])
        xb = sb("xb", [P, 2, BT, C])
        stats = sb("stats", [P, BT, 6])
        mv = sb("mv", [P, BT, 2])
        std = sb("std", [P, BT])
        rstd = sb("rstd", [P, BT])
        xn = sb("xn", [P, BT, C])
        xt = sb("xt", [P, BTOK])
        xhl = [sb(f"xhl{i}", [P, 2, BTOK], F32R) for i in range(2)]
        sqj = sb("sqj", [P, BT, P])
        ssq = sb("ssq", [P, 2, BT])
        sstd = sb("sstd", [P, 2, BT])
        rr = sb("rr", [P, 2, BT])
        nqc = sb("nqc", [P, BT, P])
        nhl = [sb(f"nhl{i}", [P, 2, BTOK], F32R) for i in range(2)]
        kcos = sb("kcos", [P, BT, ROPE])
        ksin = sb("ksin", [P, BT, ROPE])
        kr = sb("kr", [P, BT, ROPE])
        krt = [sb(f"krt{i}", [ROPE, BTOK]) for i in range(2)]
        rmx = sb("rmx", [P, BT])
        rd = sb("rd", [P, BT, NE])
        rex = sb("rex", [P, BT, NE])
        rsum = sb("rsum", [P, BT])
        rrec = sb("rrec", [P, BT])
        rp = sb("rp", [P, BT, NE])
        rgt = sb("rgt", [P, BT, NE, NE])
        req = sb("req", [P, BT, NE, NE])
        rank = sb("rank", [P, BT, NE])
        rsel = sb("rsel", [P, BT, NE])
        rs2 = sb("rs2", [P, BT])
        rr2 = sb("rr2", [P, BT])
        cw = [sb(f"cw{i}", [P, BT, NE]) for i in range(2)]
        silu = sb("silu", [P, HC, BTOK])
        hid = sb("hid", [P, 2, HC, BTOK])
        acc = sb("acc", [P, 2, BT, C])

        pf = ps("pf", [P, 2, 512])
        ph = ps("ph", [P, 2 * HC, 512])
        py = ps("py", [P, 2, 512])
        pa = pf[:, :, :].rearrange("p b (t c) -> p (b t) c", c=256)

        names = ("w2_in wa_in raw_free w_hi w_lo wa_scaled bn var ln_std ln_rstd xn_ready xn_kept "
                 "xT_ps xt_ready xh_ready xl_ready a_ps sq rms_std misc_ready rr_ready nq_ready kr_part kr_ready "
                 "rmax rdiff rexp rchain cw_ready a_used nT_ps krT_ps nh_ready nl_ready krt_ready "
                 "h_ps silu_ready hid_ready y_ps acc_ready gate").split()
        s = {n: sem("m_" + n) for n in names}
        w_in = [sem(f"m_w_in{i}") for i in range(2)]
        x_in = [sem(f"m_x_in{i}") for i in range(2)]
        xt_out = [sem(f"m_xt_out{i}") for i in range(2)]
        nt_out = [sem(f"m_nt_out{i}") for i in range(2)]
        kr_out = [sem(f"m_kr_out{i}") for i in range(2)]
        acc_out = [sem(f"m_acc_out{i}") for i in range(2)]

        x_v = a["L0_attn_x"].rearrange("b (t p) c -> p (b t) c", p=P)
        res_v = res_d.rearrange("(n p) c -> p n c", p=P)
        ident = cst("ident")

        def w_src(e):
            if e < NE:
                return a["L0_ffn_w1"][e], a["L0_ffn_w3"][e]
            return a["L0_ffn_sw1"], a["L0_ffn_sw3"]

        def half(k, par):
            return k

        with nc.Block() as block:
            @block.sync
            def _(sp):
                for n in range(2):
                    sp.sem_inc(xt_out[n], 16 * SPB)
                    sp.sem_inc(nt_out[n], 16 * SPB)
                    sp.sem_inc(kr_out[n], 16 * SPB)
                    sp.sem_inc(acc_out[n], 16)
                sp.dma_start(const[:, :], a["constants"]).then_inc(const_in, 16)
                for n in range(2):
                    sp.dma_start(xb[:, n], x_v[:, n * BT:(n + 1) * BT, :]).then_inc(x_in[n], 16)
                for at, name, n in [(0, "L0_attn_w_cq", QL), (A_CKV, "L0_attn_w_ckv", KL), (A_KR, "L0_attn_w_krope", ROPE),
                                    (A_IMP, "L0_attn_w_imp", 1), (A_GATE, "L0_attn_w_gate", 3), (A_ROUT, "L0_ffn_w_router", NE)]:
                    sp.dma_start(wa[:, at:at + n], a[name]).then_inc(s["wa_in"], 16)
                for e in range(E1):
                    if e >= 2:
                        sp.wait_ge(s["w_lo"], e - 1)
                    for j, src in enumerate(w_src(e)):
                        sp.dma_start(w13_raw[:, e % 2, j, :], src).then_inc(w_in[e % 2], 16)
                    src = a["L0_ffn_w2"][e] if e < NE else a["L0_ffn_sw2"]
                    sp.dma_start(w2[:, e], src.rearrange("(c p) d -> p c d", p=P)).then_inc(s["w2_in"], 16)

                def store(f, par):
                    sp.wait_ge(s["xl_ready"], f + 1)
                    for q in range(SPB):
                        sp.dma_start(xt_d[f * SPB + q], xhl[par][:, :, q * T:(q + 1) * T].bitcast(F32)).then_inc(xt_out[par], 16)
                    sp.wait_ge(s["nl_ready"], f + 2)
                    for q in range(SPB):
                        sp.dma_start(nt_d[f * SPB + q], nhl[par][:, :, q * T:(q + 1) * T].bitcast(F32)).then_inc(nt_out[par], 16)
                    sp.wait_ge(s["krt_ready"], f + 2)
                    for q in range(SPB):
                        sp.dma_start(kr_d[f * SPB + q], krt[par][:, q * T:(q + 1) * T]).then_inc(kr_out[par], 16)

                def body(j, last):
                    for par in range(2):
                        k = j * 2 + par
                        if not last:
                            sp.wait_ge(s["acc_ready"], k * E1 + 3)
                            sp.dma_start(xb[:, par], x_v[:, bass.ds((k + 2) * BT, BT), :]).then_inc(x_in[par], 16)
                        if not (last and par):
                            store(k + 1, 1 - par)
                        sp.wait_ge(s["acc_ready"], k * E1 + E1 + 2)
                        sp.dma_start(res_v[:, bass.ds(k * BT, BT), :], acc[:, par]).then_inc(acc_out[par], 16)

                store(0, 0)
                with sp.Fori(0, NBLK // 2 - 1) as j:
                    body(j, False)
                body(NBLK // 2 - 1, True)
                for n in range(2):
                    sp.wait_ge(xt_out[n], 16 * SPB * (NBLK // 2 + 1))
                    sp.wait_ge(nt_out[n], 16 * SPB * (NBLK // 2 + 1))
                    sp.wait_ge(kr_out[n], 16 * SPB * (NBLK // 2 + 1))
                    sp.wait_ge(acc_out[n], 16 * (NBLK // 2 + 1))

            @block.scalar
            def _(act):
                act.wait_ge(s["wa_in"], 16 * 6)
                nc.scalar.mul(wa[:, A_KR:A_KR + ROPE], wa[:, A_KR:A_KR + ROPE], 1.0 / H).then_inc(s["wa_scaled"], 1)

                def norm_std(f):
                    act.wait_ge(const_in, 16)
                    act.wait_ge(s["var"], f * BT + BT)
                    nc.scalar.activation(std[:, :], mv[:, :, 1], ACT.Sqrt, bias=cst("eps")[:, 0:1]).then_inc(s["ln_std"], 1)

                def keep_xn(f):
                    act.wait_ge(s["xn_ready"], f * BT + BT)
                    nc.scalar.copy(xn_all[:, bass.ds(f * BT, BT), :], xn[:, :, :]).then_inc(s["xn_kept"], 1)

                def split_x(f, par, uses):
                    act.wait_ge(s["xT_ps"], f + 1)
                    nc.scalar.copy(xt[:, :], pf[:, 1, :]).then_inc(s["xt_ready"], 1)
                    act.wait_ge(xt_out[par], 16 * SPB * (uses + 1))
                    nc.scalar.copy(xhl[par][:, 0, :], pf[:, 1, :]).then_inc(s["xh_ready"], 1)

                def small(f):
                    act.wait_ge(s["a_ps"], f + 1)
                    for t in range(BT):
                        nc.scalar.activation(sqj[:, t, 0:QL], pa[:, t, 0:QL], ACT.Square, accum_out=ssq[:, 0, t:t + 1]).then_inc(s["sq"], 1)
                        nc.scalar.activation(sqj[:, t, QL:P], pa[:, t, A_CKV:A_CKV + KL], ACT.Square, accum_out=ssq[:, 1, t:t + 1]).then_inc(s["sq"], 1)
                    nc.scalar.copy(misc[:, bass.ds(f * BT, BT), :], pa[:, :, A_IMP:A_IMP + 4]).then_inc(s["misc_ready"], 1)
                    act.wait_ge(s["sq"], f * 2 * BT + 2 * BT)
                    nc.scalar.activation(sstd[:, 0, :], ssq[:, 0, :], ACT.Sqrt, bias=cst("eps")[:, 1:2], scale=1.0 / QL).then_inc(s["rms_std"], 1)
                    nc.scalar.activation(sstd[:, 1, :], ssq[:, 1, :], ACT.Sqrt, bias=cst("eps")[:, 1:2], scale=1.0 / KL).then_inc(s["rms_std"], 1)
                    act.wait_ge(s["rdiff"], f + 1)
                    nc.scalar.activation(rex[:, :, :], rd[:, :, :], ACT.Exp).then_inc(s["rexp"], 1)

                def split_n(f, par, uses):
                    act.wait_ge(s["nT_ps"], f + 1)
                    act.wait_ge(nt_out[par], 16 * SPB * (uses + 1))
                    nc.scalar.copy(nhl[par][:, 0, :], pf[:, 0, :]).then_inc(s["nh_ready"], 1)
                    act.wait_ge(s["krT_ps"], f + 1)
                    act.wait_ge(kr_out[par], 16 * SPB * (uses + 1))
                    nc.scalar.copy(krt[par][:, :], pf[0:ROPE, 1, :]).then_inc(s["krt_ready"], 1)

                def silus(k, e):
                    for c in range(HC):
                        n = k * (E1 * HC) + e * HC + c
                        act.wait_ge(s["h_ps"], n + 1)
                        act.wait_ge(s["hid_ready"], n + 1)
                        nc.scalar.activation(silu[:, c, :], ph[:, 2 * c, :], ACT.Silu).then_inc(s["silu_ready"], 1)

                def body(j, last):
                    for par in range(2):
                        k = j * 2 + par
                        front = not (last and par)
                        f, fp, uses = k + 1, 1 - par, j + par
                        for e in range(E1):
                            silus(k, e)
                            if not front:
                                continue
                            if e == 0:
                                norm_std(f)
                            if e == 1:
                                keep_xn(f)
                            if e == 2:
                                split_x(f, fp, uses)
                            if e == 4:
                                small(f)
                            if e == 8:
                                split_n(f, fp, uses)

                norm_std(0)
                act.sem_inc(s["krt_ready"], 1)
                keep_xn(0)
                split_x(0, 0, 0)
                small(0)
                split_n(0, 0, 0)
                for e in range(E1):
                    act.wait_ge(w_in[e % 2], 32 * (e // 2 + 1))
                    nc.scalar.copy(w13[:, 0, e], w13_raw[:, e % 2]).then_inc(s["w_hi"], 1)
                with act.Fori(0, NBLK // 2 - 1) as j:
                    body(j, False)
                body(NBLK // 2 - 1, True)

            @block.vector
            def _(dve):
                def norm_stats(f, par, uses):
                    dve.wait_ge(x_in[par], 16 * (uses + 1))
                    for t in range(BT):
                        nc.vector.bn_stats(stats[:, t, :], xb[:, par, t, :]).then_inc(s["bn"], 1)
                    wait_alone(dve, s["bn"], f * BT + BT, s["gate"])
                    for t in range(BT):
                        nc.vector.bn_aggr(mv[:, t, :], stats[:, t, :]).then_inc(s["var"], 1)

                def norm_apply(f, par):
                    dve.wait_ge(s["ln_std"], f + 1)
                    nc.vector.reciprocal(rstd[:, :], std[:, :]).then_inc(s["ln_rstd"], 1)
                    dve.wait_ge(s["ln_rstd"], f + 1)
                    for t in range(BT):
                        nc.vector.tensor_scalar(xn[:, t, :], xb[:, par, t, :], mv[:, t, 0:1], rstd[:, t:t + 1],
                                                ALU.subtract, ALU.mult).then_inc(s["xn_ready"], 1)

                def x_lo(f, par):
                    dve.wait_ge(s["xh_ready"], f + 1)
                    nc.vector.tensor_tensor(xhl[par][:, 1, :], pf[:, 1, :], xhl[par][:, 0, :].bitcast(F32), ALU.subtract).then_inc(s["xl_ready"], 1)

                def chain(f, n, ins):
                    ins.then_inc(s["rchain"], 1)
                    dve.wait_ge(s["rchain"], f * 9 + n)

                def small(f, par):
                    dve.wait_ge(s["misc_ready"], f + 1)
                    nc.vector.tensor_reduce(rmx[:, :], pa[:, :, A_ROUT:A_N], X, ALU.max).then_inc(s["rmax"], 1)
                    dve.wait_ge(s["rmax"], f + 1)
                    nc.vector.tensor_tensor(rd[:, :, :], pa[:, :, A_ROUT:A_N], rmx[:, :].unsqueeze(2).to_broadcast([P, BT, NE]),
                                            ALU.subtract).then_inc(s["rdiff"], 1)
                    for q in range(SPB):
                        t = slice(q * NT, (q + 1) * NT)
                        src = pa[:, t, A_KR:A_KR + ROPE]
                        nc.vector.tensor_tensor(kcos[:, t, :], src, cst("cos").rearrange("p (t c) -> p t c", c=ROPE), ALU.mult).then_inc(s["kr_part"], 1)
                        nc.vector.tensor_tensor(ksin[:, t, :].rearrange("p t (a c) -> p t a c", a=2),
                                                src.rearrange("p t (a c) -> p t a c", a=2)[:, :, ::-1, :],
                                                cst("sin").rearrange("p (t a c) -> p t a c", a=2, c=HALF), ALU.mult).then_inc(s["kr_part"], 1)
                    dve.wait_ge(s["rms_std"], f * 2 + 2)
                    nc.vector.reciprocal(rr[:, :, :], sstd[:, :, :]).then_inc(s["rr_ready"], 1)
                    dve.wait_ge(s["rr_ready"], f + 1)
                    nc.vector.tensor_tensor(nqc[:, :, 0:QL], pa[:, :, 0:QL], rr[:, 0, :].unsqueeze(2).to_broadcast([P, BT, QL]),
                                            ALU.mult).then_inc(s["nq_ready"], 1)
                    nc.vector.tensor_tensor(nqc[:, :, QL:P], pa[:, :, A_CKV:A_CKV + KL], rr[:, 1, :].unsqueeze(2).to_broadcast([P, BT, KL]),
                                            ALU.mult).then_inc(s["nq_ready"], 1)
                    dve.wait_ge(s["kr_part"], f * (2 * SPB) + 2 * SPB)
                    nc.vector.tensor_tensor(kr[:, :, :], kcos[:, :, :], ksin[:, :, :], ALU.add).then_inc(s["kr_ready"], 1)
                    dve.wait_ge(s["rexp"], f + 1)
                    chain(f, 1, nc.vector.tensor_reduce(rsum[:, :], rex[:, :, :], X, ALU.add))
                    chain(f, 2, nc.vector.reciprocal(rrec[:, :], rsum[:, :]))
                    chain(f, 3, nc.vector.tensor_tensor(rp[:, :, :], rex[:, :, :], rrec[:, :].unsqueeze(2).to_broadcast([P, BT, NE]), ALU.mult))
                    other = rp[:, :, :].unsqueeze(2).to_broadcast([P, BT, NE, NE])
                    own = rp[:, :, :].unsqueeze(3).to_broadcast([P, BT, NE, NE])
                    chain(f, 4, nc.vector.tensor_tensor(req[:, :, :, :], other, own, ALU.is_equal))
                    tri = cst("tri").unsqueeze(1).to_broadcast([P, BT, NE * NE])
                    chain(f, 5, nc.vector.tensor_tensor(rgt[:, :, :, :].rearrange("p t e f -> p t (e f)"),
                                                        req[:, :, :, :].rearrange("p t e f -> p t (e f)"), tri, ALU.mult))
                    chain(f, 6, nc.vector.tensor_tensor(req[:, :, :, :], other, own, ALU.is_gt))
                    chain(f, 7, nc.vector.tensor_tensor(rgt[:, :, :, :], rgt[:, :, :, :], req[:, :, :, :], ALU.add))
                    chain(f, 8, nc.vector.tensor_reduce(rank[:, :, :], rgt[:, :, :, :], X, ALU.add))
                    chain(f, 9, nc.vector.scalar_tensor_tensor(rsel[:, :, :], rank[:, :, :], 1.5, rp[:, :, :], ALU.is_lt, ALU.mult))
                    nc.vector.tensor_reduce(rs2[:, :], rsel[:, :, :], X, ALU.add).then_inc(s["cw_ready"], 1)
                    dve.wait_ge(s["cw_ready"], f * 3 + 1)
                    nc.vector.reciprocal(rr2[:, :], rs2[:, :]).then_inc(s["cw_ready"], 1)
                    dve.wait_ge(s["cw_ready"], f * 3 + 2)
                    nc.vector.tensor_tensor(cw[par][:, :, :], rsel[:, :, :], rr2[:, :].unsqueeze(2).to_broadcast([P, BT, NE]),
                                            ALU.mult).then_inc(s["cw_ready"], 1)

                def n_lo(f, par):
                    dve.wait_ge(s["nh_ready"], f + 1)
                    nc.vector.tensor_tensor(nhl[par][:, 1, :], pf[:, 0, :], nhl[par][:, 0, :].bitcast(F32), ALU.subtract).then_inc(s["nl_ready"], 1)

                def hidden(k, e, par):
                    for c in range(HC):
                        n = k * (E1 * HC) + e * HC + c
                        dve.wait_ge(s["silu_ready"], n + 1)
                        if c == 0:
                            dve.wait_ge(s["y_ps"], k * E1 + e + 1)
                        nc.vector.tensor_tensor(hid[:, (par + e) % 2, c, :], ph[:, 2 * c + 1, :], silu[:, c, :],
                                                ALU.mult).then_inc(s["hid_ready"], 1)

                def accumulate(k, e, par, uses):
                    m = k * E1 + e
                    dve.wait_ge(s["y_ps"], m + 3)
                    dve.wait_ge(s["acc_ready"], m + 2)
                    if e == 0:
                        dve.wait_ge(s["cw_ready"], k * 3 + 3)
                        dve.wait_ge(acc_out[par], 16 * (uses + 1))
                    y = py[:, (par + e) % 2, :].rearrange("p (t c) -> p t c", c=C)
                    if e == NE:
                        nc.vector.tensor_tensor(acc[:, par], y, acc[:, par], ALU.add).then_inc(s["acc_ready"], 1)
                        return
                    so_far = xb if e == 0 else acc
                    for t in range(BT):
                        ins = nc.vector.scalar_tensor_tensor(acc[:, par, t, :], y[:, t, :], cw[par][:, t, e:e + 1], so_far[:, par, t, :],
                                                             ALU.mult, ALU.add)
                    ins.then_inc(s["acc_ready"], 1)

                def body(j, last):
                    for par in range(2):
                        k = j * 2 + par
                        front = not (last and par)
                        f, fp, uses = k + 1, 1 - par, j + par
                        if front:
                            norm_stats(f, fp, uses)
                        for e in range(E1):
                            hidden(k, e, par)
                            if e:
                                accumulate(k, e - 1, par, j)
                            if not front:
                                continue
                            if e == 0:
                                norm_apply(f, fp)
                            if e == 2:
                                x_lo(f, fp)
                            if e == 4:
                                small(f, fp)
                        if front:
                            n_lo(f, fp)
                        accumulate(k, E1 - 1, par, j)

                dve.sem_inc(s["hid_ready"], 2)
                dve.sem_inc(s["acc_ready"], 2)
                dve.sem_inc(s["nl_ready"], 1)
                norm_stats(0, 0, 0)
                norm_apply(0, 0)
                x_lo(0, 0)
                small(0, 0)
                n_lo(0, 0)
                for e in range(E1):
                    dve.wait_ge(s["w_hi"], e + 1)
                    nc.vector.tensor_tensor(w13[:, 1, e], w13_raw[:, e % 2], w13[:, 0, e].bitcast(F32), ALU.subtract).then_inc(s["w_lo"], 1)
                with dve.Fori(0, NBLK // 2 - 1) as j:
                    body(j, False)
                body(NBLK // 2 - 1, True)

            @block.tensor
            def _(pe):
                def x_transposes(f):
                    pe.wait_ge(s["xn_ready"], f * BT + BT)
                    pe.wait_ge(s["krt_ready"], f + 1)
                    for t in range(BT):
                        last = nc.tensor.transpose(pf[:, 1, t * P:(t + 1) * P], xn[:, t, :], ident)
                    last.then_inc(s["xT_ps"], 1)

                def small(f):
                    pe.wait_ge(s["xt_ready"], f + 1)
                    pe.wait_ge(s["nl_ready"], f + 1)
                    for t in range(BT):
                        if t == BT // 2:
                            pe.wait_ge(s["xl_ready"], f + 1)
                        last = nc.tensor.matmul(pa[:, t, 0:A_N], xt[:, t * P:(t + 1) * P], wa[:, :], start=True, stop=True)
                    last.then_inc(s["a_ps"], 1)

                def n_transposes(f):
                    pe.wait_ge(s["nq_ready"], f * 2 + 2)
                    pe.wait_ge(s["misc_ready"], f + 1)
                    pe.wait_ge(s["kr_ready"], f + 1)
                    for t in range(BT):
                        last = nc.tensor.transpose(pf[:, 0, t * P:(t + 1) * P], nqc[:, t, :], ident)
                    last.then_inc(s["nT_ps"], 1)
                    for t in range(BT):
                        last = nc.tensor.transpose(pf[0:ROPE, 1, t * P:(t + 1) * P], kr[:, t, :], ident)
                    last.then_inc(s["krT_ps"], 1)

                def up(k, e, par):
                    for c in range(HC):
                        pe.wait_ge(s["hid_ready"], k * (E1 * HC) + e * HC + c + 1)
                        for j in range(2):
                            w = [w13[:, hl, e, j, c * P:(c + 1) * P] for hl in range(2)]
                            x = [xhl[par][:, hl, :] for hl in range(2)]
                            for n, (wi, xi) in enumerate([(0, 0), (0, 1), (1, 0)]):
                                last = nc.tensor.matmul(ph[:, 2 * c + j, :], w[wi], x[xi], start=(n == 0), stop=(n == 2))
                        last.then_inc(s["h_ps"], 1)

                def down(k, e, par):
                    m = k * E1 + e
                    pe.wait_ge(s["hid_ready"], m * HC + HC + 2)
                    pe.wait_ge(s["acc_ready"], m + 1)
                    for t in range(BT):
                        for c in range(HC):
                            last = nc.tensor.matmul(py[:, (par + e) % 2, t * C:(t + 1) * C], hid[:, (par + e) % 2, c, t * P:(t + 1) * P],
                                                    w2[:, e, c, :], start=(c == 0), stop=(c == HC - 1))
                    last.then_inc(s["y_ps"], 1)

                def body(j, last):
                    for par in range(2):
                        k = j * 2 + par
                        front = not (last and par)
                        f = k + 1
                        for e in range(E1):
                            up(k, e, par)
                            if e:
                                down(k, e - 1, par)
                            if front and e == 1:
                                x_transposes(f)
                            if front and e == 3:
                                small(f)
                        if front:
                            n_transposes(f)
                        down(k, E1 - 1, par)

                pe.sem_inc(s["y_ps"], 2)
                pe.wait_ge(const_in, 16)
                x_transposes(0)
                pe.wait_ge(s["wa_in"], 16 * 6)
                pe.wait_ge(s["wa_scaled"], 1)
                small(0)
                n_transposes(0)
                pe.wait_ge(s["w_lo"], E1)
                pe.wait_ge(s["w2_in"], 16 * E1)
                pe.wait_ge(s["xl_ready"], 1)
                with pe.Fori(0, NBLK // 2 - 1) as j:
                    body(j, False)
                body(NBLK // 2 - 1, True)


def load_grouped(eng, dst, rows, k_src, v_src, order, done):
    n = 0
    for g in range(G):
        for (at, width, src, first, per_head) in order:
            s = src.rearrange("p (h c) -> p h c", c=per_head)[:, g * HG:(g + 1) * HG, first:first + width]
            d = dst[rows, g, 0:QC].rearrange("p (i c) -> p i c", c=D)[:, :, at:at + width]
            eng.dma_start(d, s).then_inc(done, 16)
            n += 1
    return n


def select(nc, a, sem, cst, misc, xn_all, gates, ks_d, vs_d):
    ctx = ExitStack()
    with ctx:
        def sb(name, shape, dt=F32):
            return ctx.enter_context(nc.sbuf_tensor(name, shape, dt))

        def ps(name, shape, dt=F32):
            return ctx.enter_context(nc.psum_tensor(name, shape, dt))

        NS = B * KEEP // P
        wsel = sb("wsel", [P, G, GC])
        score = [sb(f"score{i}", [B, T]) for i in range(5)]
        best = sb("best", [B, 4, 8])
        chosen = sb("chosen", [B, T])
        ones = sb("ones_row", [B, T])
        count = sb("count", [B, T])
        place = sb("place", [B, T])
        place_t = sb("place_t", [P, B, NT])
        onehot = sb("onehot", [P, B * NT, KEEP])
        xsel = sb("xsel", [P, B * KEEP])
        kcos = sb("s_kcos", [P, 2, HG, ROPE])
        ksin = sb("s_ksin", [P, 2, HG, ROPE])
        ktok = sb("s_ktok", [P, NS, H, D])
        vtok = sb("s_vtok", [P, NS, H * VH])
        kt = sb("s_kt", [P, NS, P // KEEP, H, KEEP])
        glog = sb("glog", [P, B, 3])
        gmx = sb("gmx", [P, B])
        gd = sb("gd", [P, B, 3])
        gex = sb("gex", [P, B, 3])
        gsum = sb("gsum", [P, B])
        grec = sb("grec", [P, B])

        p_row = ps("p_row", [P, 512])
        p_place = ps("p_place", [P, 512])
        p_sel = ps("p_sel", [P, 512])
        p_gate = ps("p_gate", [P, 512])
        p_k = ps("p_k", [P, 2, 512])
        p_t = ps("p_t", [P, 2, 512])

        names = ("w_in v_in row_ps gate_ps score_in round ones_set place_done place_ps place_t_done onehot_done sel_ps sel_done "
                 "k_ps k_cos k_sin k_used k_nope v_done k_tok kT_ps kt_done kt_const gred gdiff gexp gchain k_out v_out").split()
        s = {n: sem("s_" + n) for n in names}
        ident = cst("ident")
        nw = 2 * G

        with nc.Block() as block:
            @block.sync
            def _(sp):
                load_grouped(sp, wsel, slice(0, P), None, None,
                             [(0, ROPE, a["L0_attn_w_selk"], NOPE, D), (ROPE, NOPE, a["L0_attn_w_selk"], 0, D)], s["w_in"])
                for g in range(G):
                    sp.dma_start(wsel[:, g, QC:GC], a["L0_attn_w_selv"][:, g * HG * VH:(g + 1) * HG * VH]).then_inc(s["v_in"], 16)
                for n in range(NS):
                    sp.wait_ge(s["v_done"], (n + 1) * G)
                    sp.dma_start(vs_d[n * (P // KEEP):(n + 1) * (P // KEEP)].rearrange("b k c -> (b k) c"), vtok[:, n, :]).then_inc(s["v_out"], 16)
                    sp.wait_ge(s["kt_done"], (n + 1) * G)
                    sp.wait_ge(s["kt_const"], 1)
                    for q in range(P // KEEP):
                        sp.dma_start(ks_d[n * (P // KEEP) + q], kt[:, n, q].rearrange("p h c -> p (h c)")).then_inc(s["k_out"], 16)
                sp.wait_ge(s["v_out"], 16 * NS)
                sp.wait_ge(s["k_out"], 16 * B)

            @block.tensor
            def _(pe):
                for t in range(NT):
                    imp = misc[:, :, 0:1].rearrange("p (b t) c -> p t (b c)", t=NT)[:, t, :]
                    last = nc.tensor.transpose(p_row[0:B, t * P:(t + 1) * P], imp, ident)
                last.then_inc(s["row_ps"], 1)
                nc.tensor.matmul(p_gate[:, 0:B * NT * 3], cst("mean"), misc[:, :, 1:4], start=True, stop=True).then_inc(s["gate_ps"], 1)
                pe.wait_ge(s["place_done"], 1)
                for t in range(NT):
                    last = nc.tensor.transpose(p_place[:, t * B:(t + 1) * B], place[:, t * P:(t + 1) * P], ident[0:B, 0:B])
                last.then_inc(s["place_ps"], 1)
                pe.wait_ge(s["onehot_done"], 1)
                for b in range(B):
                    for t in range(NT):
                        last = nc.tensor.matmul(p_sel[:, b * KEEP:(b + 1) * KEEP], xn_all[:, b * NT + t, :], onehot[:, b * NT + t, :],
                                                start=(t == 0), stop=(t == NT - 1))
                last.then_inc(s["sel_ps"], 1)
                pe.wait_ge(s["sel_done"], 1)
                pe.wait_ge(s["w_in"], 16 * nw)
                pe.wait_ge(s["v_in"], 16 * G)

                def project(u):
                    n, g = divmod(u, G)
                    if u >= 2:
                        pe.wait_ge(s["k_used"], 2 * (u - 1))
                        pe.wait_ge(s["k_nope"], u - 1)
                        pe.wait_ge(s["v_done"], u - 1)
                    nc.tensor.matmul(p_k[:, u % 2, :], xsel[:, n * P:(n + 1) * P], wsel[:, g, :], start=True, stop=True).then_inc(s["k_ps"], 1)

                def transposes(u):
                    n, g = divmod(u, G)
                    pe.wait_ge(s["k_tok"], u + 1)
                    pe.wait_ge(s["k_nope"], u + 1)
                    if u >= 2:
                        pe.wait_ge(s["kt_done"], u - 1)
                    for i in range(HG):
                        last = nc.tensor.transpose(p_t[0:D, u % 2, i * P:(i + 1) * P], ktok[:, n, g * HG + i, :], ident)
                    last.then_inc(s["kT_ps"], 1)

                for u in range(NS * G):
                    project(u)
                    if u >= 2:
                        transposes(u - 2)
                transposes(NS * G - 2)
                transposes(NS * G - 1)

            @block.vector
            def _(dve):
                nc.vector.memset(ones[:, :], 1.0).then_inc(s["ones_set"], 1)
                nc.vector.tensor_copy(kt[D:P].rearrange("p a b c d -> p (a b c d)"),
                                      cst("mrow")[D:P, BR2:BR2 + 1].to_broadcast([P - D, NS * P * H])).then_inc(s["kt_const"], 1)
                dve.wait_ge(s["row_ps"], 1)
                nc.vector.tensor_copy(score[0][:, :], p_row[0:B, 0:T]).then_inc(s["round"], 1)
                r = 1
                for n in range(KEEP // 8):
                    dve.wait_ge(s["round"], r)
                    nc.vector.max(best[:, n, :], score[n][:, :]).then_inc(s["round"], 1)
                    dve.wait_ge(s["round"], r + 1)
                    nc.vector.match_replace(score[n + 1][:, :], best[:, n, :], score[n][:, :], -3e38).then_inc(s["round"], 1)
                    r += 2
                dve.wait_ge(s["round"], r)
                nc.vector.tensor_tensor(chosen[:, :], score[0][:, :], score[KEEP // 8][:, :], ALU.not_equal).then_inc(s["round"], 1)
                dve.wait_ge(s["round"], r + 1)
                dve.wait_ge(s["ones_set"], 1)
                nc.vector.tensor_tensor_scan(count[:, :], ones[:, :], chosen[:, :], 0.0, ALU.mult, ALU.add).then_inc(s["round"], 1)
                dve.wait_ge(s["round"], r + 2)
                nc.vector.tensor_tensor(place[:, :], count[:, :], chosen[:, :], ALU.mult).then_inc(s["place_done"], 1)
                dve.wait_ge(s["gate_ps"], 1)
                nc.vector.tensor_reduce(glog[:, :, :], p_gate[:, 0:B * NT * 3].rearrange("p (b t c) -> p b c t", t=NT, c=3), X, ALU.add).then_inc(s["gchain"], 1)
                dve.wait_ge(s["gchain"], 1)
                nc.vector.tensor_reduce(gmx[:, :], glog[:, :, :], X, ALU.max).then_inc(s["gchain"], 1)
                dve.wait_ge(s["gchain"], 2)
                nc.vector.tensor_tensor(gd[:, :, :], glog[:, :, :], gmx[:, :].unsqueeze(2).to_broadcast([P, B, 3]), ALU.subtract).then_inc(s["gdiff"], 1)
                dve.wait_ge(s["place_ps"], 1)
                nc.vector.tensor_copy(place_t[:, :, :].rearrange("p b t -> p t b"), p_place[:, 0:B * NT].rearrange("p (t b) -> p t b", t=NT)).then_inc(s["place_t_done"], 1)
                dve.wait_ge(s["place_t_done"], 1)
                nc.vector.tensor_tensor(onehot[:, :, :], cst("iota").unsqueeze(1).to_broadcast([P, B * NT, KEEP]),
                                        place_t[:, :, :].rearrange("p b t -> p (b t)").unsqueeze(2).to_broadcast([P, B * NT, KEEP]),
                                        ALU.is_equal).then_inc(s["onehot_done"], 1)
                dve.wait_ge(s["gexp"], 1)
                nc.vector.tensor_reduce(gsum[:, :], gex[:, :, :], X, ALU.add).then_inc(s["gchain"], 1)
                dve.wait_ge(s["gchain"], 3)
                nc.vector.reciprocal(grec[:, :], gsum[:, :]).then_inc(s["gchain"], 1)
                dve.wait_ge(s["gchain"], 4)
                nc.vector.tensor_tensor(gates[:, :, :], gex[:, :, :], grec[:, :].unsqueeze(2).to_broadcast([P, B, 3]), ALU.mult).then_inc(s["gchain"], 1)
                dve.wait_ge(s["sel_ps"], 1)
                nc.vector.tensor_copy(xsel[:, :], p_sel[:, :]).then_inc(s["sel_done"], 1)
                for u in range(NS * G):
                    n, g = divmod(u, G)
                    dve.wait_ge(s["k_ps"], u + 1)
                    if u >= 2:
                        dve.wait_ge(s["k_tok"], u - 1)
                    src = p_k[:, u % 2, 0:QC].rearrange("p (i c) -> p i c", c=D)[:, :, 0:ROPE]
                    nc.vector.tensor_tensor(kcos[:, u % 2], src, cst("scos").unsqueeze(1).to_broadcast([P, HG, ROPE]), ALU.mult).then_inc(s["k_used"], 1)
                    nc.vector.tensor_tensor(ksin[:, u % 2].rearrange("p i (a c) -> p i a c", a=2),
                                            src.rearrange("p i (a c) -> p i a c", a=2)[:, :, ::-1, :],
                                            cst("ssin").rearrange("p (a c) -> p a c", a=2).unsqueeze(1).to_broadcast([P, HG, 2, HALF]),
                                            ALU.mult).then_inc(s["k_used"], 1)

            @block.gpsimd
            def _(pool):
                for u in range(NS * G):
                    n, g = divmod(u, G)
                    pool.wait_ge(s["k_used"], 2 * (u + 1))
                    nc.gpsimd.tensor_tensor(ktok[:, n, g * HG:(g + 1) * HG, 0:ROPE], kcos[:, u % 2], ksin[:, u % 2], ALU.add).then_inc(s["k_tok"], 1)

            @block.scalar
            def _(act):
                def transposed(u):
                    n, g = divmod(u, G)
                    act.wait_ge(s["kT_ps"], u + 1)
                    src = p_t[0:D, u % 2, :].rearrange("p (i q c) -> p q i c", i=HG, c=KEEP)
                    nc.scalar.copy(kt[0:D, n, :, g * HG:(g + 1) * HG, :], src).then_inc(s["kt_done"], 1)

                act.wait_ge(s["gdiff"], 1)
                nc.scalar.activation(gex[:, :, :], gd[:, :, :], ACT.Exp).then_inc(s["gexp"], 1)
                for u in range(NS * G):
                    n, g = divmod(u, G)
                    act.wait_ge(s["k_used"], 2 * (u + 1))
                    nc.scalar.copy(ktok[:, n, g * HG:(g + 1) * HG, ROPE:D],
                                   p_k[:, u % 2, 0:QC].rearrange("p (i c) -> p i c", c=D)[:, :, ROPE:D]).then_inc(s["k_nope"], 1)
                    nc.scalar.copy(vtok[:, n, g * HG * VH:(g + 1) * HG * VH], p_k[:, u % 2, QC:GC]).then_inc(s["v_done"], 1)
                    if u >= 2:
                        transposed(u - 2)
                transposed(NS * G - 2)
                transposed(NS * G - 1)


def attend(nc, a, sem, cst, gates, xt_d, nt_d, kr_d, res_d, ks_d, vs_d, out):
    ctx = ExitStack()
    with ctx:
        def sb(name, shape, dt=F32):
            return ctx.enter_context(nc.sbuf_tensor(name, shape, dt))

        def ps(name, shape, dt=F32):
            return ctx.enter_context(nc.psum_tensor(name, shape, dt))

        HT = HG * T
        TQ = T + P
        wraw = sb("wraw", [P, G, GC])
        nraw = sb("nraw", [P, H * NOPE])
        gain = sb("gain", [P, 1])
        wq = sb("wq", [P, 2, G, GC], F32R)
        wk = sb("wk", [P, 2, G, GC], F32R)
        wn = sb("wn", [P, 2, H * NOPE], F32R)
        wkraw = sb("wkraw", [P, G, GC])
        wp = sb("wp", [P, G, C])
        xt = sb("a_xt", [P, 2, T], F32R)
        nt = sb("a_nt", [P, 2, T], F32R)
        krt = sb("a_krt", [ROPE, T])
        res = sb("a_res", [P, NT, C])
        ot = sb("a_ot", [P, NT, C])
        gcur = sb("gcur", [P, 3])
        ks = [sb(f"ks{i}", [P, HG, KEEP]) for i in range(2)]
        vc = [sb(f"vc{i}", [P, VH]) for i in range(2)]
        ksb = sb("ksb", [D, HG, KEEP], BF16)
        vbd = [sb(f"vbd{i}", [P, HG, VH]) for i in range(2)]
        rcos = {x: sb(f"rcos_{x}", [P, NT, HG, ROPE]) for x in "qk"}
        rsin = {x: sb(f"rsin_{x}", [P, NT, HG, ROPE]) for x in "qk"}
        tok = {x: sb(f"tok_{x}", [P, NT, HG, D]) for x in "qk"}
        qt = [sb(f"qt{i}", [P, HG, T]) for i in range(2)]
        kw = [sb(f"kw{i}", [P, HG, T]) for i in range(2)]
        k1 = [sb(f"k1{i}", [P, HG, T]) for i in range(2)]
        qb = sb("qb", [D, HG, T], BF16)
        kwb = sb("kwb", [D, HG, T], BF16)
        k1b = sb("k1b", [D, HG, T], BF16)
        v1 = [sb(f"v1{i}", [P, NT, HG * VH]) for i in range(2)]
        vw = [sb(f"vw{i}", [P, NT, HG * VH]) for i in range(2)]
        mtok = sb("mtok", [P, NT, P])
        junk = sb("junk", [P, 16, T], BF16)
        prob = [sb(f"prob{i}", [P, HG, 2, TQ]) for i in range(2)]
        prob2 = sb("prob2", [P, T])
        rden = sb("rden", [P, 2, T])
        rden2 = sb("rden2", [P, T])
        o1, o3, o2, o13 = (sb(n, [P, T]) for n in ("o1", "o3", "o2", "o13"))
        att = sb("att", [P, G, T])

        pj = ps("pj", [P, 2, 512])
        mx = [ps(f"mx{i}", [P, 512]) for i in range(2)]
        sc = ps("sc", [P, 2, 512])
        av = ps("av", [P, 2, T])
        dn = ps("dn", [P, 2, T])

        names = ("raw_zero w_in kw_in g_in p_in n_in scaled w_hi w_lo mtok_zero rows_set xt_in nt_in kr_in res_in out_done "
                 "pq pkw kn_ps trq_ps trk_ps mx_ps mT_ps sc_ps s2_ps av_ps av2_ps op_ps "
                 "rq rk q_copied k_copied q_add k_add kn_copied kr_copied k1b_ready ksb_ready qt_ready kt_ready mrow "
                 "max_op exp_done masked vbd_ready g_ready n_rec n13 n_rec2 n2 att13 att_ready out_ready gate pgate").split()
        s = {n: sem("a_" + n) for n in names}
        ks_in = [sem(f"a_ks_in{i}") for i in range(2)]
        vc_in = [sem(f"a_vc_in{i}") for i in range(2)]
        ident = cst("ident")
        cos = cst("cos").rearrange("p (t c) -> p t c", c=ROPE)
        sin = cst("sin").rearrange("p (t a c) -> p t a c", a=2, c=HALF)
        out_v = out.rearrange("b (t p) c -> b p t c", p=P)
        res_v = res_d.rearrange("(b t p) c -> b p t c", t=NT, p=P)
        RAW = 16 * 2 * G

        def nxt(b, g, d=1):
            return (b, g + d) if g + d < G else (b + 1, g + d - G)

        def step(b, g):
            return b * G + g

        def loop(eng, body):
            body(0, True, False)
            with eng.Fori(1, B - 1) as b:
                body(b, False, False)
            body(B - 1, False, True)

        with nc.Block() as block:
            @block.sync
            def _(sp):
                sp.wait_ge(s["raw_zero"], 2)
                load_grouped(sp, wraw, slice(0, QL), None, None,
                             [(0, ROPE, a["L0_attn_w_dq_rope"], 0, ROPE), (ROPE, NOPE, a["L0_attn_w_dq_nope"], 0, NOPE)], s["w_in"])
                for g in range(G):
                    sp.dma_start(wraw[QL:P, g, QC:GC], a["L0_attn_w_dv"][:, g * HG * VH:(g + 1) * HG * VH]).then_inc(s["w_in"], 16)
                sp.dma_start(nraw[QL:P, :], a["L0_attn_w_dk_nope"]).then_inc(s["n_in"], 16)
                sp.dma_start(gain[0:QL, :], a["L0_attn_g_qnorm"].rearrange("(p c) -> p c", c=1)).then_inc(s["g_in"], 16)
                sp.dma_start(gain[QL:P, :], a["L0_attn_g_kvnorm"].rearrange("(p c) -> p c", c=1)).then_inc(s["g_in"], 16)
                load_grouped(sp, wkraw, slice(0, P), None, None,
                             [(0, ROPE, a["L0_attn_w_wink"], NOPE, D), (ROPE, NOPE, a["L0_attn_w_wink"], 0, D)], s["kw_in"])
                for g in range(G):
                    sp.dma_start(wkraw[:, g, QC:GC], a["L0_attn_w_winv"][:, g * HG * VH:(g + 1) * HG * VH]).then_inc(s["kw_in"], 16)
                sp.dma_start(wp[:, :, :], a["L0_attn_w_proj"].rearrange("(g p) c -> p g c", p=P)).then_inc(s["p_in"], 16)

                def load_seq(b):
                    sp.dma_start(nt[:, :, :].bitcast(F32), nt_d[b]).then_inc(s["nt_in"], 16)
                    sp.dma_start(xt[:, :, :].bitcast(F32), xt_d[b]).then_inc(s["xt_in"], 16)
                    sp.dma_start(krt[:, :], kr_d[b]).then_inc(s["kr_in"], 16)

                def load_sel(b, g):
                    par = g % 2
                    sp.dma_start(ks[par][:, :, :].rearrange("p i c -> p (i c)"), ks_d[b][:, g * P:(g + 1) * P]).then_inc(ks_in[par], 16)
                    for i in range(HG):
                        at = (g * HG + i) * VH
                        sp.dma_start(vc[par][i * KEEP:(i + 1) * KEEP, :], vs_d[b][:, at:at + VH]).then_inc(vc_in[par], 16)

                def body(b, first, last):
                    for g in range(G):
                        n = nxt(b, g)
                        if g == 0 and not first:
                            sp.wait_ge(s["out_ready"], b)
                            sp.dma_start(out_v[bass.ds(b - 1, 1)].rearrange("b p t c -> p (b t) c"), ot[:, :, :]).then_inc(s["out_done"], 16)
                        if g == 1:
                            if not first:
                                sp.wait_ge(s["out_ready"], b)
                            sp.dma_start(res[:, :, :], res_v[bass.ds(b, 1)].rearrange("b p t c -> p (b t) c")).then_inc(s["res_in"], 16)
                        if g == 2 and not last:
                            sp.wait_ge(s["kn_ps"], step(*n) + 1)
                            sp.wait_ge(s["pkw"], step(*n) + 1)
                            sp.wait_ge(s["kr_copied"], b * 2 + 2)
                            load_seq(b + 1)
                        if not (last and g >= 2):
                            sp.wait_ge(s["s2_ps"], step(b, g) + 1)
                            sp.wait_ge(s["vbd_ready"], step(b, g) + 1)
                            load_sel(*nxt(b, g, 2))

                load_seq(0)
                load_sel(0, 0)
                load_sel(0, 1)
                loop(sp, body)
                sp.wait_ge(s["out_ready"], B)
                sp.dma_start(out_v[B - 1], ot[:, :, :]).then_inc(s["out_done"], 16)
                sp.wait_ge(s["out_done"], 16 * B)

            @block.tensor
            def _(pe):
                def three(dst, w, wcols, x, xcols, w_moves):
                    for n, (i, j) in enumerate([(0, 0), (0, 1), (1, 0)]):
                        wi, xi = w[:, i][wcols], x[:, j][xcols]
                        left, right = (xi, wi) if w_moves else (wi, xi)
                        last = nc.tensor.matmul(dst, left, right, start=(n == 0), stop=(n == 2))
                    return last

                def project(w, x, g):
                    for t in range(NT):
                        for n, (i, j) in enumerate([(0, 0), (1, 0), (0, 1)]):
                            last = nc.tensor.matmul(pj[:, t, :], x[:, j, t * P:(t + 1) * P], w[:, i, g, :], start=(n == 0), stop=(n == 2))
                    return last

                def q_project(b, g):
                    if g == 0:
                        pe.wait_ge(s["nt_in"], 16 * (b + 1))
                        pe.wait_ge(s["xt_in"], 16 * (b + 1))
                    pe.wait_ge(s["kt_ready"], step(b, g) * 2 + 2)
                    project(wq, nt, g).then_inc(s["pq"], 1)

                def k_nope(b, g):
                    pe.wait_ge(s["mrow"], step(b, g) * 4 + 4)
                    for n, (i, j) in enumerate([(0, 0), (0, 1), (1, 0)]):
                        last = nc.tensor.matmul(mx[0][:, 0:T], wn[:, i, g * P:(g + 1) * P], nt[:, j, :], start=(n == 0), stop=(n == 2))
                    last.then_inc(s["kn_ps"], 1)

                def kw_project(b, g):
                    pe.wait_ge(s["rq"], step(b, g) * 3 + 3)
                    pe.wait_ge(s["q_copied"], step(b, g) * 2 + 2)
                    project(wk, xt, g).then_inc(s["pkw"], 1)

                def transposes(x):
                    for i in range(HG):
                        for t in range(NT):
                            last = nc.tensor.transpose(pj[0:D, i // 2, (i % 2) * T + t * P:(i % 2) * T + (t + 1) * P], tok[x][:, t, i, :], ident)
                    return last

                def q_transposes(b, g):
                    pe.wait_ge(s["rk"], step(b, g) * 3 + 3)
                    pe.wait_ge(s["k_copied"], step(b, g) * 2 + 2)
                    pe.wait_ge(s["q_add"], step(b, g) + 2)
                    transposes("q").then_inc(s["trq_ps"], 1)

                def kw_transposes(b, g):
                    pe.wait_ge(s["qt_ready"], step(b, g) * 2 + 2)
                    pe.wait_ge(s["k_add"], step(b, g) + 2)
                    transposes("k").then_inc(s["trk_ps"], 1)

                def rough(b, g, u):
                    st = step(b, g)
                    done = st * 17 + 4
                    if u == 0:
                        pe.wait_ge(s["qt_ready"], st * 2 + 2)
                        pe.wait_ge(s["k1b_ready"], st + 1)
                        pe.wait_ge(s["kt_ready"], st * 2 + 4)
                        pe.wait_ge(s["ksb_ready"], st + 1)

                    def late(i, bank):
                        nc.tensor.matmul(bank[:, 0:T], qb[:, i, P:T], k1b[:, i, :], start=True, stop=True)
                        return nc.tensor.matmul(bank[:, T:2 * T], qb[:, i, P:T], kwb[:, i, :], start=True, stop=True)

                    def early(i, bank):
                        for j in range(2):
                            nc.tensor.matmul(bank[:, j * T:j * T + P], qb[:, i + j, 0:P], k1b[:, i + j, 0:P], start=True, stop=True)
                            last = nc.tensor.matmul(bank[:, j * T + P:j * T + T], qb[:, i + j, 0:P], kwb[:, i + j, 0:P], start=True, stop=True)
                        return last

                    if u == 0:
                        last = late(0, mx[1])
                    if u == 1:
                        last = early(0, mx[0])
                    if u == 2:
                        pe.wait_ge(s["max_op"], done + 2)
                        last = late(1, mx[1])
                    if u == 3:
                        pe.wait_ge(s["max_op"], done + 6)
                        last = late(2, mx[0])
                    if u == 4:
                        pe.wait_ge(s["max_op"], done + 8)
                        last = early(2, mx[1])
                    if u == 5:
                        pe.wait_ge(s["max_op"], done + 10)
                        last = late(3, mx[0])
                    if u == 6:
                        pe.wait_ge(s["max_op"], done + 14)
                        for t in range(NT):
                            for i in range(HG):
                                at = (t * HG + i) * KEEP
                                last = nc.tensor.matmul(mx[1][:, at:at + KEEP], qb[:, i, t * P:(t + 1) * P], ksb[:, i, :], start=True, stop=True)
                    last.then_inc(s["mx_ps"], 1)

                def max_transposes(b, g):
                    pe.wait_ge(s["max_op"], step(b, g) * 17 + 17 + 4)
                    for t in range(NT):
                        last = nc.tensor.transpose(mx[0][:, t * P:(t + 1) * P], mtok[:, t, :], ident)
                    last.then_inc(s["mT_ps"], 1)

                def scores(b, g, i):
                    st, par = step(b, g), g % 2
                    pe.wait_ge(s["mrow"], st * 4 + 4 + i + 1)
                    pe.wait_ge(s["exp_done"], st * 5 + 5 + i)
                    for j, k in enumerate((k1[par], kw[par])):
                        nc.tensor.matmul(sc[:, j, 0:T], k[:, i, 0:P], qt[par][:, i, :], start=True, stop=True)
                        last = nc.tensor.matmul(sc[:, j, T:TQ], k[:, i, P:T], qt[par][:, i, P:T], start=True, stop=True)
                    last.then_inc(s["sc_ps"], 1)

                def selected_scores(b, g):
                    st, par = step(b, g), g % 2
                    pe.wait_ge(s["exp_done"], st * 5 + 5 + 4)
                    pe.wait_ge(ks_in[par], (b * 2 + g // 2 + 1) * 16)
                    for i in range(HG):
                        last = nc.tensor.matmul(sc[i * KEEP:(i + 1) * KEEP, 0, 0:T], ks[par][:, i, :], qt[par][:, i, :], start=True, stop=True)
                    last.then_inc(s["s2_ps"], 1)

                def weigh(b, g, j, what):
                    st, par = step(b, g), g % 2
                    pe.wait_ge(s["masked"], st * 4 + 4)
                    pe.wait_ge(s["n13"], st * 2 + 2)
                    v = (v1, vw)[j][par]
                    for kt in range(NT):
                        for i in range(HG):
                            left = v[:, kt, i * VH:(i + 1) * VH] if what else cst("ones")
                            dst = (av if what else dn)[i * VH:(i + 1) * VH, j, kt * P:T]
                            right = prob[par][:, i, j, 0:T] if kt == 0 else prob[par][:, i, j, T:TQ]
                            last = nc.tensor.matmul(dst, left, right, start=(kt == 0), stop=(kt == NT - 1))
                    return last

                def weigh_selected(b, g):
                    st, par = step(b, g), g % 2
                    pe.wait_ge(s["exp_done"], st * 5 + 5 + 5)
                    pe.wait_ge(s["vbd_ready"], st + 1)
                    nc.tensor.matmul(mx[1][:, 0:T], vbd[par][:, :, :].rearrange("p i c -> p (i c)"), prob2[:, :], start=True, stop=True)
                    nc.tensor.matmul(mx[1][:, T:2 * T], cst("block"), prob2[:, :], start=True, stop=True).then_inc(s["av2_ps"], 1)

                def out_project(b):
                    pe.wait_ge(s["att_ready"], b * G + G + 1)
                    for t in range(NT):
                        for g in range(G):
                            last = nc.tensor.matmul(mx[1][:, t * C:(t + 1) * C], att[:, g, t * P:(t + 1) * P], wp[:, g, :],
                                                    start=(g == 0), stop=(g == G - 1))
                    last.then_inc(s["op_ps"], 1)

                def body(b, first, last):
                    for g in range(G):
                        n = nxt(b, g)
                        prep = not (last and g == G - 1)
                        if prep:
                            q_project(*n)
                        scores(b, g, 0)
                        if prep:
                            k_nope(*n)
                            kw_project(*n)
                        scores(b, g, 1)
                        if prep:
                            q_transposes(*n)
                        scores(b, g, 2)
                        if prep:
                            kw_transposes(*n)
                        scores(b, g, 3)
                        selected_scores(b, g)
                        if g == 0 and not first:
                            out_project(b - 1)
                        if not (first and g == 0):
                            pe.wait_ge(s["n2"], step(b, g))
                        if g == 0 and not first:
                            pe.wait_ge(s["out_ready"], b)
                        if prep:
                            rough(*n, 0)
                            rough(*n, 1)
                        weigh(b, g, 0, True)
                        if prep:
                            rough(*n, 2)
                        weigh(b, g, 0, False)
                        if prep:
                            rough(*n, 3)
                            rough(*n, 4)
                        weigh(b, g, 1, True)
                        if prep:
                            rough(*n, 5)
                            rough(*n, 6)
                        weigh(b, g, 1, False).then_inc(s["av_ps"], 1)
                        if prep:
                            max_transposes(*n)
                        weigh_selected(b, g)

                for x in ("w_lo", "p_in", "rows_set"):
                    pe.wait_ge(s[x], {"w_lo": 3, "p_in": 16, "rows_set": 4}[x])
                q_project(0, 0)
                k_nope(0, 0)
                kw_project(0, 0)
                q_transposes(0, 0)
                kw_transposes(0, 0)
                for u in range(7):
                    rough(0, 0, u)
                max_transposes(0, 0)
                loop(pe, body)
                out_project(B - 1)

            @block.scalar
            def _(act):
                def copies(b, g, x, rotated, done, v):
                    act.wait_ge(s[rotated], step(b, g) * 3 + 3)
                    nc.scalar.copy(tok[x][:, :, :, ROPE:D], pj[:, :, 0:QC].rearrange("p t (i c) -> p t i c", c=D)[:, :, :, ROPE:D]).then_inc(s[done], 1)
                    nc.scalar.copy(v[g % 2][:, :, :], pj[:, :, QC:GC]).then_inc(s[done], 1)

                def knope_rows(b, g):
                    act.wait_ge(s["kn_ps"], step(b, g) + 1)
                    for i in range(HG):
                        nc.scalar.copy(k1[g % 2][ROPE:D, i, :], mx[0][i * NOPE:(i + 1) * NOPE, 0:T]).then_inc(s["kn_copied"], 1)

                def transposed(b, g, ready, done, exact, rounded):
                    act.wait_ge(s[ready], step(b, g) + 1)
                    src = pj[0:D, :, :].rearrange("p b c -> p (b c)")
                    nc.scalar.copy(rounded[:, :, :].rearrange("p i c -> p (i c)"), src).then_inc(s[done], 1)
                    nc.scalar.copy(exact[g % 2][0:D].rearrange("p i c -> p (i c)"), src).then_inc(s[done], 1)

                def max_rows(b, g):
                    act.wait_ge(s["mT_ps"], step(b, g) + 1)
                    for i in range(HG):
                        nc.scalar.copy(qt[g % 2][D:P, i, :], mx[0][i * 32:(i + 1) * 32, 0:T]).then_inc(s["mrow"], 1)

                def exps(b, g, i):
                    act.wait_ge(s["sc_ps"], step(b, g) * 4 + i + 1)
                    nc.scalar.activation(prob[g % 2][:, i, :, :], sc[:, :, 0:TQ], ACT.Exp, scale=SCALE).then_inc(s["exp_done"], 1)

                def exp_selected(b, g):
                    act.wait_ge(s["s2_ps"], step(b, g) + 1)
                    nc.scalar.activation(prob2[:, :], sc[:, 0, 0:T], ACT.Exp, scale=SCALE).then_inc(s["exp_done"], 1)

                def body(b, first, last):
                    for g in range(G):
                        n = nxt(b, g)
                        prep = not (last and g == G - 1)
                        if prep:
                            copies(*n, "q", "rq", "q_copied", v1)
                        exps(b, g, 0)
                        if prep:
                            knope_rows(*n)
                            copies(*n, "k", "rk", "k_copied", vw)
                        exps(b, g, 1)
                        if prep:
                            transposed(*n, "trq_ps", "qt_ready", qt, qb)
                        exps(b, g, 2)
                        if prep:
                            transposed(*n, "trk_ps", "kt_ready", kw, kwb)
                        exps(b, g, 3)
                        exp_selected(b, g)
                        if prep:
                            max_rows(*n)

                act.sem_inc(s["kt_ready"], 2)
                act.sem_inc(s["mrow"], 4)
                act.sem_inc(s["exp_done"], 5)
                act.wait_ge(s["scaled"], 2)
                nc.scalar.copy(wq[:, 0], wraw[:, :, :]).then_inc(s["w_hi"], 1)
                nc.scalar.copy(wn[:, 0], nraw[:, :]).then_inc(s["w_hi"], 1)
                act.wait_ge(s["kw_in"], 16 * 3 * G)
                nc.scalar.copy(wk[:, 0], wkraw[:, :, :]).then_inc(s["w_hi"], 1)
                copies(0, 0, "q", "rq", "q_copied", v1)
                knope_rows(0, 0)
                copies(0, 0, "k", "rk", "k_copied", vw)
                transposed(0, 0, "trq_ps", "qt_ready", qt, qb)
                transposed(0, 0, "trk_ps", "kt_ready", kw, kwb)
                max_rows(0, 0)
                loop(act, body)

            @block.vector
            def _(dve):
                def rotate(b, g, x, ready, done, added):
                    st = step(b, g)
                    dve.wait_ge(s[ready], st + 1)
                    dve.wait_ge(s[added], st + 1)
                    src = pj[:, :, 0:QC].rearrange("p t (i c) -> p t i c", c=D)[:, :, :, 0:ROPE]
                    nc.vector.tensor_tensor(rcos[x][:, :, :, :], src, cos.unsqueeze(2).to_broadcast([P, NT, HG, ROPE]), ALU.mult).then_inc(s[done], 1)
                    for t in range(NT):
                        nc.vector.tensor_tensor(rsin[x][:, t].rearrange("p i (a c) -> p i a c", a=2),
                                                src[:, t].rearrange("p i (a c) -> p i a c", a=2)[:, :, ::-1, :],
                                                sin[:, t].unsqueeze(1).to_broadcast([P, HG, 2, HALF]), ALU.mult).then_inc(s[done], 1)

                def rough_keys(b, g):
                    st = step(b, g)
                    if g < 2:
                        dve.wait_ge(s["kr_in"], 16 * (b + 1))
                        nc.vector.tensor_copy(k1[g][0:ROPE, :, :], krt[:, :].unsqueeze(1).to_broadcast([ROPE, HG, T])).then_inc(s["kr_copied"], 1)
                        dve.wait_ge(s["kr_copied"], b * 2 + g + 1)
                    dve.wait_ge(s["kn_copied"], st * 4 + 4)
                    nc.vector.tensor_copy(k1b[:, :, :], k1[g % 2][0:D]).then_inc(s["k1b_ready"], 1)
                    dve.wait_ge(ks_in[g % 2], (b * 2 + g // 2 + 1) * 16)
                    nc.vector.tensor_copy(ksb[:, :, :], ks[g % 2][0:D]).then_inc(s["ksb_ready"], 1)

                def maxima(b, g):
                    st = step(b, g)
                    done = [0]

                    def row_max(bank, at, width, t, i, branch):
                        n = done[0]
                        nc.vector.tensor_tensor_reduce(out=junk[:, n, 0:width], in0=bank[:, at:at + width],
                                                       in1=cst("mask")[:, T - width:T], scale=1.0, scalar=-3e38, op0=ALU.add, op1=ALU.max,
                                                       accum_out=mtok[:, t, 32 * i + branch:32 * i + branch + 1]).then_inc(s["max_op"], 1)
                        done[0] += 1

                    def late(u, i, bank):
                        wait_alone(dve, s["mx_ps"], st * 7 + u + 1, s["gate"])
                        row_max(bank, 0, T, 1, i, BR1)
                        row_max(bank, T, T, 1, i, BR3)

                    def early(u, i, bank):
                        wait_alone(dve, s["mx_ps"], st * 7 + u + 1, s["gate"])
                        for j in range(2):
                            row_max(bank, j * T, P, 0, i + j, BR1)
                            row_max(bank, j * T + P, P, 0, i + j, BR3)

                    dve.wait_ge(s["max_op"], st * 17 + 4)
                    late(0, 0, mx[1])
                    early(1, 0, mx[0])
                    late(2, 1, mx[1])
                    late(3, 2, mx[0])
                    early(4, 2, mx[1])
                    late(5, 3, mx[0])
                    dve.wait_ge(s["mx_ps"], st * 7 + 7)
                    nc.vector.tensor_reduce(mtok[:, :, :].rearrange("p t (i c) -> p t i c", c=32)[:, :, :, BR2],
                                            mx[1][:, 0:NT * HG * KEEP].rearrange("p (t i c) -> p t i c", i=HG, c=KEEP), X, ALU.max).then_inc(s["max_op"], 1)

                def normalise13(b, g):
                    st = step(b, g)
                    if g == 0:
                        nc.vector.tensor_copy(gcur[:, :], gates[:, bass.ds(b, 1), :].rearrange("p b c -> p (b c)")).then_inc(s["g_ready"], 1)
                        dve.wait_ge(s["g_ready"], b + 1)
                    dve.wait_ge(s["av_ps"], st + 1)
                    nc.vector.reciprocal(rden[:, :, :], dn[:, :, :]).then_inc(s["n_rec"], 1)
                    dve.wait_ge(s["n_rec"], st + 1)
                    dve.wait_ge(s["att_ready"], st + 1)
                    nc.vector.scalar_tensor_tensor(o1[:, :], av[:, 0, :], gcur[:, 0:1], rden[:, 0, :], ALU.mult, ALU.mult).then_inc(s["n13"], 1)
                    nc.vector.scalar_tensor_tensor(o3[:, :], av[:, 1, :], gcur[:, 2:3], rden[:, 1, :], ALU.mult, ALU.mult).then_inc(s["n13"], 1)

                def normalise2(b, g):
                    st = step(b, g)
                    dve.wait_ge(s["av2_ps"], st + 1)
                    nc.vector.reciprocal(rden2[:, :], mx[1][:, T:2 * T]).then_inc(s["n_rec2"], 1)
                    dve.wait_ge(s["n_rec2"], st + 1)
                    nc.vector.scalar_tensor_tensor(o2[:, :], mx[1][:, 0:T], gcur[:, 1:2], rden2[:, :], ALU.mult, ALU.mult).then_inc(s["n2"], 1)

                def finish(b, first_out):
                    dve.wait_ge(s["op_ps"], b + 1)
                    dve.wait_ge(s["res_in"], 16 * (b + 1))
                    if not first_out:
                        dve.wait_ge(s["out_done"], 16 * b)
                    nc.vector.tensor_tensor(ot[:, :, :], mx[1][:, 0:NT * C].rearrange("p (t c) -> p t c", c=C), res[:, :, :], ALU.add).then_inc(s["out_ready"], 1)

                def body(b, first, last):
                    for g in range(G):
                        n = nxt(b, g)
                        before = (b, g - 1) if g else (b - 1, G - 1)
                        prep = not (last and g == G - 1)
                        if prep:
                            rotate(*n, "q", "pq", "rq", "q_add")
                        if not (first and g == 0):
                            normalise13(*before)
                        if prep:
                            rotate(*n, "k", "pkw", "rk", "k_add")
                        if not (first and g == 0):
                            normalise2(*before)
                        if prep:
                            rough_keys(*n)
                        if g == 0 and not first:
                            finish_at(b)
                        if prep:
                            maxima(*n)

                def finish_at(b):
                    finish(b - 1, isinstance(b, int) and b == 1)

                dve.sem_inc(s["max_op"], 4)
                dve.sem_inc(s["n13"], 2)
                nc.vector.memset(wraw[:, :, :], 0.0).then_inc(s["raw_zero"], 1)
                nc.vector.memset(nraw[:, :], 0.0).then_inc(s["raw_zero"], 1)
                nc.vector.memset(mtok[:, :, :], 0.0).then_inc(s["mtok_zero"], 1)
                for i in range(2):
                    for j, k in enumerate((k1, kw)):
                        nc.vector.tensor_copy(k[i][D:P].rearrange("p i c -> p (i c)"),
                                              cst("mrow")[D:P, j:j + 1].to_broadcast([P - D, HT])).then_inc(s["rows_set"], 1)
                dve.wait_ge(s["mtok_zero"], 1)
                dve.wait_ge(s["rows_set"], 4)
                dve.wait_ge(s["g_in"], 32)
                dve.wait_ge(s["raw_zero"], 2)
                dve.wait_ge(s["w_in"], 16 * 3 * G)
                nc.vector.tensor_scalar(wraw[:, :, :], wraw[:, :, :], gain[:, 0:1], None, ALU.mult).then_inc(s["scaled"], 1)
                dve.wait_ge(s["n_in"], 16)
                nc.vector.tensor_scalar(nraw[:, :], nraw[:, :], gain[:, 0:1], None, ALU.mult).then_inc(s["scaled"], 1)
                dve.wait_ge(s["scaled"], 2)
                dve.wait_ge(s["w_hi"], 1)
                nc.vector.tensor_tensor(wq[:, 1], wraw[:, :, :], wq[:, 0].bitcast(F32), ALU.subtract).then_inc(s["w_lo"], 1)
                dve.wait_ge(s["w_hi"], 2)
                nc.vector.tensor_tensor(wn[:, 1], nraw[:, :], wn[:, 0].bitcast(F32), ALU.subtract).then_inc(s["w_lo"], 1)
                dve.wait_ge(s["w_hi"], 3)
                nc.vector.tensor_tensor(wk[:, 1], wkraw[:, :, :], wk[:, 0].bitcast(F32), ALU.subtract).then_inc(s["w_lo"], 1)
                rotate(0, 0, "q", "pq", "rq", "q_add")
                rotate(0, 0, "k", "pkw", "rk", "k_add")
                rough_keys(0, 0)
                maxima(0, 0)
                loop(dve, body)
                normalise13(B - 1, G - 1)
                normalise2(B - 1, G - 1)
                finish(B - 1, False)

            @block.gpsimd
            def _(pool):
                def add(b, g, x, parts, done):
                    pool.wait_ge(s[parts], step(b, g) * 3 + 3)
                    nc.gpsimd.tensor_tensor(tok[x][:, :, :, 0:ROPE], rcos[x][:, :, :, :], rsin[x][:, :, :, :], ALU.add).then_inc(s[done], 1)

                def mask(b, g, i):
                    wait_alone(pool, s["exp_done"], step(b, g) * 5 + 5 + i + 1, s["pgate"])
                    blocks = prob[g % 2][:, i, :, :]
                    at = [blocks[:, :, 0:P], blocks[:, :, T:TQ]]
                    for j in range(2):
                        ins = nc.gpsimd.affine_select(out=at[j], in_=at[j], compare_op=ALU.is_ge, fill=0.0, base=0,
                                                      pattern=[[0, 2], [1, P]], channel_multiplier=-1)
                    ins.then_inc(s["masked"], 1)

                def blocks(b, g):
                    pool.wait_ge(vc_in[g % 2], (b * 2 + g // 2 + 1) * 64)
                    nc.gpsimd.tensor_tensor(vbd[g % 2][:, :, :], vc[g % 2][:, :].unsqueeze(1).to_broadcast([P, HG, VH]),
                                            cst("block").rearrange("p (i c) -> p i c", c=VH), ALU.mult).then_inc(s["vbd_ready"], 1)

                def branches(b, g):
                    st = step(b, g)
                    pool.wait_ge(s["n13"], st * 2 + 4)
                    if isinstance(b, int) and b == 0 and g == 0:
                        pass
                    nc.gpsimd.tensor_tensor(o13[:, :], o1[:, :], o3[:, :], ALU.add).then_inc(s["att13"], 1)
                    pool.wait_ge(s["att13"], st + 1)
                    pool.wait_ge(s["n2"], st + 1)
                    if g == 0 and not (isinstance(b, int) and b == 0):
                        pool.wait_ge(s["op_ps"], b)
                    nc.gpsimd.tensor_tensor(att[:, g, :], o13[:, :], o2[:, :], ALU.add).then_inc(s["att_ready"], 1)

                def body(b, first, last):
                    for g in range(G):
                        n = nxt(b, g)
                        before = (b, g - 1) if g else (b - 1, G - 1)
                        prep = not (last and g == G - 1)
                        if prep:
                            add(*n, "q", "rq", "q_add")
                        mask(b, g, 0)
                        if prep:
                            add(*n, "k", "rk", "k_add")
                        mask(b, g, 1)
                        if not (first and g == 0):
                            branches(*before)
                        mask(b, g, 2)
                        blocks(b, g)
                        mask(b, g, 3)

                pool.sem_inc(s["q_add"], 1)
                pool.sem_inc(s["k_add"], 1)
                pool.sem_inc(s["att_ready"], 1)
                add(0, 0, "q", "rq", "q_add")
                add(0, 0, "k", "rk", "k_add")
                loop(pool, body)
                branches(B - 1, G - 1)


_INS = ["L0_attn_x", "L0_attn_w_cq", "L0_attn_g_qnorm", "L0_attn_w_dq_nope", "L0_attn_w_dq_rope", "L0_attn_w_ckv", "L0_attn_g_kvnorm",
        "L0_attn_w_dk_nope", "L0_attn_w_dv", "L0_attn_w_krope", "L0_attn_w_imp", "L0_attn_w_selk", "L0_attn_w_selv", "L0_attn_w_wink",
        "L0_attn_w_winv", "L0_attn_w_gate", "L0_attn_w_proj", "L0_ffn_w_router", "L0_ffn_w1", "L0_ffn_w3", "L0_ffn_w2", "L0_ffn_sw1",
        "L0_ffn_sw3", "L0_ffn_sw2"]


def kernel(**inputs):
    import numpy as _np
    import concourse.bacc as _bacc
    from concourse import mybir as _mybir
    from concourse.bass_utils import run_bass_kernel_spmd as _run

    nc = _bacc.Bacc("TRN2", target_bir_lowering=False, num_devices=1)
    arrays, args = {}, {}
    for name in _INS:
        x = _np.ascontiguousarray(inputs[name])
        arrays[f"in_{name}"] = x
        args[name] = nc.dram_tensor(f"in_{name}", x.shape, _mybir.dt.from_np(x.dtype), kind="ExternalInput").ap()
    arrays["in_constants"] = constants(_np)
    args["constants"] = nc.dram_tensor("in_constants", (P, NCONST), F32, kind="ExternalInput").ap()
    out = nc.dram_tensor("out_0", (B, T, C), F32, kind="ExternalOutput").ap()
    layer_kernel(nc, args, out)
    r = _run(nc, [arrays], core_ids=[0])
    return r.results[0]["out_0"]
```

```python
from contextlib import ExitStack

import concourse.bass as bass
from concourse import mybir

F32 = mybir.dt.float32
F32R = mybir.dt.float32r
BF16 = mybir.dt.bfloat16
ALU = mybir.AluOpType
ACT = mybir.ActivationFunctionType
X = mybir.AxisListType.X

B, T, C = 16, 256, 128
P = 128
NT = T // P
H, HG = 16, 4
G = H // HG
NOPE, ROPE, VH = 32, 64, 32
HALF = ROPE // 2
D = NOPE + ROPE
QL, KL = 96, 32
KEEP = 32
QC = HG * D
GC = QC + HG * VH
E1 = 9
NE = E1 - 1
HID = 256
HC = HID // P
BT = 4
NBLK = B * T // (BT * P)
BTOK = BT * P
SPB = B // (BTOK // T) and BTOK // T
A_CKV, A_KR, A_IMP, A_GATE, A_ROUT = QL, QL + KL, QL + KL + ROPE, QL + KL + ROPE + 1, QL + KL + ROPE + 4
A_N = A_ROUT + NE
EPS_LN, EPS_RMS = 1e-5, 1e-6
SCALE = float(D) ** -0.5
NEG = -1e30
BR1, BR3, BR2 = 0, 1, 2

CONST_COLS = {}


def _layout():
    at = 0
    for name, n in [("ident", P), ("cos", NT * ROPE), ("sin", NT * ROPE), ("scos", ROPE), ("ssin", ROPE),
                    ("mask", T), ("mrow", 3), ("iota", KEEP), ("tri", NE * NE), ("block", P),
                    ("mean", P), ("ones", VH), ("eps", 2)]:
        CONST_COLS[name] = (at, n)
        at += n
    return at


NCONST = _layout()


def constants(np):
    c = np.zeros((P, NCONST), np.float32)

    def put(name, a):
        at, n = CONST_COLS[name]
        c[:, at:at + n] = np.asarray(a, np.float32).reshape(P, n)

    inv = (np.float32(1.0) / np.float32(10000.0) ** (np.arange(0, ROPE, 2, dtype=np.float32) / np.float32(ROPE))).astype(np.float32)
    ang = np.outer(np.arange(T, dtype=np.float32), inv).astype(np.float32)
    cos, sin = np.cos(ang), np.sin(ang)
    two_c, two_s = np.concatenate([cos, cos], 1), np.concatenate([-sin, sin], 1)
    p = np.arange(P)
    put("ident", np.eye(P))
    put("cos", two_c.reshape(NT, P, ROPE).transpose(1, 0, 2))
    put("sin", two_s.reshape(NT, P, ROPE).transpose(1, 0, 2))
    put("scos", two_c[p % KEEP])
    put("ssin", two_s[p % KEEP])
    put("mask", np.where(np.arange(T)[None, :] <= p[:, None] + T - P, 0.0, NEG))
    put("mrow", np.where(p[:, None] == D + np.arange(3)[None, :], -1.0, 0.0))
    put("iota", np.broadcast_to(np.arange(1, KEEP + 1), (P, KEEP)))
    e = np.arange(NE)
    put("tri", np.broadcast_to((e[None, :] < e[:, None]).reshape(1, -1), (P, NE * NE)))
    put("block", (p[:, None] // KEEP == p[None, :] // VH))
    put("mean", np.full((P, P), 1.0 / T))
    put("ones", np.ones((P, VH)))
    put("eps", np.broadcast_to([EPS_LN, EPS_RMS], (P, 2)))
    return c


def wait_alone(eng, semaphore, value, passed):
    eng.wait_ge(semaphore, value)
    eng.sem_inc(passed, 1)


def layer_kernel(nc, a, out):
    ctx = ExitStack()
    with ctx:
        def sem(name):
            return ctx.enter_context(nc.semaphore(name))

        def keep(name, shape, dt=F32):
            return ctx.enter_context(nc.sbuf_tensor(name, shape, dt))

        dram = lambda name, shape: nc.dram_tensor(name, shape, F32, kind="Internal").ap()
        xt_d = dram("xt_d", (B, C, 2, T))
        nt_d = dram("nt_d", (B, P, 2, T))
        kr_d = dram("kr_d", (B, ROPE, T))
        res_d = dram("res_d", (B * T, C))
        ks_d = dram("ks_d", (B, P, H * KEEP))
        vs_d = dram("vs_d", (B, KEEP, H * VH))

        const = keep("const", [P, NCONST])
        misc = keep("misc", [P, B * NT, 4])
        xn_all = keep("xn_all", [P, B * NT, C])
        gates = keep("gates", [P, B, 3])

        def cst(name):
            at, n = CONST_COLS[name]
            return const[:, at:at + n]

        const_in = sem("const_in")
        mixture(nc, ctx, a, sem, cst, const, const_in, misc, xn_all, xt_d, nt_d, kr_d, res_d)
        select(nc, a, sem, cst, misc, xn_all, gates, ks_d, vs_d)
        attend(nc, a, sem, cst, gates, xt_d, nt_d, kr_d, res_d, ks_d, vs_d, out)


def mixture(nc, octx, a, sem, cst, const, const_in, misc, xn_all, xt_d, nt_d, kr_d, res_d):
    ctx = ExitStack()
    with ctx:
        def sb(name, shape, dt=F32):
            return ctx.enter_context(nc.sbuf_tensor(name, shape, dt))

        def ps(name, shape, dt=F32):
            return ctx.enter_context(nc.psum_tensor(name, shape, dt))

        w13_raw = sb("w13_raw", [P, E1, 2, HID])
        w13 = sb("w13", [P, 2, E1, 2, HID], F32R)
        w2 = sb("w2", [P, E1, HC, C])
        wa = sb("wa", [P, A_N])
        xb = sb("xb", [P, 2, BT, C])
        stats = sb("stats", [P, BT, 6])
        mv = sb("mv", [P, 2, BT, 2])
        lnv = sb("lnv", [P, BT])
        rstd = sb("rstd", [P, 2, BT])
        xn = sb("xn", [P, BT, C])
        xt = sb("xt", [P, BTOK])
        xhl = [sb(f"xhl{i}", [P, 2, BTOK], F32R) for i in range(2)]
        sqj = sb("sqj", [P, BT, P])
        ssq = sb("ssq", [P, 2, BT])
        lns = sb("lns", [P, 2, BT])
        rr = sb("rr", [P, 2, BT])
        nqc = sb("nqc", [P, BT, P])
        nhl = [sb(f"nhl{i}", [P, 2, BTOK], F32R) for i in range(2)]
        kcos = sb("kcos", [P, BT, ROPE])
        ksin = sb("ksin", [P, BT, ROPE])
        kr = sb("kr", [P, BT, ROPE])
        krt = [sb(f"krt{i}", [ROPE, BTOK]) for i in range(2)]
        rmx = sb("rmx", [P, BT])
        rd = sb("rd", [P, BT, NE])
        rex = sb("rex", [P, BT, NE])
        rsum = sb("rsum", [P, BT])
        rrec = sb("rrec", [P, BT])
        rp = sb("rp", [P, BT, NE])
        rgt = sb("rgt", [P, BT, NE, NE])
        req = sb("req", [P, BT, NE, NE])
        rank = sb("rank", [P, BT, NE])
        rsel = sb("rsel", [P, BT, NE])
        rs2 = sb("rs2", [P, BT])
        rr2 = sb("rr2", [P, BT])
        cw = [sb(f"cw{i}", [P, BT, NE]) for i in range(2)]
        silu = sb("silu", [P, HC, BTOK])
        hid = sb("hid", [P, 2, HC, BTOK])
        acc = sb("acc", [P, 2, BT, C])

        pf = ps("pf", [P, 2, 512])
        ph = ps("ph", [P, 2 * HC, 512])
        py = ps("py", [P, 2, 512])
        pa = pf[:, :, :].rearrange("p b (t c) -> p (b t) c", c=256)

        names = ("w2_in wa_in raw_free w_hi w_lo wa_scaled bn var ln_log ln_rstd xn_ready xn_kept "
                 "xT_ps xt_ready xh_ready xl_ready a_ps sq rms_log misc_ready rr_ready nq_ready kr_part kr_ready "
                 "rmax rdiff rexp rchain cw_ready a_used nT_ps krT_ps nh_ready nl_ready krt_ready "
                 "h_ps silu_ready hid_ready y_ps acc_ready gate").split()
        s = {n: sem("m_" + n) for n in names}
        w_in = [sem(f"m_w_in{i}") for i in range(3)]
        x_in = [sem(f"m_x_in{i}") for i in range(2)]
        xt_out = [sem(f"m_xt_out{i}") for i in range(2)]
        nt_out = [sem(f"m_nt_out{i}") for i in range(2)]
        kr_out = [sem(f"m_kr_out{i}") for i in range(2)]
        acc_out = [sem(f"m_acc_out{i}") for i in range(2)]

        x_v = a["L0_attn_x"].rearrange("b (t p) c -> p (b t) c", p=P)
        res_v = res_d.rearrange("(n p) c -> p n c", p=P)
        ident = cst("ident")

        with nc.Block() as block:
            @block.sync
            def _(sp):
                for n in range(2):
                    sp.sem_inc(xt_out[n], 16 * SPB)
                    sp.sem_inc(nt_out[n], 16 * SPB)
                    sp.sem_inc(kr_out[n], 16 * SPB)
                    sp.sem_inc(acc_out[n], 16)
                sp.dma_start(const[:, :], a["constants"]).then_inc(const_in, 16)
                for n in range(2):
                    sp.dma_start(xb[:, n], x_v[:, n * BT:(n + 1) * BT, :]).then_inc(x_in[n], 16)
                for at, name, n in [(0, "L0_attn_w_cq", QL), (A_CKV, "L0_attn_w_ckv", KL), (A_KR, "L0_attn_w_krope", ROPE),
                                    (A_IMP, "L0_attn_w_imp", 1), (A_GATE, "L0_attn_w_gate", 3), (A_ROUT, "L0_ffn_w_router", NE)]:
                    sp.dma_start(wa[:, at:at + n], a[name]).then_inc(s["wa_in"], 16)
                third = E1 // 3
                for n in range(3):
                    for j, (w, shared) in enumerate([("L0_ffn_w1", "L0_ffn_sw1"), ("L0_ffn_w3", "L0_ffn_sw3")]):
                        many = slice(n * third, min((n + 1) * third, NE))
                        sp.dma_start(w13_raw[:, many, j, :], a[w][many].rearrange("e p h -> p e h")).then_inc(w_in[n], 16)
                        if n == 2:
                            sp.dma_start(w13_raw[:, NE, j, :], a[shared]).then_inc(w_in[n], 16)
                    if n == 0:
                        sp.dma_start(w2[:, 0:NE], a["L0_ffn_w2"].rearrange("e (c p) d -> p e c d", p=P)).then_inc(s["w2_in"], 16)
                        sp.dma_start(w2[:, NE], a["L0_ffn_sw2"].rearrange("(c p) d -> p c d", p=P)).then_inc(s["w2_in"], 16)

                def store(f, par):
                    sp.wait_ge(s["xl_ready"], f + 1)
                    for q in range(SPB):
                        sp.dma_start(xt_d[f * SPB + q], xhl[par][:, :, q * T:(q + 1) * T].bitcast(F32)).then_inc(xt_out[par], 16)
                    sp.wait_ge(s["nl_ready"], f + 2)
                    for q in range(SPB):
                        sp.dma_start(nt_d[f * SPB + q], nhl[par][:, :, q * T:(q + 1) * T].bitcast(F32)).then_inc(nt_out[par], 16)
                    sp.wait_ge(s["krt_ready"], f + 2)
                    for q in range(SPB):
                        sp.dma_start(kr_d[f * SPB + q], krt[par][:, q * T:(q + 1) * T]).then_inc(kr_out[par], 16)

                def body(j, last):
                    for par in range(2):
                        k = j * 2 + par
                        if not last:
                            sp.wait_ge(s["acc_ready"], k * E1 + 3)
                            sp.dma_start(xb[:, par], x_v[:, bass.ds((k + 2) * BT, BT), :]).then_inc(x_in[par], 16)
                        if not (last and par):
                            store(k + 1, 1 - par)
                        sp.wait_ge(s["acc_ready"], k * E1 + E1 + 2)
                        sp.dma_start(res_v[:, bass.ds(k * BT, BT), :], acc[:, par]).then_inc(acc_out[par], 16)

                store(0, 0)
                with sp.Fori(0, NBLK // 2 - 1) as j:
                    body(j, False)
                body(NBLK // 2 - 1, True)
                for n in range(2):
                    sp.wait_ge(xt_out[n], 16 * SPB * (NBLK // 2 + 1))
                    sp.wait_ge(nt_out[n], 16 * SPB * (NBLK // 2 + 1))
                    sp.wait_ge(kr_out[n], 16 * SPB * (NBLK // 2 + 1))
                    sp.wait_ge(acc_out[n], 16 * (NBLK // 2 + 1))

            @block.gpsimd
            def _(pool):
                for e in range(E1):
                    pool.wait_ge(s["w_hi"], e + 1)
                    nc.gpsimd.tensor_tensor(w13[:, 1, e], w13_raw[:, e], w13[:, 0, e].bitcast(F32), ALU.subtract).then_inc(s["w_lo"], 1)

            @block.scalar
            def _(act):
                nc.scalar.preload_act_table_set("natural_log_exp_and_others")
                act.wait_ge(s["wa_in"], 16 * 6)
                nc.scalar.mul(wa[:, A_KR:A_KR + ROPE], wa[:, A_KR:A_KR + ROPE], 1.0 / H).then_inc(s["wa_scaled"], 1)

                def norm_rstd(f, par):
                    act.wait_ge(const_in, 16)
                    act.wait_ge(s["var"], f * BT + BT)
                    nc.scalar.activation(lnv[:, :], mv[:, par, :, 1], ACT.Ln, bias=cst("eps")[:, 0:1]).then_inc(s["ln_log"], 1)
                    act.wait_ge(s["ln_log"], f + 1)
                    nc.scalar.activation(rstd[:, par, :], lnv[:, :], ACT.Exp, scale=-0.5).then_inc(s["ln_rstd"], 1)

                def keep_xn(f):
                    act.wait_ge(s["xn_ready"], f * BT + BT)
                    nc.scalar.copy(xn_all[:, bass.ds(f * BT, BT), :], xn[:, :, :]).then_inc(s["xn_kept"], 1)

                def split_x(f, par, uses):
                    act.wait_ge(s["xT_ps"], f + 1)
                    nc.scalar.copy(xt[:, :], pf[:, 1, :]).then_inc(s["xt_ready"], 1)
                    act.wait_ge(xt_out[par], 16 * SPB * (uses + 1))
                    nc.scalar.copy(xhl[par][:, 0, :], pf[:, 1, :]).then_inc(s["xh_ready"], 1)

                def small(f):
                    act.wait_ge(s["a_ps"], f + 1)
                    for t in range(BT):
                        nc.scalar.activation(sqj[:, t, 0:QL], pa[:, t, 0:QL], ACT.Square, accum_out=ssq[:, 0, t:t + 1]).then_inc(s["sq"], 1)
                        nc.scalar.activation(sqj[:, t, QL:P], pa[:, t, A_CKV:A_CKV + KL], ACT.Square, accum_out=ssq[:, 1, t:t + 1]).then_inc(s["sq"], 1)
                    nc.scalar.copy(misc[:, bass.ds(f * BT, BT), :], pa[:, :, A_IMP:A_IMP + 4]).then_inc(s["misc_ready"], 1)

                def small_exps(f):
                    act.wait_ge(s["sq"], f * 2 * BT + 2 * BT)
                    nc.scalar.activation(lns[:, 0, :], ssq[:, 0, :], ACT.Ln, bias=cst("eps")[:, 1:2], scale=1.0 / QL).then_inc(s["rms_log"], 1)
                    nc.scalar.activation(lns[:, 1, :], ssq[:, 1, :], ACT.Ln, bias=cst("eps")[:, 1:2], scale=1.0 / KL).then_inc(s["rms_log"], 1)
                    act.wait_ge(s["rms_log"], f * 2 + 2)
                    nc.scalar.activation(rr[:, :, :], lns[:, :, :], ACT.Exp, scale=-0.5).then_inc(s["rr_ready"], 1)
                    act.wait_ge(s["rdiff"], f + 1)
                    nc.scalar.activation(rex[:, :, :], rd[:, :, :], ACT.Exp).then_inc(s["rexp"], 1)

                def split_n(f, par, uses):
                    act.wait_ge(s["nT_ps"], f + 1)
                    act.wait_ge(nt_out[par], 16 * SPB * (uses + 1))
                    nc.scalar.copy(nhl[par][:, 0, :], pf[:, 0, :]).then_inc(s["nh_ready"], 1)
                    act.wait_ge(s["krT_ps"], f + 1)
                    act.wait_ge(kr_out[par], 16 * SPB * (uses + 1))
                    nc.scalar.copy(krt[par][:, :], pf[0:ROPE, 1, :]).then_inc(s["krt_ready"], 1)

                def silus(k, e):
                    for c in range(HC):
                        n = k * (E1 * HC) + e * HC + c
                        act.wait_ge(s["h_ps"], n + 1)
                        act.wait_ge(s["hid_ready"], n + 1)
                        nc.scalar.activation(silu[:, c, :], ph[:, 2 * c, :], ACT.Silu).then_inc(s["silu_ready"], 1)

                def body(j, last):
                    for par in range(2):
                        k = j * 2 + par
                        front = not (last and par)
                        f, fp, uses = k + 1, 1 - par, j + par
                        for e in range(E1):
                            silus(k, e)
                            if not front:
                                continue
                            if e == 1:
                                keep_xn(f)
                            if e == 2:
                                split_x(f, fp, uses)
                            if e == 4:
                                small(f)
                            if e == 5:
                                nc.scalar.preload_act_table_set("natural_log_exp_and_others")
                                small_exps(f)
                                if not last:
                                    norm_rstd(f + 1, par)
                            if e == 8:
                                split_n(f, fp, uses)

                act.sem_inc(s["krt_ready"], 1)
                norm_rstd(0, 0)
                keep_xn(0)
                split_x(0, 0, 0)
                for e in range(E1):
                    if e % 3 == 0:
                        act.wait_ge(w_in[e // 3], 64 if e // 3 == 2 else 32)
                    if e == 3:
                        small(0)
                        small_exps(0)
                        norm_rstd(1, 1)
                    if e == 6:
                        split_n(0, 0, 0)
                    nc.scalar.copy(w13[:, 0, e], w13_raw[:, e]).then_inc(s["w_hi"], 1)
                with act.Fori(0, NBLK // 2 - 1) as j:
                    body(j, False)
                body(NBLK // 2 - 1, True)

            @block.vector
            def _(dve):
                def norm_stats(f, par, uses):
                    dve.wait_ge(x_in[par], 16 * (uses + 1))
                    for t in range(BT):
                        nc.vector.bn_stats(stats[:, t, :], xb[:, par, t, :]).then_inc(s["bn"], 1)
                    wait_alone(dve, s["bn"], f * BT + BT, s["gate"])
                    for t in range(BT):
                        nc.vector.bn_aggr(mv[:, par, t, :], stats[:, t, :]).then_inc(s["var"], 1)

                def norm_apply(f, par):
                    dve.wait_ge(s["ln_rstd"], f + 1)
                    for t in range(BT):
                        nc.vector.tensor_scalar(xn[:, t, :], xb[:, par, t, :], mv[:, par, t, 0:1], rstd[:, par, t:t + 1],
                                                ALU.subtract, ALU.mult).then_inc(s["xn_ready"], 1)

                def x_lo(f, par):
                    dve.wait_ge(s["xh_ready"], f + 1)
                    nc.vector.tensor_tensor(xhl[par][:, 1, :], pf[:, 1, :], xhl[par][:, 0, :].bitcast(F32), ALU.subtract).then_inc(s["xl_ready"], 1)

                def chain(f, n, ins):
                    ins.then_inc(s["rchain"], 1)
                    dve.wait_ge(s["rchain"], f * 9 + n)

                def small_parts(f):
                    dve.wait_ge(s["misc_ready"], f + 1)
                    nc.vector.tensor_reduce(rmx[:, :], pa[:, :, A_ROUT:A_N], X, ALU.max).then_inc(s["rmax"], 1)
                    dve.wait_ge(s["rmax"], f + 1)
                    nc.vector.tensor_tensor(rd[:, :, :], pa[:, :, A_ROUT:A_N], rmx[:, :].unsqueeze(2).to_broadcast([P, BT, NE]),
                                            ALU.subtract).then_inc(s["rdiff"], 1)
                    for q in range(SPB):
                        t = slice(q * NT, (q + 1) * NT)
                        src = pa[:, t, A_KR:A_KR + ROPE]
                        nc.vector.tensor_tensor(kcos[:, t, :], src, cst("cos").rearrange("p (t c) -> p t c", c=ROPE), ALU.mult).then_inc(s["kr_part"], 1)
                        nc.vector.tensor_tensor(ksin[:, t, :].rearrange("p t (a c) -> p t a c", a=2),
                                                src.rearrange("p t (a c) -> p t a c", a=2)[:, :, ::-1, :],
                                                cst("sin").rearrange("p (t a c) -> p t a c", a=2, c=HALF), ALU.mult).then_inc(s["kr_part"], 1)

                def small_norms(f):
                    dve.wait_ge(s["rr_ready"], f + 1)
                    nc.vector.tensor_tensor(nqc[:, :, 0:QL], pa[:, :, 0:QL], rr[:, 0, :].unsqueeze(2).to_broadcast([P, BT, QL]),
                                            ALU.mult).then_inc(s["nq_ready"], 1)
                    nc.vector.tensor_tensor(nqc[:, :, QL:P], pa[:, :, A_CKV:A_CKV + KL], rr[:, 1, :].unsqueeze(2).to_broadcast([P, BT, KL]),
                                            ALU.mult).then_inc(s["nq_ready"], 1)
                    dve.wait_ge(s["kr_part"], f * (2 * SPB) + 2 * SPB)
                    nc.vector.tensor_tensor(kr[:, :, :], kcos[:, :, :], ksin[:, :, :], ALU.add).then_inc(s["kr_ready"], 1)

                def router(f):
                    dve.wait_ge(s["rexp"], f + 1)
                    chain(f, 1, nc.vector.tensor_reduce(rsum[:, :], rex[:, :, :], X, ALU.add))
                    chain(f, 2, nc.vector.reciprocal(rrec[:, :], rsum[:, :]))
                    chain(f, 3, nc.vector.tensor_tensor(rp[:, :, :], rex[:, :, :], rrec[:, :].unsqueeze(2).to_broadcast([P, BT, NE]), ALU.mult))
                    other = rp[:, :, :].unsqueeze(2).to_broadcast([P, BT, NE, NE])
                    own = rp[:, :, :].unsqueeze(3).to_broadcast([P, BT, NE, NE])
                    chain(f, 4, nc.vector.tensor_tensor(req[:, :, :, :], other, own, ALU.is_equal))
                    tri = cst("tri").unsqueeze(1).to_broadcast([P, BT, NE * NE])
                    chain(f, 5, nc.vector.tensor_tensor(rgt[:, :, :, :].rearrange("p t e f -> p t (e f)"),
                                                        req[:, :, :, :].rearrange("p t e f -> p t (e f)"), tri, ALU.mult))

                def router_weights(f, par):
                    other = rp[:, :, :].unsqueeze(2).to_broadcast([P, BT, NE, NE])
                    own = rp[:, :, :].unsqueeze(3).to_broadcast([P, BT, NE, NE])
                    chain(f, 6, nc.vector.tensor_tensor(req[:, :, :, :], other, own, ALU.is_gt))
                    chain(f, 7, nc.vector.tensor_tensor(rgt[:, :, :, :], rgt[:, :, :, :], req[:, :, :, :], ALU.add))
                    chain(f, 8, nc.vector.tensor_reduce(rank[:, :, :], rgt[:, :, :, :], X, ALU.add))
                    chain(f, 9, nc.vector.scalar_tensor_tensor(rsel[:, :, :], rank[:, :, :], 1.5, rp[:, :, :], ALU.is_lt, ALU.mult))
                    nc.vector.tensor_reduce(rs2[:, :], rsel[:, :, :], X, ALU.add).then_inc(s["cw_ready"], 1)
                    dve.wait_ge(s["cw_ready"], f * 3 + 1)
                    nc.vector.reciprocal(rr2[:, :], rs2[:, :]).then_inc(s["cw_ready"], 1)
                    dve.wait_ge(s["cw_ready"], f * 3 + 2)
                    nc.vector.tensor_tensor(cw[par][:, :, :], rsel[:, :, :], rr2[:, :].unsqueeze(2).to_broadcast([P, BT, NE]),
                                            ALU.mult).then_inc(s["cw_ready"], 1)

                def n_lo(f, par):
                    dve.wait_ge(s["nh_ready"], f + 1)
                    nc.vector.tensor_tensor(nhl[par][:, 1, :], pf[:, 0, :], nhl[par][:, 0, :].bitcast(F32), ALU.subtract).then_inc(s["nl_ready"], 1)

                def hidden(k, e, par):
                    for c in range(HC):
                        n = k * (E1 * HC) + e * HC + c
                        dve.wait_ge(s["silu_ready"], n + 1)
                        if c == 0:
                            dve.wait_ge(s["y_ps"], k * E1 + e + 1)
                        nc.vector.tensor_tensor(hid[:, (par + e) % 2, c, :], ph[:, 2 * c + 1, :], silu[:, c, :],
                                                ALU.mult).then_inc(s["hid_ready"], 1)

                def accumulate(k, e, par, uses):
                    m = k * E1 + e
                    dve.wait_ge(s["y_ps"], m + 3)
                    dve.wait_ge(s["acc_ready"], m + 2)
                    if e == 0:
                        dve.wait_ge(s["cw_ready"], k * 3 + 3)
                        dve.wait_ge(acc_out[par], 16 * (uses + 1))
                    y = py[:, (par + e) % 2, :].rearrange("p (t c) -> p t c", c=C)
                    if e == NE:
                        nc.vector.tensor_tensor(acc[:, par], y, acc[:, par], ALU.add).then_inc(s["acc_ready"], 1)
                        return
                    so_far = xb if e == 0 else acc
                    for t in range(BT):
                        ins = nc.vector.scalar_tensor_tensor(acc[:, par, t, :], y[:, t, :], cw[par][:, t, e:e + 1], so_far[:, par, t, :],
                                                             ALU.mult, ALU.add)
                    ins.then_inc(s["acc_ready"], 1)

                def body(j, last):
                    for par in range(2):
                        k = j * 2 + par
                        front = not (last and par)
                        f, fp, uses = k + 1, 1 - par, j + par
                        for e in range(E1):
                            hidden(k, e, par)
                            if e:
                                accumulate(k, e - 1, par, j)
                            if not front:
                                continue
                            if e == 0:
                                norm_apply(f, fp)
                            if e == 2:
                                x_lo(f, fp)
                            if e == 4:
                                if not last:
                                    norm_stats(f + 1, par, j + 1)
                                small_parts(f)
                            if e == 5:
                                small_norms(f)
                            if e == 6:
                                router(f)
                            if e == 7:
                                router_weights(f, fp)
                        if front:
                            n_lo(f, fp)
                        accumulate(k, E1 - 1, par, j)

                dve.sem_inc(s["hid_ready"], 2)
                dve.sem_inc(s["acc_ready"], 2)
                dve.sem_inc(s["nl_ready"], 1)
                norm_stats(0, 0, 0)
                dve.wait_ge(s["var"], BT)
                norm_stats(1, 1, 0)
                norm_apply(0, 0)
                x_lo(0, 0)
                small_parts(0)
                small_norms(0)
                router(0)
                router_weights(0, 0)
                n_lo(0, 0)
                with dve.Fori(0, NBLK // 2 - 1) as j:
                    body(j, False)
                body(NBLK // 2 - 1, True)

            @block.tensor
            def _(pe):
                def x_transposes(f):
                    pe.wait_ge(s["xn_ready"], f * BT + BT)
                    pe.wait_ge(s["krt_ready"], f + 1)
                    for t in range(BT):
                        last = nc.tensor.transpose(pf[:, 1, t * P:(t + 1) * P], xn[:, t, :], ident)
                    last.then_inc(s["xT_ps"], 1)

                def small(f):
                    pe.wait_ge(s["xt_ready"], f + 1)
                    pe.wait_ge(s["nl_ready"], f + 1)
                    for t in range(BT):
                        if t == BT // 2:
                            pe.wait_ge(s["xl_ready"], f + 1)
                        last = nc.tensor.matmul(pa[:, t, 0:A_N], xt[:, t * P:(t + 1) * P], wa[:, :], start=True, stop=True)
                    last.then_inc(s["a_ps"], 1)

                def n_transposes(f):
                    pe.wait_ge(s["nq_ready"], f * 2 + 2)
                    pe.wait_ge(s["misc_ready"], f + 1)
                    pe.wait_ge(s["kr_ready"], f + 1)
                    for t in range(BT):
                        last = nc.tensor.transpose(pf[:, 0, t * P:(t + 1) * P], nqc[:, t, :], ident)
                    last.then_inc(s["nT_ps"], 1)
                    for t in range(BT):
                        last = nc.tensor.transpose(pf[0:ROPE, 1, t * P:(t + 1) * P], kr[:, t, :], ident)
                    last.then_inc(s["krT_ps"], 1)

                def up(k, e, par):
                    pe.wait_ge(s["w_lo"], e + 1)
                    for c in range(HC):
                        pe.wait_ge(s["hid_ready"], k * (E1 * HC) + e * HC + c + 1)
                        for j in range(2):
                            w = [w13[:, hl, e, j, c * P:(c + 1) * P] for hl in range(2)]
                            x = [xhl[par][:, hl, :] for hl in range(2)]
                            for n, (wi, xi) in enumerate([(0, 0), (0, 1), (1, 0)]):
                                last = nc.tensor.matmul(ph[:, 2 * c + j, :], w[wi], x[xi], start=(n == 0), stop=(n == 2))
                        last.then_inc(s["h_ps"], 1)

                def down(k, e, par):
                    m = k * E1 + e
                    pe.wait_ge(s["hid_ready"], m * HC + HC + 2)
                    pe.wait_ge(s["acc_ready"], m + 1)
                    for t in range(BT):
                        for c in range(HC):
                            last = nc.tensor.matmul(py[:, (par + e) % 2, t * C:(t + 1) * C], hid[:, (par + e) % 2, c, t * P:(t + 1) * P],
                                                    w2[:, e, c, :], start=(c == 0), stop=(c == HC - 1))
                    last.then_inc(s["y_ps"], 1)

                def body(j, last):
                    for par in range(2):
                        k = j * 2 + par
                        front = not (last and par)
                        f = k + 1
                        for e in range(E1):
                            up(k, e, par)
                            if e:
                                down(k, e - 1, par)
                            if front and e == 1:
                                x_transposes(f)
                            if front and e == 3:
                                small(f)
                        if front:
                            n_transposes(f)
                        down(k, E1 - 1, par)

                pe.sem_inc(s["y_ps"], 2)
                pe.wait_ge(const_in, 16)
                x_transposes(0)
                pe.wait_ge(s["wa_in"], 16 * 6)
                pe.wait_ge(s["wa_scaled"], 1)
                small(0)
                n_transposes(0)
                pe.wait_ge(s["w2_in"], 32)
                pe.wait_ge(s["xl_ready"], 1)
                with pe.Fori(0, NBLK // 2 - 1) as j:
                    body(j, False)
                body(NBLK // 2 - 1, True)


def load_grouped(eng, dst, rows, k_src, v_src, order, done):
    n = 0
    for g in range(G):
        for (at, width, src, first, per_head) in order:
            s = src.rearrange("p (h c) -> p h c", c=per_head)[:, g * HG:(g + 1) * HG, first:first + width]
            d = dst[rows, g, 0:QC].rearrange("p (i c) -> p i c", c=D)[:, :, at:at + width]
            eng.dma_start(d, s).then_inc(done, 16)
            n += 1
    return n


def select(nc, a, sem, cst, misc, xn_all, gates, ks_d, vs_d):
    ctx = ExitStack()
    with ctx:
        def sb(name, shape, dt=F32):
            return ctx.enter_context(nc.sbuf_tensor(name, shape, dt))

        def ps(name, shape, dt=F32):
            return ctx.enter_context(nc.psum_tensor(name, shape, dt))

        NS = B * KEEP // P
        wsel = sb("wsel", [P, G, GC])
        score = [sb(f"score{i}", [B, T]) for i in range(5)]
        best = sb("best", [B, 4, 8])
        chosen = sb("chosen", [B, T])
        ones = sb("ones_row", [B, T])
        count = sb("count", [B, T])
        place = sb("place", [B, T])
        place_t = sb("place_t", [P, B, NT])
        onehot = sb("onehot", [P, B * NT, KEEP])
        xsel = sb("xsel", [P, B * KEEP])
        kcos = sb("s_kcos", [P, 2, HG, ROPE])
        ksin = sb("s_ksin", [P, 2, HG, ROPE])
        ktok = sb("s_ktok", [P, NS, H, D])
        vtok = sb("s_vtok", [P, NS, H * VH])
        kt = sb("s_kt", [P, NS, P // KEEP, H, KEEP])
        glog = sb("glog", [P, B, 3])
        gmx = sb("gmx", [P, B])
        gd = sb("gd", [P, B, 3])
        gex = sb("gex", [P, B, 3])
        gsum = sb("gsum", [P, B])
        grec = sb("grec", [P, B])

        p_row = ps("p_row", [P, 512])
        p_place = ps("p_place", [P, 512])
        p_sel = ps("p_sel", [P, 512])
        p_gate = ps("p_gate", [P, 512])
        p_k = ps("p_k", [P, 2, 512])
        p_t = ps("p_t", [P, 2, 512])

        names = ("w_in v_in row_ps gate_ps score_in round ones_set place_done place_ps place_t_done onehot_done sel_ps sel_done "
                 "k_ps k_cos k_sin k_used k_nope v_done k_tok kT_ps kt_done kt_const gred gdiff gexp gchain k_out v_out").split()
        s = {n: sem("s_" + n) for n in names}
        ident = cst("ident")
        nw = 2 * G

        with nc.Block() as block:
            @block.sync
            def _(sp):
                load_grouped(sp, wsel, slice(0, P), None, None,
                             [(0, ROPE, a["L0_attn_w_selk"], NOPE, D), (ROPE, NOPE, a["L0_attn_w_selk"], 0, D)], s["w_in"])
                for g in range(G):
                    sp.dma_start(wsel[:, g, QC:GC], a["L0_attn_w_selv"][:, g * HG * VH:(g + 1) * HG * VH]).then_inc(s["v_in"], 16)
                for n in range(NS):
                    sp.wait_ge(s["v_done"], (n + 1) * G)
                    sp.dma_start(vs_d[n * (P // KEEP):(n + 1) * (P // KEEP)].rearrange("b k c -> (b k) c"), vtok[:, n, :]).then_inc(s["v_out"], 16)
                    sp.wait_ge(s["kt_done"], (n + 1) * G)
                    sp.wait_ge(s["kt_const"], 1)
                    for q in range(P // KEEP):
                        sp.dma_start(ks_d[n * (P // KEEP) + q], kt[:, n, q].rearrange("p h c -> p (h c)")).then_inc(s["k_out"], 16)
                sp.wait_ge(s["v_out"], 16 * NS)
                sp.wait_ge(s["k_out"], 16 * B)

            @block.tensor
            def _(pe):
                for t in range(NT):
                    imp = misc[:, :, 0:1].rearrange("p (b t) c -> p t (b c)", t=NT)[:, t, :]
                    last = nc.tensor.transpose(p_row[0:B, t * P:(t + 1) * P], imp, ident)
                last.then_inc(s["row_ps"], 1)
                nc.tensor.matmul(p_gate[:, 0:B * NT * 3], cst("mean"), misc[:, :, 1:4], start=True, stop=True).then_inc(s["gate_ps"], 1)
                pe.wait_ge(s["place_done"], 1)
                for t in range(NT):
                    last = nc.tensor.transpose(p_place[:, t * B:(t + 1) * B], place[:, t * P:(t + 1) * P], ident[0:B, 0:B])
                last.then_inc(s["place_ps"], 1)
                pe.wait_ge(s["onehot_done"], 1)
                for b in range(B):
                    for t in range(NT):
                        last = nc.tensor.matmul(p_sel[:, b * KEEP:(b + 1) * KEEP], xn_all[:, b * NT + t, :], onehot[:, b * NT + t, :],
                                                start=(t == 0), stop=(t == NT - 1))
                last.then_inc(s["sel_ps"], 1)
                pe.wait_ge(s["sel_done"], 1)
                pe.wait_ge(s["w_in"], 16 * nw)
                pe.wait_ge(s["v_in"], 16 * G)

                def project(u):
                    n, g = divmod(u, G)
                    if u >= 2:
                        pe.wait_ge(s["k_used"], 2 * (u - 1))
                        pe.wait_ge(s["k_nope"], u - 1)
                        pe.wait_ge(s["v_done"], u - 1)
                    nc.tensor.matmul(p_k[:, u % 2, :], xsel[:, n * P:(n + 1) * P], wsel[:, g, :], start=True, stop=True).then_inc(s["k_ps"], 1)

                def transposes(u):
                    n, g = divmod(u, G)
                    pe.wait_ge(s["k_tok"], u + 1)
                    pe.wait_ge(s["k_nope"], u + 1)
                    if u >= 2:
                        pe.wait_ge(s["kt_done"], u - 1)
                    for i in range(HG):
                        last = nc.tensor.transpose(p_t[0:D, u % 2, i * P:(i + 1) * P], ktok[:, n, g * HG + i, :], ident)
                    last.then_inc(s["kT_ps"], 1)

                for u in range(NS * G):
                    project(u)
                    if u >= 2:
                        transposes(u - 2)
                transposes(NS * G - 2)
                transposes(NS * G - 1)

            @block.vector
            def _(dve):
                nc.vector.memset(ones[:, :], 1.0).then_inc(s["ones_set"], 1)
                nc.vector.tensor_copy(kt[D:P].rearrange("p a b c d -> p (a b c d)"),
                                      cst("mrow")[D:P, BR2:BR2 + 1].to_broadcast([P - D, NS * P * H])).then_inc(s["kt_const"], 1)
                dve.wait_ge(s["row_ps"], 1)
                nc.vector.tensor_copy(score[0][:, :], p_row[0:B, 0:T]).then_inc(s["round"], 1)
                r = 1
                for n in range(KEEP // 8):
                    dve.wait_ge(s["round"], r)
                    nc.vector.max(best[:, n, :], score[n][:, :]).then_inc(s["round"], 1)
                    dve.wait_ge(s["round"], r + 1)
                    nc.vector.match_replace(score[n + 1][:, :], best[:, n, :], score[n][:, :], -3e38).then_inc(s["round"], 1)
                    r += 2
                dve.wait_ge(s["round"], r)
                nc.vector.tensor_tensor(chosen[:, :], score[0][:, :], score[KEEP // 8][:, :], ALU.not_equal).then_inc(s["round"], 1)
                dve.wait_ge(s["round"], r + 1)
                dve.wait_ge(s["ones_set"], 1)
                nc.vector.tensor_tensor_scan(count[:, :], ones[:, :], chosen[:, :], 0.0, ALU.mult, ALU.add).then_inc(s["round"], 1)
                dve.wait_ge(s["round"], r + 2)
                nc.vector.tensor_tensor(place[:, :], count[:, :], chosen[:, :], ALU.mult).then_inc(s["place_done"], 1)
                dve.wait_ge(s["gate_ps"], 1)
                nc.vector.tensor_reduce(glog[:, :, :], p_gate[:, 0:B * NT * 3].rearrange("p (b t c) -> p b c t", t=NT, c=3), X, ALU.add).then_inc(s["gchain"], 1)
                dve.wait_ge(s["gchain"], 1)
                nc.vector.tensor_reduce(gmx[:, :], glog[:, :, :], X, ALU.max).then_inc(s["gchain"], 1)
                dve.wait_ge(s["gchain"], 2)
                nc.vector.tensor_tensor(gd[:, :, :], glog[:, :, :], gmx[:, :].unsqueeze(2).to_broadcast([P, B, 3]), ALU.subtract).then_inc(s["gdiff"], 1)
                dve.wait_ge(s["place_ps"], 1)
                nc.vector.tensor_copy(place_t[:, :, :].rearrange("p b t -> p t b"), p_place[:, 0:B * NT].rearrange("p (t b) -> p t b", t=NT)).then_inc(s["place_t_done"], 1)
                dve.wait_ge(s["place_t_done"], 1)
                nc.vector.tensor_tensor(onehot[:, :, :], cst("iota").unsqueeze(1).to_broadcast([P, B * NT, KEEP]),
                                        place_t[:, :, :].rearrange("p b t -> p (b t)").unsqueeze(2).to_broadcast([P, B * NT, KEEP]),
                                        ALU.is_equal).then_inc(s["onehot_done"], 1)
                dve.wait_ge(s["gexp"], 1)
                nc.vector.tensor_reduce(gsum[:, :], gex[:, :, :], X, ALU.add).then_inc(s["gchain"], 1)
                dve.wait_ge(s["gchain"], 3)
                nc.vector.reciprocal(grec[:, :], gsum[:, :]).then_inc(s["gchain"], 1)
                dve.wait_ge(s["gchain"], 4)
                nc.vector.tensor_tensor(gates[:, :, :], gex[:, :, :], grec[:, :].unsqueeze(2).to_broadcast([P, B, 3]), ALU.mult).then_inc(s["gchain"], 1)
                dve.wait_ge(s["sel_ps"], 1)
                nc.vector.tensor_copy(xsel[:, :], p_sel[:, :]).then_inc(s["sel_done"], 1)
                for u in range(NS * G):
                    n, g = divmod(u, G)
                    dve.wait_ge(s["k_ps"], u + 1)
                    if u >= 2:
                        dve.wait_ge(s["k_tok"], u - 1)
                    src = p_k[:, u % 2, 0:QC].rearrange("p (i c) -> p i c", c=D)[:, :, 0:ROPE]
                    nc.vector.tensor_tensor(kcos[:, u % 2], src, cst("scos").unsqueeze(1).to_broadcast([P, HG, ROPE]), ALU.mult).then_inc(s["k_used"], 1)
                    nc.vector.tensor_tensor(ksin[:, u % 2].rearrange("p i (a c) -> p i a c", a=2),
                                            src.rearrange("p i (a c) -> p i a c", a=2)[:, :, ::-1, :],
                                            cst("ssin").rearrange("p (a c) -> p a c", a=2).unsqueeze(1).to_broadcast([P, HG, 2, HALF]),
                                            ALU.mult).then_inc(s["k_used"], 1)

            @block.gpsimd
            def _(pool):
                for u in range(NS * G):
                    n, g = divmod(u, G)
                    pool.wait_ge(s["k_used"], 2 * (u + 1))
                    nc.gpsimd.tensor_tensor(ktok[:, n, g * HG:(g + 1) * HG, 0:ROPE], kcos[:, u % 2], ksin[:, u % 2], ALU.add).then_inc(s["k_tok"], 1)

            @block.scalar
            def _(act):
                def transposed(u):
                    n, g = divmod(u, G)
                    act.wait_ge(s["kT_ps"], u + 1)
                    src = p_t[0:D, u % 2, :].rearrange("p (i q c) -> p q i c", i=HG, c=KEEP)
                    nc.scalar.copy(kt[0:D, n, :, g * HG:(g + 1) * HG, :], src).then_inc(s["kt_done"], 1)

                act.wait_ge(s["gdiff"], 1)
                nc.scalar.activation(gex[:, :, :], gd[:, :, :], ACT.Exp).then_inc(s["gexp"], 1)
                for u in range(NS * G):
                    n, g = divmod(u, G)
                    act.wait_ge(s["k_used"], 2 * (u + 1))
                    nc.scalar.copy(ktok[:, n, g * HG:(g + 1) * HG, ROPE:D],
                                   p_k[:, u % 2, 0:QC].rearrange("p (i c) -> p i c", c=D)[:, :, ROPE:D]).then_inc(s["k_nope"], 1)
                    nc.scalar.copy(vtok[:, n, g * HG * VH:(g + 1) * HG * VH], p_k[:, u % 2, QC:GC]).then_inc(s["v_done"], 1)
                    if u >= 2:
                        transposed(u - 2)
                transposed(NS * G - 2)
                transposed(NS * G - 1)


def attend(nc, a, sem, cst, gates, xt_d, nt_d, kr_d, res_d, ks_d, vs_d, out):
    ctx = ExitStack()
    with ctx:
        def sb(name, shape, dt=F32):
            return ctx.enter_context(nc.sbuf_tensor(name, shape, dt))

        def ps(name, shape, dt=F32):
            return ctx.enter_context(nc.psum_tensor(name, shape, dt))

        HT = HG * T
        TQ = T + P
        wraw = sb("wraw", [P, G, GC])
        nraw = sb("nraw", [P, H * NOPE])
        gain = sb("gain", [P, 1])
        wq = sb("wq", [P, 2, G, GC], F32R)
        wk = sb("wk", [P, 2, G, GC], F32R)
        wn = sb("wn", [P, 2, H * NOPE], F32R)
        wkraw = sb("wkraw", [P, G, GC])
        wp = sb("wp", [P, G, C])
        xt = sb("a_xt", [P, 2, T], F32R)
        nt = sb("a_nt", [P, 2, T], F32R)
        nk = sb("a_nk", [P, 2, T], F32R)
        krt = sb("a_krt", [ROPE, T])
        res = sb("a_res", [P, NT, C])
        ot = sb("a_ot", [P, NT, C])
        gcur = sb("gcur", [P, 3])
        ks = [sb(f"ks{i}", [P, HG, KEEP]) for i in range(2)]
        vc = [sb(f"vc{i}", [P, VH]) for i in range(2)]
        ksb = sb("ksb", [D, HG, KEEP], BF16)
        vbd = [sb(f"vbd{i}", [P, HG, VH]) for i in range(2)]
        rcos = {x: sb(f"rcos_{x}", [P, NT, HG, ROPE]) for x in "qk"}
        rsin = {x: sb(f"rsin_{x}", [P, NT, HG, ROPE]) for x in "qk"}
        tok = {x: sb(f"tok_{x}", [P, NT, HG, D]) for x in "qk"}
        qt = [sb(f"qt{i}", [P, HG, T]) for i in range(2)]
        kw = [sb(f"kw{i}", [P, HG, T]) for i in range(2)]
        k1 = [sb(f"k1{i}", [P, HG, T]) for i in range(2)]
        qb = sb("qb", [D, HG, T], BF16)
        kwb = sb("kwb", [D, HG, T], BF16)
        k1b = sb("k1b", [D, HG, T], BF16)
        v1 = [sb(f"v1{i}", [P, NT, HG * VH]) for i in range(G)]
        vw = [sb(f"vw{i}", [P, NT, HG * VH]) for i in range(2)]
        mtok = sb("mtok", [P, NT, P])
        junk = sb("junk", [P, 16, T], BF16)
        prob = [sb(f"prob{i}", [P, HG, 2, TQ]) for i in range(2)]
        prob2 = sb("prob2", [P, T])
        lden = sb("lden", [P, 3, T])
        rden = sb("rden", [P, 3, T])
        o1, o3, o2, o13 = (sb(n, [P, T]) for n in ("o1", "o3", "o2", "o13"))
        att = sb("att", [P, G, T])

        pj = ps("pj", [P, 2, 512])
        mx = [ps(f"mx{i}", [P, 512]) for i in range(2)]
        sc = ps("sc", [P, 2, 512])
        av = ps("av", [P, 2, T])
        dn = ps("dn", [P, 2, T])

        names = ("raw_zero w_in kw_in g_in p_in n_in scaled w_hi w_lo mtok_zero rows_set xt_in nt_in nk_in kr_in res_in out_done "
                 "pq pkw kn_ps trq_ps trk_ps mx_ps mT_ps sc_ps s2_ps av_ps av2_ps op_ps "
                 "rq rk q_copied k_copied q_add k_add kn_copied kr_copied k1b_ready ksb_ready qb_ready kwb_ready qt_ready kt_ready mrow "
                 "max_op exp_done masked vbd_ready g_ready lden_ready n_rec n13 n2 att13 att_ready out_ready gate pgate").split()
        s = {n: sem("a_" + n) for n in names}
        ks_in = [sem(f"a_ks_in{i}") for i in range(2)]
        vc_in = [sem(f"a_vc_in{i}") for i in range(2)]
        ident = cst("ident")
        cos = cst("cos").rearrange("p (t c) -> p t c", c=ROPE)
        sin = cst("sin").rearrange("p (t a c) -> p t a c", a=2, c=HALF)
        out_v = out.rearrange("b (t p) c -> b p t c", p=P)
        res_v = res_d.rearrange("(b t p) c -> b p t c", t=NT, p=P)
        RAW = 16 * 2 * G

        def nxt(b, g, d=1):
            return (b, g + d) if g + d < G else (b + 1, g + d - G)

        def stages(last, g):
            return not (last and g >= G - 1), not (last and g >= G - 2)

        def step(b, g):
            return b * G + g

        def loop(eng, body):
            body(0, True, False)
            with eng.Fori(1, B - 1) as b:
                body(b, False, False)
            body(B - 1, False, True)

        with nc.Block() as block:
            @block.sync
            def _(sp):
                sp.wait_ge(s["raw_zero"], 2)
                load_grouped(sp, wraw, slice(0, QL), None, None,
                             [(0, ROPE, a["L0_attn_w_dq_rope"], 0, ROPE), (ROPE, NOPE, a["L0_attn_w_dq_nope"], 0, NOPE)], s["w_in"])
                for g in range(G):
                    sp.dma_start(wraw[QL:P, g, QC:GC], a["L0_attn_w_dv"][:, g * HG * VH:(g + 1) * HG * VH]).then_inc(s["w_in"], 16)
                sp.dma_start(nraw[QL:P, :], a["L0_attn_w_dk_nope"]).then_inc(s["n_in"], 16)
                sp.dma_start(gain[0:QL, :], a["L0_attn_g_qnorm"].rearrange("(p c) -> p c", c=1)).then_inc(s["g_in"], 16)
                sp.dma_start(gain[QL:P, :], a["L0_attn_g_kvnorm"].rearrange("(p c) -> p c", c=1)).then_inc(s["g_in"], 16)
                load_grouped(sp, wkraw, slice(0, P), None, None,
                             [(0, ROPE, a["L0_attn_w_wink"], NOPE, D), (ROPE, NOPE, a["L0_attn_w_wink"], 0, D)], s["kw_in"])
                for g in range(G):
                    sp.dma_start(wkraw[:, g, QC:GC], a["L0_attn_w_winv"][:, g * HG * VH:(g + 1) * HG * VH]).then_inc(s["kw_in"], 16)
                sp.dma_start(wp[:, :, :], a["L0_attn_w_proj"].rearrange("(g p) c -> p g c", p=P)).then_inc(s["p_in"], 16)

                def load_latents(b):
                    sp.dma_start(nt[:, :, :].bitcast(F32), nt_d[b]).then_inc(s["nt_in"], 16)

                def load_seq(b):
                    sp.dma_start(xt[:, :, :].bitcast(F32), xt_d[b]).then_inc(s["xt_in"], 16)
                    sp.dma_start(nk[QL:P, :, :].bitcast(F32), nt_d[b][QL:P]).then_inc(s["nk_in"], 16)
                    sp.dma_start(krt[:, :], kr_d[b]).then_inc(s["kr_in"], 16)

                def load_sel(b, g):
                    par = g % 2
                    sp.dma_start(ks[par][:, :, :].rearrange("p i c -> p (i c)"), ks_d[b][:, g * P:(g + 1) * P]).then_inc(ks_in[par], 16)
                    for i in range(HG):
                        at = (g * HG + i) * VH
                        sp.dma_start(vc[par][i * KEEP:(i + 1) * KEEP, :], vs_d[b][:, at:at + VH]).then_inc(vc_in[par], 16)

                def body(b, first, last):
                    for g in range(G):
                        n = nxt(b, g)
                        if g == 0 and not first:
                            sp.wait_ge(s["out_ready"], b)
                            sp.dma_start(out_v[bass.ds(b - 1, 1)].rearrange("b p t c -> p (b t) c"), ot[:, :, :]).then_inc(s["out_done"], 16)
                        if g == 1:
                            if not first:
                                sp.wait_ge(s["out_ready"], b)
                            sp.dma_start(res[:, :, :], res_v[bass.ds(b, 1)].rearrange("b p t c -> p (b t) c")).then_inc(s["res_in"], 16)
                            if not last:
                                sp.wait_ge(s["pq"], step(b, G - 1) * NT + NT)
                                load_latents(b + 1)
                        if g == 2 and not last:
                            sp.wait_ge(s["kn_ps"], step(*n) + 1)
                            sp.wait_ge(s["pkw"], step(*n) * NT + NT)
                            sp.wait_ge(s["kr_copied"], b * 2 + 2)
                            load_seq(b + 1)
                        if not (last and g >= 2):
                            sp.wait_ge(s["s2_ps"], step(b, g) + 1)
                            sp.wait_ge(s["vbd_ready"], step(b, g) + 1)
                            load_sel(*nxt(b, g, 2))

                load_latents(0)
                sp.wait_ge(s["rows_set"], 5)
                load_seq(0)
                load_sel(0, 0)
                load_sel(0, 1)
                loop(sp, body)
                sp.wait_ge(s["out_ready"], B)
                sp.dma_start(out_v[B - 1], ot[:, :, :]).then_inc(s["out_done"], 16)
                sp.wait_ge(s["out_done"], 16 * B)

            @block.tensor
            def _(pe):
                def project(w, x, g, t):
                    for n, (i, j) in enumerate([(0, 0), (1, 0), (0, 1)]):
                        last = nc.tensor.matmul(pj[:, t, :], x[:, j, t * P:(t + 1) * P], w[:, i, g, :], start=(n == 0), stop=(n == 2))
                    return last

                def q_project(b, g, t):
                    if g == 0 and t == 0:
                        pe.wait_ge(s["nt_in"], 16 * (b + 1))
                    if t == 0:
                        pe.wait_ge(s["kt_ready"], step(b, g) + 1)
                    project(wq, nt, g, t).then_inc(s["pq"], 1)

                def k_nope(b, g):
                    if g == 0:
                        pe.wait_ge(s["nk_in"], 16 * (b + 1))
                    pe.wait_ge(s["mrow"], step(b, g) * 4 + 4)
                    for n, (i, j) in enumerate([(0, 0), (0, 1), (1, 0)]):
                        last = nc.tensor.matmul(mx[0][:, 0:T], wn[:, i, g * P:(g + 1) * P], nk[:, j, :], start=(n == 0), stop=(n == 2))
                    last.then_inc(s["kn_ps"], 1)

                def kw_project(b, g):
                    if g == 0:
                        pe.wait_ge(s["xt_in"], 16 * (b + 1))
                    for t in range(NT):
                        done = (step(b, g) * NT + t + 1) * 2
                        pe.wait_ge(s["rq"], done)
                        pe.wait_ge(s["q_copied"], done)
                        project(wk, xt, g, t).then_inc(s["pkw"], 1)

                def transposes(x):
                    for i in range(HG):
                        for t in range(NT):
                            last = nc.tensor.transpose(pj[0:D, i // 2, (i % 2) * T + t * P:(i % 2) * T + (t + 1) * P], tok[x][:, t, i, :], ident)
                    return last

                def q_transposes(b, g):
                    done = (step(b, g) + 1) * 2 * NT
                    pe.wait_ge(s["rk"], done)
                    pe.wait_ge(s["k_copied"], done)
                    pe.wait_ge(s["q_add"], (step(b, g) + 2) * NT)
                    transposes("q").then_inc(s["trq_ps"], 1)

                def kw_transposes(b, g):
                    pe.wait_ge(s["qt_ready"], step(b, g) + 1)
                    pe.wait_ge(s["k_add"], (step(b, g) + 2) * NT)
                    transposes("k").then_inc(s["trk_ps"], 1)

                def rough(b, g, u):
                    st = step(b, g)
                    done = st * 17 + 4
                    if u == 0:
                        pe.wait_ge(s["qb_ready"], st + 1)
                        pe.wait_ge(s["k1b_ready"], st + 1)
                        pe.wait_ge(s["ksb_ready"], st + 1)
                        pe.wait_ge(s["kwb_ready"], st + 1)

                    def late(i, bank):
                        nc.tensor.matmul(bank[:, 0:T], qb[:, i, P:T], k1b[:, i, :], start=True, stop=True)
                        return nc.tensor.matmul(bank[:, T:2 * T], qb[:, i, P:T], kwb[:, i, :], start=True, stop=True)

                    def early(i, bank):
                        for j in range(2):
                            nc.tensor.matmul(bank[:, j * T:j * T + P], qb[:, i + j, 0:P], k1b[:, i + j, 0:P], start=True, stop=True)
                            last = nc.tensor.matmul(bank[:, j * T + P:j * T + T], qb[:, i + j, 0:P], kwb[:, i + j, 0:P], start=True, stop=True)
                        return last

                    if u == 0:
                        last = late(0, mx[1])
                    if u == 1:
                        last = early(0, mx[0])
                    if u == 2:
                        pe.wait_ge(s["max_op"], done + 2)
                        last = late(1, mx[1])
                    if u == 3:
                        pe.wait_ge(s["max_op"], done + 6)
                        last = late(2, mx[0])
                    if u == 4:
                        pe.wait_ge(s["max_op"], done + 8)
                        last = early(2, mx[1])
                    if u == 5:
                        pe.wait_ge(s["max_op"], done + 10)
                        last = late(3, mx[0])
                    if u == 6:
                        pe.wait_ge(s["max_op"], done + 14)
                        for t in range(NT):
                            for i in range(HG):
                                at = (t * HG + i) * KEEP
                                last = nc.tensor.matmul(mx[1][:, at:at + KEEP], qb[:, i, t * P:(t + 1) * P], ksb[:, i, :], start=True, stop=True)
                    last.then_inc(s["mx_ps"], 1)

                def max_transposes(b, g):
                    pe.wait_ge(s["max_op"], step(b, g) * 17 + 17 + 4)
                    for t in range(NT):
                        last = nc.tensor.transpose(mx[0][:, t * P:(t + 1) * P], mtok[:, t, :], ident)
                    last.then_inc(s["mT_ps"], 1)

                def scores(b, g, i):
                    st, par = step(b, g), g % 2
                    pe.wait_ge(s["mrow"], st * 4 + 4 + i + 1)
                    pe.wait_ge(s["exp_done"], st * 5 + 5 + i)
                    for j, k in enumerate((k1[par], kw[par])):
                        nc.tensor.matmul(sc[:, j, 0:T], k[:, i, 0:P], qt[par][:, i, :], start=True, stop=True)
                        last = nc.tensor.matmul(sc[:, j, T:TQ], k[:, i, P:T], qt[par][:, i, P:T], start=True, stop=True)
                    last.then_inc(s["sc_ps"], 1)

                def selected_scores(b, g):
                    st, par = step(b, g), g % 2
                    pe.wait_ge(s["exp_done"], st * 5 + 5 + 4)
                    pe.wait_ge(ks_in[par], (b * 2 + g // 2 + 1) * 16)
                    for i in range(HG):
                        last = nc.tensor.matmul(sc[i * KEEP:(i + 1) * KEEP, 0, 0:T], ks[par][:, i, :], qt[par][:, i, :], start=True, stop=True)
                    last.then_inc(s["s2_ps"], 1)

                def weigh(b, g, j, what):
                    st, par = step(b, g), g % 2
                    pe.wait_ge(s["n13"], st * 2 + 2)
                    v = vw[par] if j else v1[g]
                    for kt in range(NT):
                        for i in range(HG):
                            if kt == 0 and j == 0 and what:
                                pe.wait_ge(s["masked"], st * 4 + i + 1)
                            left = v[:, kt, i * VH:(i + 1) * VH] if what else cst("ones")
                            dst = (av if what else dn)[i * VH:(i + 1) * VH, j, kt * P:T]
                            right = prob[par][:, i, j, 0:T] if kt == 0 else prob[par][:, i, j, T:TQ]
                            last = nc.tensor.matmul(dst, left, right, start=(kt == 0), stop=(kt == NT - 1))
                    return last

                def weigh_selected(b, g):
                    st, par = step(b, g), g % 2
                    pe.wait_ge(s["exp_done"], st * 5 + 5 + 5)
                    pe.wait_ge(s["vbd_ready"], st + 1)
                    nc.tensor.matmul(mx[1][:, 0:T], vbd[par][:, :, :].rearrange("p i c -> p (i c)"), prob2[:, :], start=True, stop=True)
                    nc.tensor.matmul(mx[1][:, T:2 * T], cst("block"), prob2[:, :], start=True, stop=True).then_inc(s["av2_ps"], 1)

                def out_project(b):
                    pe.wait_ge(s["att_ready"], b * G + G + 1)
                    for t in range(NT):
                        for g in range(G):
                            last = nc.tensor.matmul(mx[1][:, t * C:(t + 1) * C], att[:, g, t * P:(t + 1) * P], wp[:, g, :],
                                                    start=(g == 0), stop=(g == G - 1))
                    last.then_inc(s["op_ps"], 1)

                def body(b, first, last):
                    for g in range(G):
                        n, m = nxt(b, g), nxt(b, g, 2)
                        prep, ahead = stages(last, g)
                        if prep:
                            kw_project(*n)
                        scores(b, g, 0)
                        if prep:
                            k_nope(*n)
                            q_transposes(*n)
                        scores(b, g, 1)
                        if prep:
                            kw_transposes(*n)
                        if g == 0 and not first:
                            out_project(b - 1)
                        scores(b, g, 2)
                        if ahead:
                            q_project(*m, 0)
                        if not (first and g == 0):
                            pe.wait_ge(s["n2"], step(b, g))
                        if g == 0 and not first:
                            pe.wait_ge(s["out_ready"], b)
                        if prep:
                            rough(*n, 0)
                            rough(*n, 1)
                        scores(b, g, 3)
                        if ahead:
                            q_project(*m, 1)
                        if prep:
                            rough(*n, 2)
                            rough(*n, 3)
                        selected_scores(b, g)
                        weigh(b, g, 0, True)
                        if prep:
                            rough(*n, 4)
                        weigh(b, g, 0, False)
                        if prep:
                            rough(*n, 5)
                        weigh(b, g, 1, True)
                        if prep:
                            rough(*n, 6)
                        weigh(b, g, 1, False).then_inc(s["av_ps"], 1)
                        if prep:
                            max_transposes(*n)
                        weigh_selected(b, g)

                for x in ("w_lo", "p_in", "rows_set"):
                    pe.wait_ge(s[x], {"w_lo": 3, "p_in": 16, "rows_set": 5}[x])
                for t in range(NT):
                    q_project(0, 0, t)
                kw_project(0, 0)
                k_nope(0, 0)
                q_transposes(0, 0)
                kw_transposes(0, 0)
                for t in range(NT):
                    q_project(0, 1, t)
                for u in range(7):
                    rough(0, 0, u)
                max_transposes(0, 0)
                loop(pe, body)
                out_project(B - 1)

            @block.scalar
            def _(act):
                def copies(b, g, t, x, rotated, done, v):
                    act.wait_ge(s[rotated], (step(b, g) * NT + t + 1) * 2)
                    nc.scalar.copy(tok[x][:, t, :, ROPE:D], pj[:, t, 0:QC].rearrange("p (i c) -> p i c", c=D)[:, :, ROPE:D]).then_inc(s[done], 1)
                    nc.scalar.copy(v[:, t, :], pj[:, t, QC:GC]).then_inc(s[done], 1)

                def q_copies(b, g, t):
                    copies(b, g, t, "q", "rq", "q_copied", v1[g])

                def k_copies(b, g):
                    for t in range(NT):
                        copies(b, g, t, "k", "rk", "k_copied", vw[g % 2])

                def knope_rows(b, g, heads):
                    act.wait_ge(s["kn_ps"], step(b, g) + 1)
                    for i in heads:
                        nc.scalar.copy(k1[g % 2][ROPE:D, i, :], mx[0][i * NOPE:(i + 1) * NOPE, 0:T]).then_inc(s["kn_copied"], 1)

                def transposed(b, g, ready, done, exact):
                    act.wait_ge(s[ready], step(b, g) + 1)
                    nc.scalar.copy(exact[g % 2][0:D].rearrange("p i c -> p (i c)"), pj[0:D, :, :].rearrange("p b c -> p (b c)")).then_inc(s[done], 1)

                def reciprocals(b, g):
                    st = step(b, g)
                    act.wait_ge(s["av_ps"], st + 1)
                    nc.scalar.activation(lden[:, 0:2, :], dn[:, :, :], ACT.Ln).then_inc(s["lden_ready"], 1)
                    act.wait_ge(s["av2_ps"], st + 1)
                    nc.scalar.activation(lden[:, 2, :], mx[1][:, T:2 * T], ACT.Ln).then_inc(s["lden_ready"], 1)
                    act.wait_ge(s["lden_ready"], st * 2 + 2)
                    nc.scalar.activation(rden[:, :, :], lden[:, :, :], ACT.Exp, scale=-1.0).then_inc(s["n_rec"], 1)

                def max_rows(b, g):
                    act.wait_ge(s["mT_ps"], step(b, g) + 1)
                    for i in range(HG):
                        nc.scalar.copy(qt[g % 2][D:P, i, :], mx[0][i * 32:(i + 1) * 32, 0:T]).then_inc(s["mrow"], 1)

                def exps(b, g, i):
                    act.wait_ge(s["sc_ps"], step(b, g) * 4 + i + 1)
                    nc.scalar.activation(prob[g % 2][:, i, :, :], sc[:, :, 0:TQ], ACT.Exp, scale=SCALE).then_inc(s["exp_done"], 1)

                def exp_selected(b, g):
                    act.wait_ge(s["s2_ps"], step(b, g) + 1)
                    nc.scalar.activation(prob2[:, :], sc[:, 0, 0:T], ACT.Exp, scale=SCALE).then_inc(s["exp_done"], 1)

                def body(b, first, last):
                    for g in range(G):
                        n, m = nxt(b, g), nxt(b, g, 2)
                        before = (b, g - 1) if g else (b - 1, G - 1)
                        prep, ahead = stages(last, g)
                        if not (first and g == 0):
                            reciprocals(*before)
                        if prep:
                            k_copies(*n)
                        exps(b, g, 0)
                        if prep:
                            knope_rows(*n, range(0, HG // 2))
                            transposed(*n, "trq_ps", "qt_ready", qt)
                            knope_rows(*n, range(HG // 2, HG))
                        exps(b, g, 1)
                        if prep:
                            transposed(*n, "trk_ps", "kt_ready", kw)
                        exps(b, g, 2)
                        exps(b, g, 3)
                        if ahead:
                            q_copies(*m, 0)
                        exp_selected(b, g)
                        if ahead:
                            q_copies(*m, 1)
                        if prep:
                            max_rows(*n)

                nc.scalar.preload_act_table_set("natural_log_exp_and_others")
                act.sem_inc(s["kt_ready"], 1)
                act.sem_inc(s["mrow"], 4)
                act.sem_inc(s["exp_done"], 5)
                act.wait_ge(s["scaled"], 2)
                nc.scalar.copy(wq[:, 0], wraw[:, :, :]).then_inc(s["w_hi"], 1)
                nc.scalar.copy(wn[:, 0], nraw[:, :]).then_inc(s["w_hi"], 1)
                act.wait_ge(s["kw_in"], 16 * 3 * G)
                nc.scalar.copy(wk[:, 0], wkraw[:, :, :]).then_inc(s["w_hi"], 1)
                for t in range(NT):
                    q_copies(0, 0, t)
                k_copies(0, 0)
                transposed(0, 0, "trq_ps", "qt_ready", qt)
                knope_rows(0, 0, range(HG))
                transposed(0, 0, "trk_ps", "kt_ready", kw)
                for t in range(NT):
                    q_copies(0, 1, t)
                max_rows(0, 0)
                loop(act, body)
                reciprocals(B - 1, G - 1)

            @block.vector
            def _(dve):
                def rotate(b, g, t, x, ready, done, added):
                    tile = step(b, g) * NT + t
                    dve.wait_ge(s[ready], tile + 1)
                    dve.wait_ge(s[added], tile + 1)
                    src = pj[:, t, 0:QC].rearrange("p (i c) -> p i c", c=D)[:, :, 0:ROPE]
                    nc.vector.tensor_tensor(rcos[x][:, t], src, cos[:, t].unsqueeze(1).to_broadcast([P, HG, ROPE]), ALU.mult).then_inc(s[done], 1)
                    nc.vector.tensor_tensor(rsin[x][:, t].rearrange("p i (a c) -> p i a c", a=2),
                                            src.rearrange("p i (a c) -> p i a c", a=2)[:, :, ::-1, :],
                                            sin[:, t].unsqueeze(1).to_broadcast([P, HG, 2, HALF]), ALU.mult).then_inc(s[done], 1)

                def rotate_q(b, g):
                    for t in range(NT):
                        rotate(b, g, t, "q", "pq", "rq", "q_add")

                def rotate_k(b, g):
                    for t in range(NT):
                        rotate(b, g, t, "k", "pkw", "rk", "k_add")

                def cast(b, g, ready, ahead, exact, rounded, done):
                    dve.wait_ge(s[ready], step(b, g) + ahead + 1)
                    nc.vector.tensor_copy(rounded[:, :, :], exact[g % 2][0:D]).then_inc(s[done], 1)

                def rough_keys(b, g):
                    st = step(b, g)
                    if g < 2:
                        dve.wait_ge(s["kr_in"], 16 * (b + 1))
                        nc.vector.tensor_copy(k1[g][0:ROPE, :, :], krt[:, :].unsqueeze(1).to_broadcast([ROPE, HG, T])).then_inc(s["kr_copied"], 1)
                        dve.wait_ge(s["kr_copied"], b * 2 + g + 1)
                    dve.wait_ge(s["kn_copied"], st * 4 + 4)
                    nc.vector.tensor_copy(k1b[:, :, :], k1[g % 2][0:D]).then_inc(s["k1b_ready"], 1)
                    dve.wait_ge(ks_in[g % 2], (b * 2 + g // 2 + 1) * 16)
                    nc.vector.tensor_copy(ksb[:, :, :], ks[g % 2][0:D]).then_inc(s["ksb_ready"], 1)

                def maxima(b, g, part):
                    st = step(b, g)
                    done = [0 if part == 0 else 6]

                    def row_max(bank, at, width, t, i, branch):
                        n = done[0]
                        nc.vector.tensor_tensor_reduce(out=junk[:, n, 0:width], in0=bank[:, at:at + width],
                                                       in1=cst("mask")[:, T - width:T], scale=1.0, scalar=-3e38, op0=ALU.add, op1=ALU.max,
                                                       accum_out=mtok[:, t, 32 * i + branch:32 * i + branch + 1]).then_inc(s["max_op"], 1)
                        done[0] += 1

                    def late(u, i, bank):
                        wait_alone(dve, s["mx_ps"], st * 7 + u + 1, s["gate"])
                        row_max(bank, 0, T, 1, i, BR1)
                        row_max(bank, T, T, 1, i, BR3)

                    def early(u, i, bank):
                        wait_alone(dve, s["mx_ps"], st * 7 + u + 1, s["gate"])
                        for j in range(2):
                            row_max(bank, j * T, P, 0, i + j, BR1)
                            row_max(bank, j * T + P, P, 0, i + j, BR3)

                    if part == 0:
                        dve.wait_ge(s["max_op"], st * 17 + 4)
                        late(0, 0, mx[1])
                        early(1, 0, mx[0])
                        return
                    late(2, 1, mx[1])
                    late(3, 2, mx[0])
                    early(4, 2, mx[1])
                    late(5, 3, mx[0])
                    dve.wait_ge(s["mx_ps"], st * 7 + 7)
                    nc.vector.tensor_reduce(mtok[:, :, :].rearrange("p t (i c) -> p t i c", c=32)[:, :, :, BR2],
                                            mx[1][:, 0:NT * HG * KEEP].rearrange("p (t i c) -> p t i c", i=HG, c=KEEP), X, ALU.max).then_inc(s["max_op"], 1)

                def normalise13(b, g):
                    st = step(b, g)
                    if g == 0:
                        nc.vector.tensor_copy(gcur[:, :], gates[:, bass.ds(b, 1), :].rearrange("p b c -> p (b c)")).then_inc(s["g_ready"], 1)
                        dve.wait_ge(s["g_ready"], b + 1)
                    dve.wait_ge(s["n_rec"], st + 1)
                    dve.wait_ge(s["att_ready"], st + 1)
                    nc.vector.scalar_tensor_tensor(o1[:, :], av[:, 0, :], gcur[:, 0:1], rden[:, 0, :], ALU.mult, ALU.mult).then_inc(s["n13"], 1)
                    nc.vector.scalar_tensor_tensor(o3[:, :], av[:, 1, :], gcur[:, 2:3], rden[:, 1, :], ALU.mult, ALU.mult).then_inc(s["n13"], 1)

                def normalise2(b, g):
                    nc.vector.scalar_tensor_tensor(o2[:, :], mx[1][:, 0:T], gcur[:, 1:2], rden[:, 2, :], ALU.mult, ALU.mult).then_inc(s["n2"], 1)

                def finish(b, first_out):
                    dve.wait_ge(s["op_ps"], b + 1)
                    dve.wait_ge(s["res_in"], 16 * (b + 1))
                    if not first_out:
                        dve.wait_ge(s["out_done"], 16 * b)
                    nc.vector.tensor_tensor(ot[:, :, :], mx[1][:, 0:NT * C].rearrange("p (t c) -> p t c", c=C), res[:, :, :], ALU.add).then_inc(s["out_ready"], 1)

                def body(b, first, last):
                    for g in range(G):
                        n, m = nxt(b, g), nxt(b, g, 2)
                        before = (b, g - 1) if g else (b - 1, G - 1)
                        prep, ahead = stages(last, g)
                        if prep:
                            rotate_k(*n)
                        if not (first and g == 0):
                            normalise13(*before)
                            normalise2(*before)
                        if prep:
                            cast(*n, "qt_ready", 0, qt, qb, "qb_ready")
                            rough_keys(*n)
                            cast(*n, "kt_ready", 1, kw, kwb, "kwb_ready")
                        if g == 0 and not first:
                            finish_at(b)
                        if prep:
                            maxima(*n, 0)
                        if ahead:
                            rotate_q(*m)
                        if prep:
                            maxima(*n, 1)

                def finish_at(b):
                    finish(b - 1, isinstance(b, int) and b == 1)

                dve.sem_inc(s["max_op"], 4)
                dve.sem_inc(s["n13"], 2)
                nc.vector.memset(wraw[:, :, :], 0.0).then_inc(s["raw_zero"], 1)
                nc.vector.memset(nraw[:, :], 0.0).then_inc(s["raw_zero"], 1)
                nc.vector.memset(mtok[:, :, :], 0.0).then_inc(s["mtok_zero"], 1)
                nc.vector.memset(nk[:, :, :].bitcast(F32), 0.0).then_inc(s["rows_set"], 1)
                for i in range(2):
                    for j, k in enumerate((k1, kw)):
                        nc.vector.tensor_copy(k[i][D:P].rearrange("p i c -> p (i c)"),
                                              cst("mrow")[D:P, j:j + 1].to_broadcast([P - D, HT])).then_inc(s["rows_set"], 1)
                dve.wait_ge(s["mtok_zero"], 1)
                dve.wait_ge(s["rows_set"], 5)
                dve.wait_ge(s["g_in"], 32)
                dve.wait_ge(s["raw_zero"], 2)
                dve.wait_ge(s["w_in"], 16 * 3 * G)
                nc.vector.tensor_scalar(wraw[:, :, :], wraw[:, :, :], gain[:, 0:1], None, ALU.mult).then_inc(s["scaled"], 1)
                dve.wait_ge(s["n_in"], 16)
                nc.vector.tensor_scalar(nraw[:, :], nraw[:, :], gain[:, 0:1], None, ALU.mult).then_inc(s["scaled"], 1)
                dve.wait_ge(s["scaled"], 2)
                dve.wait_ge(s["w_hi"], 1)
                nc.vector.tensor_tensor(wq[:, 1], wraw[:, :, :], wq[:, 0].bitcast(F32), ALU.subtract).then_inc(s["w_lo"], 1)
                dve.wait_ge(s["w_hi"], 2)
                nc.vector.tensor_tensor(wn[:, 1], nraw[:, :], wn[:, 0].bitcast(F32), ALU.subtract).then_inc(s["w_lo"], 1)
                dve.wait_ge(s["w_hi"], 3)
                nc.vector.tensor_tensor(wk[:, 1], wkraw[:, :, :], wk[:, 0].bitcast(F32), ALU.subtract).then_inc(s["w_lo"], 1)
                rotate_q(0, 0)
                rotate_k(0, 0)
                cast(0, 0, "qt_ready", 0, qt, qb, "qb_ready")
                rough_keys(0, 0)
                cast(0, 0, "kt_ready", 1, kw, kwb, "kwb_ready")
                rotate_q(0, 1)
                maxima(0, 0, 0)
                maxima(0, 0, 1)
                loop(dve, body)
                normalise13(B - 1, G - 1)
                normalise2(B - 1, G - 1)
                finish(B - 1, False)

            @block.gpsimd
            def _(pool):
                def add(b, g, x, parts, done):
                    for t in range(NT):
                        pool.wait_ge(s[parts], (step(b, g) * NT + t + 1) * 2)
                        nc.gpsimd.tensor_tensor(tok[x][:, t, :, 0:ROPE], rcos[x][:, t], rsin[x][:, t], ALU.add).then_inc(s[done], 1)

                def mask(b, g, i):
                    wait_alone(pool, s["exp_done"], step(b, g) * 5 + 5 + i + 1, s["pgate"])
                    blocks = prob[g % 2][:, i, :, :]
                    at = [blocks[:, :, 0:P], blocks[:, :, T:TQ]]
                    for j in range(2):
                        ins = nc.gpsimd.affine_select(out=at[j], in_=at[j], compare_op=ALU.is_ge, fill=0.0, base=0,
                                                      pattern=[[0, 2], [1, P]], channel_multiplier=-1)
                    ins.then_inc(s["masked"], 1)

                def blocks(b, g):
                    pool.wait_ge(vc_in[g % 2], (b * 2 + g // 2 + 1) * 64)
                    nc.gpsimd.tensor_tensor(vbd[g % 2][:, :, :], vc[g % 2][:, :].unsqueeze(1).to_broadcast([P, HG, VH]),
                                            cst("block").rearrange("p (i c) -> p i c", c=VH), ALU.mult).then_inc(s["vbd_ready"], 1)

                def branches(b, g):
                    st = step(b, g)
                    pool.wait_ge(s["n13"], st * 2 + 4)
                    nc.gpsimd.tensor_tensor(o13[:, :], o1[:, :], o3[:, :], ALU.add).then_inc(s["att13"], 1)
                    pool.wait_ge(s["att13"], st + 1)
                    pool.wait_ge(s["n2"], st + 1)
                    if g == 0 and not (isinstance(b, int) and b == 0):
                        pool.wait_ge(s["op_ps"], b)
                    nc.gpsimd.tensor_tensor(att[:, g, :], o13[:, :], o2[:, :], ALU.add).then_inc(s["att_ready"], 1)

                def body(b, first, last):
                    for g in range(G):
                        n, m = nxt(b, g), nxt(b, g, 2)
                        before = (b, g - 1) if g else (b - 1, G - 1)
                        prep, ahead = stages(last, g)
                        if prep:
                            add(*n, "k", "rk", "k_add")
                        mask(b, g, 0)
                        if not (first and g == 0):
                            branches(*before)
                        mask(b, g, 1)
                        mask(b, g, 2)
                        blocks(b, g)
                        mask(b, g, 3)
                        if ahead:
                            add(*m, "q", "rq", "q_add")

                pool.sem_inc(s["q_add"], NT)
                pool.sem_inc(s["k_add"], NT)
                pool.sem_inc(s["att_ready"], 1)
                add(0, 0, "q", "rq", "q_add")
                add(0, 0, "k", "rk", "k_add")
                add(0, 1, "q", "rq", "q_add")
                loop(pool, body)
                branches(B - 1, G - 1)


_INS = ["L0_attn_x", "L0_attn_w_cq", "L0_attn_g_qnorm", "L0_attn_w_dq_nope", "L0_attn_w_dq_rope", "L0_attn_w_ckv", "L0_attn_g_kvnorm",
        "L0_attn_w_dk_nope", "L0_attn_w_dv", "L0_attn_w_krope", "L0_attn_w_imp", "L0_attn_w_selk", "L0_attn_w_selv", "L0_attn_w_wink",
        "L0_attn_w_winv", "L0_attn_w_gate", "L0_attn_w_proj", "L0_ffn_w_router", "L0_ffn_w1", "L0_ffn_w3", "L0_ffn_w2", "L0_ffn_sw1",
        "L0_ffn_sw3", "L0_ffn_sw2"]


def kernel(**inputs):
    import numpy as _np
    import concourse.bacc as _bacc
    from concourse import mybir as _mybir
    from concourse.bass_utils import run_bass_kernel_spmd as _run

    nc = _bacc.Bacc("TRN2", target_bir_lowering=False, num_devices=1)
    arrays, args = {}, {}
    for name in _INS:
        x = _np.ascontiguousarray(inputs[name])
        arrays[f"in_{name}"] = x
        args[name] = nc.dram_tensor(f"in_{name}", x.shape, _mybir.dt.from_np(x.dtype), kind="ExternalInput").ap()
    arrays["in_constants"] = constants(_np)
    args["constants"] = nc.dram_tensor("in_constants", (P, NCONST), F32, kind="ExternalInput").ap()
    out = nc.dram_tensor("out_0", (B, T, C), F32, kind="ExternalOutput").ap()
    layer_kernel(nc, args, out)
    r = _run(nc, [arrays], core_ids=[0])
    return r.results[0]["out_0"]
```

```python
from contextlib import ExitStack

import concourse.bass as bass
from concourse import mybir

F32 = mybir.dt.float32
F32R = mybir.dt.float32r
BF16 = mybir.dt.bfloat16
ALU = mybir.AluOpType
ACT = mybir.ActivationFunctionType
X = mybir.AxisListType.X

B, T, C = 16, 256, 128
P = 128
NT = T // P
H, HG = 16, 4
G = H // HG
NOPE, ROPE, VH = 32, 64, 32
HALF = ROPE // 2
D = NOPE + ROPE
QL, KL = 96, 32
KEEP = 32
QC = HG * D
GC = QC + HG * VH
QR = HG * ROPE
RC = QR + HG * VH
E1 = 9
NE = E1 - 1
HID = 256
HC = HID // P
BT = 4
NBLK = B * T // (BT * P)
BTOK = BT * P
SPB = BTOK // T
A_CKV, A_KR, A_IMP, A_GATE, A_ROUT = QL, QL + KL, QL + KL + ROPE, QL + KL + ROPE + 1, QL + KL + ROPE + 4
A_N = A_ROUT + NE
EPS_LN, EPS_RMS = 1e-5, 1e-6
SCALE = float(D) ** -0.5
NEG = -1e30
BR1, BR3, BR2 = 0, 1, 2

CONST_COLS = {}


def _layout():
    at = 0
    for name, n in [("ident", P), ("cos", NT * ROPE), ("sin", NT * ROPE), ("scos", ROPE), ("ssin", ROPE),
                    ("mask", T), ("mrow", 3), ("iota", KEEP), ("tri", NE * NE), ("block", P),
                    ("mean", P), ("ones", VH), ("eps", 2)]:
        CONST_COLS[name] = (at, n)
        at += n
    return at


NCONST = _layout()


def constants(np):
    c = np.zeros((P, NCONST), np.float32)

    def put(name, a):
        at, n = CONST_COLS[name]
        c[:, at:at + n] = np.asarray(a, np.float32).reshape(P, n)

    inv = (np.float32(1.0) / np.float32(10000.0) ** (np.arange(0, ROPE, 2, dtype=np.float32) / np.float32(ROPE))).astype(np.float32)
    ang = np.outer(np.arange(T, dtype=np.float32), inv).astype(np.float32)
    cos, sin = np.cos(ang), np.sin(ang)
    two_c, two_s = np.concatenate([cos, cos], 1), np.concatenate([-sin, sin], 1)
    p = np.arange(P)
    put("ident", np.eye(P))
    put("cos", two_c.reshape(NT, P, ROPE).transpose(1, 0, 2))
    put("sin", two_s.reshape(NT, P, ROPE).transpose(1, 0, 2))
    put("scos", two_c[p % KEEP])
    put("ssin", two_s[p % KEEP])
    put("mask", np.where(np.arange(T)[None, :] <= p[:, None] + T - P, 0.0, NEG))
    put("mrow", np.where(p[:, None] == D + np.arange(3)[None, :], -1.0, 0.0))
    put("iota", np.broadcast_to(np.arange(1, KEEP + 1), (P, KEEP)))
    e = np.arange(NE)
    put("tri", np.broadcast_to((e[None, :] < e[:, None]).reshape(1, -1), (P, NE * NE)))
    put("block", (p[:, None] // KEEP == p[None, :] // VH))
    put("mean", np.full((P, P), 1.0 / T))
    put("ones", np.ones((P, VH)))
    put("eps", np.broadcast_to([EPS_LN, EPS_RMS], (P, 2)))
    return c


def wait_alone(eng, semaphore, value, passed):
    eng.wait_ge(semaphore, value)
    eng.sem_inc(passed, 1)


def layer_kernel(nc, a, out):
    ctx = ExitStack()
    with ctx:
        def sem(name):
            return ctx.enter_context(nc.semaphore(name))

        def keep(name, shape, dt=F32):
            return ctx.enter_context(nc.sbuf_tensor(name, shape, dt))

        dram = lambda name, shape: nc.dram_tensor(name, shape, F32, kind="Internal").ap()
        xt_d = dram("xt_d", (B, C, 2, T))
        nt_d = dram("nt_d", (B, P, 2, T))
        kr_d = dram("kr_d", (B, ROPE, T))
        res_d = dram("res_d", (B * T, C))
        ks_d = dram("ks_d", (B, D, H * KEEP))
        vs_d = dram("vs_d", (B, KEEP, H * VH))

        const = keep("const", [P, NCONST])
        misc = keep("misc", [P, B * NT, 4])
        gates = keep("gates", [P, B, 3])
        xsel = keep("xsel", [P, B * KEEP])
        w = {"q": keep("wq", [P, 2, G, RC], F32R),
             "k": keep("wk", [P, 2, G, RC], F32R),
             "n": keep("wn", [P, 2, 3, H * NOPE], F32R),
             "sel": keep("wsel", [P, G, GC]),
             "proj": keep("wp", [P, G, C])}

        def cst(name):
            at, n = CONST_COLS[name]
            return const[:, at:at + n]

        const_in = sem("const_in")
        mixture(nc, a, sem, cst, const, const_in, misc, gates, xsel, w, xt_d, nt_d, kr_d, res_d)
        attend(nc, a, sem, cst, gates, xsel, w, xt_d, nt_d, kr_d, res_d, ks_d, vs_d, out)


def mixture(nc, a, sem, cst, const, const_in, misc, gates, xsel, w, xt_d, nt_d, kr_d, res_d):
    ctx = ExitStack()
    with ctx:
        def sb(name, shape, dt=F32):
            return ctx.enter_context(nc.sbuf_tensor(name, shape, dt))

        def ps(name, shape, dt=F32):
            return ctx.enter_context(nc.psum_tensor(name, shape, dt))

        w13_raw = sb("w13_raw", [P, E1, 2, HID])
        w13 = sb("w13", [P, 2, E1, 2, HID], F32R)
        w2 = sb("w2", [P, E1, HC, C])
        wa = sb("wa", [P, A_N])
        xb = sb("xb", [P, 2, BT, C])
        stats = sb("stats", [P, BT, 6])
        mv = sb("mv", [P, 2, BT, 2])
        lnv = sb("lnv", [P, BT])
        rstd = sb("rstd", [P, 2, BT])
        xn = sb("xn", [P, BT, C])
        xt = sb("xt", [P, BTOK])
        xhl = [sb(f"xhl{i}", [P, 2, BTOK], F32R) for i in range(2)]
        sqj = sb("sqj", [P, BT, P])
        ssq = sb("ssq", [P, 2, BT])
        lns = sb("lns", [P, 2, BT])
        rr = sb("rr", [P, 2, BT])
        nqc = sb("nqc", [P, BT, P])
        nhl = [sb(f"nhl{i}", [P, 2, BTOK], F32R) for i in range(2)]
        kcos = sb("kcos", [P, BT, ROPE])
        ksin = sb("ksin", [P, BT, ROPE])
        kr = sb("kr", [P, BT, ROPE])
        krt = [sb(f"krt{i}", [ROPE, BTOK]) for i in range(2)]
        rmx = sb("rmx", [P, BT])
        rd = sb("rd", [P, BT, NE])
        rex = sb("rex", [P, BT, NE])
        rsum = sb("rsum", [P, BT])
        rrec = sb("rrec", [P, BT])
        rp = sb("rp", [P, BT, NE])
        rgt = sb("rgt", [P, BT, NE, NE])
        req = sb("req", [P, BT, NE, NE])
        rank = sb("rank", [P, BT, NE])
        rsel = sb("rsel", [P, BT, NE])
        rs2 = sb("rs2", [P, BT])
        rr2 = sb("rr2", [P, BT])
        cw = [sb(f"cw{i}", [P, BT, NE]) for i in range(2)]
        silu = sb("silu", [P, HC, BTOK])
        hid = sb("hid", [P, 2, HC, BTOK])
        acc = sb("acc", [P, 2, BT, C])
        xn_all = sb("xn_all", [P, B * NT, C])
        score = [sb(f"score{i}", [B, T]) for i in range(3)]
        best = sb("best", [B, KEEP // 8, 8])
        chosen = sb("chosen", [B, T])
        ones = sb("ones_row", [B, T])
        place = sb("place", [B, T])
        place_t = sb("place_t", [P, B, NT])
        onehot = sb("onehot", [P, B * NT, KEEP])
        xs_tok = sb("xs_tok", [P, B * KEEP])
        glog = sb("glog", [P, B, 3])
        gmx = sb("gmx", [P, B])
        gd = sb("gd", [P, B, 3])
        gex = sb("gex", [P, B, 3])
        gsum = sb("gsum", [P, B])
        grec = sb("grec", [P, B])
        gain = sb("gain", [P, 1])
        raw = w13_raw[:, :, :, :].rearrange("p e j h -> p (e j h)")
        wraw = raw[:, 0:G * RC].rearrange("p (g c) -> p g c", c=RC)
        nraw = raw[:, G * RC:G * RC + 3 * H * NOPE].rearrange("p (j c) -> p j c", j=3)
        wkraw = raw[:, G * RC + 3 * H * NOPE:2 * G * RC + 3 * H * NOPE].rearrange("p (g c) -> p g c", c=RC)
        gained = raw[:, 0:G * RC + 2 * H * NOPE]

        pf = ps("pf", [P, 2, 512])
        ph = ps("ph", [P, 2 * HC, 512])
        py = ps("py", [P, 2, 512])
        pa = pf[:, :, :].rearrange("p b (t c) -> p (b t) c", c=256)

        names = ("w2_in wa_in w_hi w_lo wa_scaled bn var ln_log ln_rstd xn_ready xn_kept "
                 "xT_ps xt_ready xh_ready xl_ready a_ps sq rms_log misc_ready rr_ready nq_ready kr_part kr_ready "
                 "rmax rdiff rexp rchain cw_ready nT_ps krT_ps nh_ready nl_ready krt_ready "
                 "h_ps silu_ready hid_ready y_ps acc_ready gate "
                 "raw_zero aw_in ow_in aw_scaled aw_hi aw_lo row_ps round ones_set place_done place_ps place_t_done onehot_done "
                 "sel_ps xs_ready selT_ps xsel_ready gdiff gexp gchain").split()
        s = {n: sem("m_" + n) for n in names}
        w_in = [sem(f"m_w_in{i}") for i in range(3)]
        x_in = [sem(f"m_x_in{i}") for i in range(2)]
        xt_out = [sem(f"m_xt_out{i}") for i in range(2)]
        nt_out = [sem(f"m_nt_out{i}") for i in range(2)]
        kr_out = [sem(f"m_kr_out{i}") for i in range(2)]
        acc_out = [sem(f"m_acc_out{i}") for i in range(2)]

        x_v = a["L0_attn_x"].rearrange("b (t p) c -> p (b t) c", p=P)
        res_v = res_d.rearrange("(n p) c -> p n c", p=P)
        ident = cst("ident")

        with nc.Block() as block:
            @block.sync
            def _(sp):
                for n in range(2):
                    sp.sem_inc(xt_out[n], 16 * SPB)
                    sp.sem_inc(nt_out[n], 16 * SPB)
                    sp.sem_inc(kr_out[n], 16 * SPB)
                    sp.sem_inc(acc_out[n], 16)
                sp.dma_start(const[:, :], a["constants"]).then_inc(const_in, 16)
                for n in range(2):
                    sp.dma_start(xb[:, n], x_v[:, n * BT:(n + 1) * BT, :]).then_inc(x_in[n], 16)
                for at, name, n in [(0, "L0_attn_w_cq", QL), (A_CKV, "L0_attn_w_ckv", KL), (A_KR, "L0_attn_w_krope", ROPE),
                                    (A_IMP, "L0_attn_w_imp", 1), (A_GATE, "L0_attn_w_gate", 3), (A_ROUT, "L0_ffn_w_router", NE)]:
                    sp.dma_start(wa[:, at:at + n], a[name]).then_inc(s["wa_in"], 16)
                third = E1 // 3
                for n in range(3):
                    for j, (experts, shared) in enumerate([("L0_ffn_w1", "L0_ffn_sw1"), ("L0_ffn_w3", "L0_ffn_sw3")]):
                        many = slice(n * third, min((n + 1) * third, NE))
                        sp.dma_start(w13_raw[:, many, j, :], a[experts][many].rearrange("e p h -> p e h")).then_inc(w_in[n], 16)
                        if n == 2:
                            sp.dma_start(w13_raw[:, NE, j, :], a[shared]).then_inc(w_in[n], 16)
                    if n == 0:
                        sp.dma_start(w2[:, 0:NE], a["L0_ffn_w2"].rearrange("e (c p) d -> p e c d", p=P)).then_inc(s["w2_in"], 16)
                        sp.dma_start(w2[:, NE], a["L0_ffn_sw2"].rearrange("(c p) d -> p c d", p=P)).then_inc(s["w2_in"], 16)

                def store(f, par):
                    sp.wait_ge(s["xl_ready"], f + 1)
                    for q in range(SPB):
                        sp.dma_start(xt_d[f * SPB + q], xhl[par][:, :, q * T:(q + 1) * T].bitcast(F32)).then_inc(xt_out[par], 16)
                    sp.wait_ge(s["nl_ready"], f + 2)
                    for q in range(SPB):
                        sp.dma_start(nt_d[f * SPB + q], nhl[par][:, :, q * T:(q + 1) * T].bitcast(F32)).then_inc(nt_out[par], 16)
                    sp.wait_ge(s["krt_ready"], f + 2)
                    for q in range(SPB):
                        sp.dma_start(kr_d[f * SPB + q], krt[par][:, q * T:(q + 1) * T]).then_inc(kr_out[par], 16)

                def body(j, last):
                    for par in range(2):
                        k = j * 2 + par
                        if not last:
                            sp.wait_ge(s["acc_ready"], k * E1 + 3)
                            sp.dma_start(xb[:, par], x_v[:, bass.ds((k + 2) * BT, BT), :]).then_inc(x_in[par], 16)
                        if not (last and par):
                            store(k + 1, 1 - par)
                        sp.wait_ge(s["acc_ready"], k * E1 + E1 + 2)
                        sp.dma_start(res_v[:, bass.ds(k * BT, BT), :], acc[:, par]).then_inc(acc_out[par], 16)

                store(0, 0)
                sp.wait_ge(s["raw_zero"], 1)
                group = lambda name, c: a[name].rearrange("p (g c) -> p g c", c=c)
                sp.dma_start(wraw[0:QL, :, 0:QR], group("L0_attn_w_dq_rope", QR)).then_inc(s["aw_in"], 16)
                sp.dma_start(wraw[QL:P, :, QR:RC], group("L0_attn_w_dv", HG * VH)).then_inc(s["aw_in"], 16)
                sp.dma_start(nraw[0:QL, 0], a["L0_attn_w_dq_nope"]).then_inc(s["aw_in"], 16)
                sp.dma_start(nraw[QL:P, 1], a["L0_attn_w_dk_nope"]).then_inc(s["aw_in"], 16)
                wink = a["L0_attn_w_wink"].rearrange("p (h c) -> p h c", c=D)
                sp.dma_start(nraw[:, 2].rearrange("p (h c) -> p h c", c=NOPE), wink[:, :, 0:NOPE]).then_inc(s["aw_in"], 16)
                for g in range(G):
                    sp.dma_start(wkraw[:, g, 0:QR].rearrange("p (h c) -> p h c", c=ROPE), wink[:, g * HG:(g + 1) * HG, NOPE:D]).then_inc(s["aw_in"], 16)
                sp.dma_start(wkraw[:, :, QR:RC], group("L0_attn_w_winv", HG * VH)).then_inc(s["aw_in"], 16)
                load_grouped(sp, w["sel"], slice(0, P),
                             [(0, ROPE, a["L0_attn_w_selk"], NOPE, D), (ROPE, NOPE, a["L0_attn_w_selk"], 0, D)], s["ow_in"])
                sp.dma_start(w["sel"][:, :, QC:GC], group("L0_attn_w_selv", HG * VH)).then_inc(s["ow_in"], 16)
                sp.dma_start(gain[0:QL, :], a["L0_attn_g_qnorm"].rearrange("(p c) -> p c", c=1)).then_inc(s["aw_in"], 16)
                sp.dma_start(gain[QL:P, :], a["L0_attn_g_kvnorm"].rearrange("(p c) -> p c", c=1)).then_inc(s["aw_in"], 16)
                sp.dma_start(w["proj"][:, :, :], a["L0_attn_w_proj"].rearrange("(g p) c -> p g c", p=P)).then_inc(s["ow_in"], 16)
                with sp.Fori(0, NBLK // 2 - 1) as j:
                    body(j, False)
                body(NBLK // 2 - 1, True)
                sp.wait_ge(s["ow_in"], 16 * (2 * G + 2))
                for n in range(2):
                    sp.wait_ge(xt_out[n], 16 * SPB * (NBLK // 2 + 1))
                    sp.wait_ge(nt_out[n], 16 * SPB * (NBLK // 2 + 1))
                    sp.wait_ge(kr_out[n], 16 * SPB * (NBLK // 2 + 1))
                    sp.wait_ge(acc_out[n], 16 * (NBLK // 2 + 1))

            @block.gpsimd
            def _(pool):
                for e in range(E1):
                    pool.wait_ge(s["w_hi"], e + 1)
                    nc.gpsimd.tensor_tensor(w13[:, 1, e], w13_raw[:, e], w13[:, 0, e].bitcast(F32), ALU.subtract).then_inc(s["w_lo"], 1)
                pool.wait_ge(s["w_lo"], E1)
                nc.gpsimd.memset(raw, 0.0).then_inc(s["raw_zero"], 1)
                pool.wait_ge(s["raw_zero"], 1)
                pool.wait_ge(s["aw_in"], 16 * (G + 8))
                nc.gpsimd.tensor_tensor(gained, gained, gain[:, 0:1].to_broadcast(list(gained.shape)), ALU.mult).then_inc(s["aw_scaled"], 1)
                pool.wait_ge(s["aw_scaled"], 1)
                for g in range(G):
                    pool.wait_ge(s["aw_hi"], 2 * g + 2)
                    nc.gpsimd.tensor_tensor(w["q"][:, 1, g], wraw[:, g], w["q"][:, 0, g].bitcast(F32), ALU.subtract).then_inc(s["aw_lo"], 1)
                    nc.gpsimd.tensor_tensor(w["k"][:, 1, g], wkraw[:, g], w["k"][:, 0, g].bitcast(F32), ALU.subtract).then_inc(s["aw_lo"], 1)
                pool.wait_ge(s["aw_hi"], 2 * G + 1)
                nc.gpsimd.tensor_tensor(w["n"][:, 1], nraw, w["n"][:, 0].bitcast(F32), ALU.subtract).then_inc(s["aw_lo"], 1)

            @block.scalar
            def _(act):
                nc.scalar.preload_act_table_set("natural_log_exp_and_others")
                act.wait_ge(s["wa_in"], 16 * 6)
                nc.scalar.mul(wa[:, A_KR:A_KR + ROPE], wa[:, A_KR:A_KR + ROPE], 1.0 / H).then_inc(s["wa_scaled"], 1)

                def norm_rstd(f, par):
                    act.wait_ge(const_in, 16)
                    act.wait_ge(s["var"], f * BT + BT)
                    nc.scalar.activation(lnv[:, :], mv[:, par, :, 1], ACT.Ln, bias=cst("eps")[:, 0:1]).then_inc(s["ln_log"], 1)
                    act.wait_ge(s["ln_log"], f + 1)
                    nc.scalar.activation(rstd[:, par, :], lnv[:, :], ACT.Exp, scale=-0.5).then_inc(s["ln_rstd"], 1)

                def keep_xn(f):
                    act.wait_ge(s["xn_ready"], f * BT + BT)
                    nc.scalar.copy(xn_all[:, bass.ds(f * BT, BT), :], xn[:, :, :]).then_inc(s["xn_kept"], 1)

                def split_x(f, par, uses):
                    act.wait_ge(s["xT_ps"], f + 1)
                    nc.scalar.copy(xt[:, :], pf[:, 1, :]).then_inc(s["xt_ready"], 1)
                    act.wait_ge(xt_out[par], 16 * SPB * (uses + 1))
                    nc.scalar.copy(xhl[par][:, 0, :], pf[:, 1, :]).then_inc(s["xh_ready"], 1)

                def small(f):
                    act.wait_ge(s["a_ps"], f + 1)
                    for t in range(BT):
                        nc.scalar.activation(sqj[:, t, 0:QL], pa[:, t, 0:QL], ACT.Square, accum_out=ssq[:, 0, t:t + 1]).then_inc(s["sq"], 1)
                        nc.scalar.activation(sqj[:, t, QL:P], pa[:, t, A_CKV:A_CKV + KL], ACT.Square, accum_out=ssq[:, 1, t:t + 1]).then_inc(s["sq"], 1)
                    nc.scalar.copy(misc[:, bass.ds(f * BT, BT), :], pa[:, :, A_IMP:A_IMP + 4]).then_inc(s["misc_ready"], 1)

                def small_exps(f):
                    act.wait_ge(s["sq"], f * 2 * BT + 2 * BT)
                    nc.scalar.activation(lns[:, 0, :], ssq[:, 0, :], ACT.Ln, bias=cst("eps")[:, 1:2], scale=1.0 / QL).then_inc(s["rms_log"], 1)
                    nc.scalar.activation(lns[:, 1, :], ssq[:, 1, :], ACT.Ln, bias=cst("eps")[:, 1:2], scale=1.0 / KL).then_inc(s["rms_log"], 1)
                    act.wait_ge(s["rms_log"], f * 2 + 2)
                    nc.scalar.activation(rr[:, :, :], lns[:, :, :], ACT.Exp, scale=-0.5).then_inc(s["rr_ready"], 1)
                    act.wait_ge(s["rdiff"], f + 1)
                    nc.scalar.activation(rex[:, :, :], rd[:, :, :], ACT.Exp).then_inc(s["rexp"], 1)

                def split_n(f, par, uses):
                    act.wait_ge(s["nT_ps"], f + 1)
                    act.wait_ge(nt_out[par], 16 * SPB * (uses + 1))
                    nc.scalar.copy(nhl[par][:, 0, :], pf[:, 0, :]).then_inc(s["nh_ready"], 1)
                    act.wait_ge(s["krT_ps"], f + 1)
                    act.wait_ge(kr_out[par], 16 * SPB * (uses + 1))
                    nc.scalar.copy(krt[par][:, :], pf[0:ROPE, 1, :]).then_inc(s["krt_ready"], 1)

                def silus(k, e):
                    for c in range(HC):
                        n = k * (E1 * HC) + e * HC + c
                        act.wait_ge(s["h_ps"], n + 1)
                        act.wait_ge(s["hid_ready"], n + 1)
                        nc.scalar.activation(silu[:, c, :], ph[:, 2 * c, :], ACT.Silu).then_inc(s["silu_ready"], 1)

                def body(j, last):
                    for par in range(2):
                        k = j * 2 + par
                        front = not (last and par)
                        f, fp, uses = k + 1, 1 - par, j + par
                        for e in range(E1):
                            silus(k, e)
                            if not front:
                                if e == 0:
                                    act.wait_ge(s["aw_scaled"], 1)
                                if e < G:
                                    nc.scalar.copy(w["q"][:, 0, e], wraw[:, e]).then_inc(s["aw_hi"], 1)
                                    nc.scalar.copy(w["k"][:, 0, e], wkraw[:, e]).then_inc(s["aw_hi"], 1)
                                if e == G:
                                    nc.scalar.copy(w["n"][:, 0], nraw).then_inc(s["aw_hi"], 1)
                                continue
                            if e == 1:
                                keep_xn(f)
                            if e == 2:
                                split_x(f, fp, uses)
                            if e == 4:
                                small(f)
                            if e == 5:
                                nc.scalar.preload_act_table_set("natural_log_exp_and_others")
                                small_exps(f)
                                if not last:
                                    norm_rstd(f + 1, par)
                            if e == 8:
                                split_n(f, fp, uses)

                act.sem_inc(s["krt_ready"], 1)
                norm_rstd(0, 0)
                keep_xn(0)
                split_x(0, 0, 0)
                for e in range(E1):
                    if e % 3 == 0:
                        act.wait_ge(w_in[e // 3], 64 if e // 3 == 2 else 32)
                    if e == 3:
                        small(0)
                        small_exps(0)
                        norm_rstd(1, 1)
                    if e == 6:
                        split_n(0, 0, 0)
                    nc.scalar.copy(w13[:, 0, e], w13_raw[:, e]).then_inc(s["w_hi"], 1)
                with act.Fori(0, NBLK // 2 - 1) as j:
                    body(j, False)
                body(NBLK // 2 - 1, True)
                nc.scalar.preload_act_table_set("natural_log_exp_and_others")
                act.wait_ge(s["gdiff"], 1)
                nc.scalar.activation(gex[:, :, :], gd[:, :, :], ACT.Exp).then_inc(s["gexp"], 1)
                act.wait_ge(s["selT_ps"], 1)
                nc.scalar.copy(xsel[:, :], pf[:, 1, :]).then_inc(s["xsel_ready"], 1)

            @block.vector
            def _(dve):
                def norm_stats(f, par, uses):
                    dve.wait_ge(x_in[par], 16 * (uses + 1))
                    for t in range(BT):
                        nc.vector.bn_stats(stats[:, t, :], xb[:, par, t, :]).then_inc(s["bn"], 1)
                    wait_alone(dve, s["bn"], f * BT + BT, s["gate"])
                    for t in range(BT):
                        nc.vector.bn_aggr(mv[:, par, t, :], stats[:, t, :]).then_inc(s["var"], 1)

                def norm_apply(f, par):
                    dve.wait_ge(s["ln_rstd"], f + 1)
                    for t in range(BT):
                        nc.vector.tensor_scalar(xn[:, t, :], xb[:, par, t, :], mv[:, par, t, 0:1], rstd[:, par, t:t + 1],
                                                ALU.subtract, ALU.mult).then_inc(s["xn_ready"], 1)

                def x_lo(f, par):
                    dve.wait_ge(s["xh_ready"], f + 1)
                    nc.vector.tensor_tensor(xhl[par][:, 1, :], pf[:, 1, :], xhl[par][:, 0, :].bitcast(F32), ALU.subtract).then_inc(s["xl_ready"], 1)

                def chain(f, n, ins):
                    ins.then_inc(s["rchain"], 1)
                    dve.wait_ge(s["rchain"], f * 9 + n)

                def small_parts(f):
                    dve.wait_ge(s["misc_ready"], f + 1)
                    nc.vector.tensor_reduce(rmx[:, :], pa[:, :, A_ROUT:A_N], X, ALU.max).then_inc(s["rmax"], 1)
                    dve.wait_ge(s["rmax"], f + 1)
                    nc.vector.tensor_tensor(rd[:, :, :], pa[:, :, A_ROUT:A_N], rmx[:, :].unsqueeze(2).to_broadcast([P, BT, NE]),
                                            ALU.subtract).then_inc(s["rdiff"], 1)
                    for q in range(SPB):
                        t = slice(q * NT, (q + 1) * NT)
                        src = pa[:, t, A_KR:A_KR + ROPE]
                        nc.vector.tensor_tensor(kcos[:, t, :], src, cst("cos").rearrange("p (t c) -> p t c", c=ROPE), ALU.mult).then_inc(s["kr_part"], 1)
                        nc.vector.tensor_tensor(ksin[:, t, :].rearrange("p t (a c) -> p t a c", a=2),
                                                src.rearrange("p t (a c) -> p t a c", a=2)[:, :, ::-1, :],
                                                cst("sin").rearrange("p (t a c) -> p t a c", a=2, c=HALF), ALU.mult).then_inc(s["kr_part"], 1)

                def small_norms(f):
                    dve.wait_ge(s["rr_ready"], f + 1)
                    nc.vector.tensor_tensor(nqc[:, :, 0:QL], pa[:, :, 0:QL], rr[:, 0, :].unsqueeze(2).to_broadcast([P, BT, QL]),
                                            ALU.mult).then_inc(s["nq_ready"], 1)
                    nc.vector.tensor_tensor(nqc[:, :, QL:P], pa[:, :, A_CKV:A_CKV + KL], rr[:, 1, :].unsqueeze(2).to_broadcast([P, BT, KL]),
                                            ALU.mult).then_inc(s["nq_ready"], 1)
                    dve.wait_ge(s["kr_part"], f * (2 * SPB) + 2 * SPB)
                    nc.vector.tensor_tensor(kr[:, :, :], kcos[:, :, :], ksin[:, :, :], ALU.add).then_inc(s["kr_ready"], 1)

                def router(f):
                    dve.wait_ge(s["rexp"], f + 1)
                    chain(f, 1, nc.vector.tensor_reduce(rsum[:, :], rex[:, :, :], X, ALU.add))
                    chain(f, 2, nc.vector.reciprocal(rrec[:, :], rsum[:, :]))
                    chain(f, 3, nc.vector.tensor_tensor(rp[:, :, :], rex[:, :, :], rrec[:, :].unsqueeze(2).to_broadcast([P, BT, NE]), ALU.mult))
                    other = rp[:, :, :].unsqueeze(2).to_broadcast([P, BT, NE, NE])
                    own = rp[:, :, :].unsqueeze(3).to_broadcast([P, BT, NE, NE])
                    chain(f, 4, nc.vector.tensor_tensor(req[:, :, :, :], other, own, ALU.is_equal))
                    tri = cst("tri").unsqueeze(1).to_broadcast([P, BT, NE * NE])
                    chain(f, 5, nc.vector.tensor_tensor(rgt[:, :, :, :].rearrange("p t e f -> p t (e f)"),
                                                        req[:, :, :, :].rearrange("p t e f -> p t (e f)"), tri, ALU.mult))

                def router_weights(f, par):
                    other = rp[:, :, :].unsqueeze(2).to_broadcast([P, BT, NE, NE])
                    own = rp[:, :, :].unsqueeze(3).to_broadcast([P, BT, NE, NE])
                    chain(f, 6, nc.vector.tensor_tensor(req[:, :, :, :], other, own, ALU.is_gt))
                    chain(f, 7, nc.vector.tensor_tensor(rgt[:, :, :, :], rgt[:, :, :, :], req[:, :, :, :], ALU.add))
                    chain(f, 8, nc.vector.tensor_reduce(rank[:, :, :], rgt[:, :, :, :], X, ALU.add))
                    chain(f, 9, nc.vector.scalar_tensor_tensor(rsel[:, :, :], rank[:, :, :], 1.5, rp[:, :, :], ALU.is_lt, ALU.mult))
                    nc.vector.tensor_reduce(rs2[:, :], rsel[:, :, :], X, ALU.add).then_inc(s["cw_ready"], 1)
                    dve.wait_ge(s["cw_ready"], f * 3 + 1)
                    nc.vector.reciprocal(rr2[:, :], rs2[:, :]).then_inc(s["cw_ready"], 1)
                    dve.wait_ge(s["cw_ready"], f * 3 + 2)
                    nc.vector.tensor_tensor(cw[par][:, :, :], rsel[:, :, :], rr2[:, :].unsqueeze(2).to_broadcast([P, BT, NE]),
                                            ALU.mult).then_inc(s["cw_ready"], 1)

                def n_lo(f, par):
                    dve.wait_ge(s["nh_ready"], f + 1)
                    nc.vector.tensor_tensor(nhl[par][:, 1, :], pf[:, 0, :], nhl[par][:, 0, :].bitcast(F32), ALU.subtract).then_inc(s["nl_ready"], 1)

                def hidden(k, e, par):
                    for c in range(HC):
                        n = k * (E1 * HC) + e * HC + c
                        dve.wait_ge(s["silu_ready"], n + 1)
                        if c == 0:
                            dve.wait_ge(s["y_ps"], k * E1 + e + 1)
                        nc.vector.tensor_tensor(hid[:, (par + e) % 2, c, :], ph[:, 2 * c + 1, :], silu[:, c, :],
                                                ALU.mult).then_inc(s["hid_ready"], 1)

                def accumulate(k, e, par, uses):
                    m = k * E1 + e
                    dve.wait_ge(s["y_ps"], m + 3)
                    dve.wait_ge(s["acc_ready"], m + 2)
                    if e == 0:
                        dve.wait_ge(s["cw_ready"], k * 3 + 3)
                        dve.wait_ge(acc_out[par], 16 * (uses + 1))
                    y = py[:, (par + e) % 2, :].rearrange("p (t c) -> p t c", c=C)
                    if e == NE:
                        nc.vector.tensor_tensor(acc[:, par], y, acc[:, par], ALU.add).then_inc(s["acc_ready"], 1)
                        return
                    so_far = xb if e == 0 else acc
                    for t in range(BT):
                        ins = nc.vector.scalar_tensor_tensor(acc[:, par, t, :], y[:, t, :], cw[par][:, t, e:e + 1], so_far[:, par, t, :],
                                                             ALU.mult, ALU.add)
                    ins.then_inc(s["acc_ready"], 1)

                def choose_round(n):
                    src, dst = score[(0, 1, 2, 1)[n]], score[(1, 2, 1, 2)[n]]
                    dve.wait_ge(s["round"], 2 * n + 1)
                    nc.vector.max(best[:, n, :], src[:, :]).then_inc(s["round"], 1)
                    dve.wait_ge(s["round"], 2 * n + 2)
                    nc.vector.match_replace(dst[:, :], best[:, n, :], src[:, :], -3e38).then_inc(s["round"], 1)

                def choose_scores():
                    nc.vector.memset(ones[:, :], 1.0).then_inc(s["ones_set"], 1)
                    dve.wait_ge(s["row_ps"], 1)
                    nc.vector.tensor_copy(score[0][:, :], pf[0:B, 0, 0:T]).then_inc(s["round"], 1)

                def choose_places():
                    r = 2 * (KEEP // 8) + 1
                    dve.wait_ge(s["round"], r)
                    nc.vector.tensor_tensor(chosen[:, :], score[0][:, :], score[2][:, :], ALU.not_equal).then_inc(s["round"], 1)
                    dve.wait_ge(s["round"], r + 1)
                    dve.wait_ge(s["ones_set"], 1)
                    nc.vector.tensor_tensor_scan(score[1][:, :], ones[:, :], chosen[:, :], 0.0, ALU.mult, ALU.add).then_inc(s["round"], 1)
                    dve.wait_ge(s["round"], r + 2)
                    nc.vector.tensor_tensor(place[:, :], score[1][:, :], chosen[:, :], ALU.mult).then_inc(s["place_done"], 1)

                def choose_gates():
                    nc.vector.tensor_reduce(glog[:, :, :], pf[:, 0, T:T + B * NT * 3].rearrange("p (b t c) -> p b c t", t=NT, c=3), X, ALU.add).then_inc(s["gchain"], 1)
                    dve.wait_ge(s["gchain"], 1)
                    nc.vector.tensor_reduce(gmx[:, :], glog[:, :, :], X, ALU.max).then_inc(s["gchain"], 1)
                    dve.wait_ge(s["gchain"], 2)
                    nc.vector.tensor_tensor(gd[:, :, :], glog[:, :, :], gmx[:, :].unsqueeze(2).to_broadcast([P, B, 3]), ALU.subtract).then_inc(s["gdiff"], 1)

                def choose_onehot():
                    dve.wait_ge(s["place_ps"], 1)
                    nc.vector.tensor_copy(place_t[:, :, :].rearrange("p b t -> p t b"), pf[:, 1, 0:B * NT].rearrange("p (t b) -> p t b", t=NT)).then_inc(s["place_t_done"], 1)
                    dve.wait_ge(s["place_t_done"], 1)
                    nc.vector.tensor_tensor(onehot[:, :, :], cst("iota").unsqueeze(1).to_broadcast([P, B * NT, KEEP]),
                                            place_t[:, :, :].rearrange("p b t -> p (b t)").unsqueeze(2).to_broadcast([P, B * NT, KEEP]),
                                            ALU.is_equal).then_inc(s["onehot_done"], 1)

                def choose(e):
                    if e == 2:
                        choose_scores()
                        choose_round(0)
                    if e == 3:
                        choose_round(1)
                        choose_gates()
                    if e == 4:
                        choose_round(2)
                        choose_round(3)
                    if e == 5:
                        choose_places()
                    if e == 6:
                        choose_onehot()
                    if e == 8:
                        dve.wait_ge(s["sel_ps"], 1)
                        nc.vector.tensor_copy(xs_tok[:, :], pf[:, 0, :]).then_inc(s["xs_ready"], 1)

                def body(j, last):
                    for par in range(2):
                        k = j * 2 + par
                        front = not (last and par)
                        f, fp, uses = k + 1, 1 - par, j + par
                        for e in range(E1):
                            hidden(k, e, par)
                            if e:
                                accumulate(k, e - 1, par, j)
                            if not front:
                                choose(e)
                                continue
                            if e == 0:
                                norm_apply(f, fp)
                            if e == 2:
                                x_lo(f, fp)
                            if e == 4:
                                if not last:
                                    norm_stats(f + 1, par, j + 1)
                                small_parts(f)
                            if e == 5:
                                small_norms(f)
                            if e == 6:
                                router(f)
                            if e == 7:
                                router_weights(f, fp)
                        if front:
                            n_lo(f, fp)
                        accumulate(k, E1 - 1, par, j)

                dve.sem_inc(s["hid_ready"], 2)
                dve.sem_inc(s["acc_ready"], 2)
                dve.sem_inc(s["nl_ready"], 1)
                norm_stats(0, 0, 0)
                dve.wait_ge(s["var"], BT)
                norm_stats(1, 1, 0)
                norm_apply(0, 0)
                x_lo(0, 0)
                small_parts(0)
                small_norms(0)
                router(0)
                router_weights(0, 0)
                n_lo(0, 0)
                with dve.Fori(0, NBLK // 2 - 1) as j:
                    body(j, False)
                body(NBLK // 2 - 1, True)
                dve.wait_ge(s["gexp"], 1)
                nc.vector.tensor_reduce(gsum[:, :], gex[:, :, :], X, ALU.add).then_inc(s["gchain"], 1)
                dve.wait_ge(s["gchain"], 3)
                nc.vector.reciprocal(grec[:, :], gsum[:, :]).then_inc(s["gchain"], 1)
                dve.wait_ge(s["gchain"], 4)
                nc.vector.tensor_tensor(gates[:, :, :], gex[:, :, :], grec[:, :].unsqueeze(2).to_broadcast([P, B, 3]), ALU.mult).then_inc(s["gchain"], 1)

            @block.tensor
            def _(pe):
                def x_transposes(f):
                    pe.wait_ge(s["xn_ready"], f * BT + BT)
                    pe.wait_ge(s["krt_ready"], f + 1)
                    for t in range(BT):
                        last = nc.tensor.transpose(pf[:, 1, t * P:(t + 1) * P], xn[:, t, :], ident)
                    last.then_inc(s["xT_ps"], 1)

                def small(f):
                    pe.wait_ge(s["xt_ready"], f + 1)
                    pe.wait_ge(s["nl_ready"], f + 1)
                    for t in range(BT):
                        if t == BT // 2:
                            pe.wait_ge(s["xl_ready"], f + 1)
                        last = nc.tensor.matmul(pa[:, t, 0:A_N], xt[:, t * P:(t + 1) * P], wa[:, :], start=True, stop=True)
                    last.then_inc(s["a_ps"], 1)

                def n_transposes(f):
                    pe.wait_ge(s["nq_ready"], f * 2 + 2)
                    pe.wait_ge(s["misc_ready"], f + 1)
                    pe.wait_ge(s["kr_ready"], f + 1)
                    for t in range(BT):
                        last = nc.tensor.transpose(pf[:, 0, t * P:(t + 1) * P], nqc[:, t, :], ident)
                    last.then_inc(s["nT_ps"], 1)
                    for t in range(BT):
                        last = nc.tensor.transpose(pf[0:ROPE, 1, t * P:(t + 1) * P], kr[:, t, :], ident)
                    last.then_inc(s["krT_ps"], 1)

                def up(k, e, par):
                    pe.wait_ge(s["w_lo"], e + 1)
                    for c in range(HC):
                        pe.wait_ge(s["hid_ready"], k * (E1 * HC) + e * HC + c + 1)
                        for j in range(2):
                            w = [w13[:, hl, e, j, c * P:(c + 1) * P] for hl in range(2)]
                            x = [xhl[par][:, hl, :] for hl in range(2)]
                            for n, (wi, xi) in enumerate([(0, 0), (0, 1), (1, 0)]):
                                last = nc.tensor.matmul(ph[:, 2 * c + j, :], w[wi], x[xi], start=(n == 0), stop=(n == 2))
                        last.then_inc(s["h_ps"], 1)

                def down(k, e, par):
                    m = k * E1 + e
                    pe.wait_ge(s["hid_ready"], m * HC + HC + 2)
                    pe.wait_ge(s["acc_ready"], m + 1)
                    for t in range(BT):
                        for c in range(HC):
                            last = nc.tensor.matmul(py[:, (par + e) % 2, t * C:(t + 1) * C], hid[:, (par + e) % 2, c, t * P:(t + 1) * P],
                                                    w2[:, e, c, :], start=(c == 0), stop=(c == HC - 1))
                    last.then_inc(s["y_ps"], 1)

                def choose(e):
                    if e == 1:
                        pe.wait_ge(s["misc_ready"], NBLK)
                        pe.wait_ge(s["nl_ready"], NBLK + 1)
                        pe.wait_ge(s["krt_ready"], NBLK + 1)
                        for t in range(NT):
                            imp = misc[:, :, 0:1].rearrange("p (b t) c -> p t (b c)", t=NT)[:, t, :]
                            nc.tensor.transpose(pf[0:B, 0, t * P:(t + 1) * P], imp, ident)
                        nc.tensor.matmul(pf[:, 0, T:T + B * NT * 3], cst("mean"), misc[:, :, 1:4], start=True, stop=True).then_inc(s["row_ps"], 1)
                    if e == 6:
                        pe.wait_ge(s["place_done"], 1)
                        for t in range(NT):
                            last = nc.tensor.transpose(pf[:, 1, t * B:(t + 1) * B], place[:, t * P:(t + 1) * P], ident[0:B, 0:B])
                        last.then_inc(s["place_ps"], 1)
                    if e == 8:
                        pe.wait_ge(s["onehot_done"], 1)
                        pe.wait_ge(s["xn_kept"], NBLK)
                        for n in range(B * KEEP // P):
                            for t in range(NT):
                                for q in range(P // KEEP):
                                    at = (n * (P // KEEP) + q) * NT + t
                                    last = nc.tensor.matmul(pf[q * KEEP:(q + 1) * KEEP, 0, n * P:(n + 1) * P], onehot[:, at, :], xn_all[:, at, :],
                                                            start=(t == 0), stop=(t == NT - 1))
                        last.then_inc(s["sel_ps"], 1)

                def choose_transposes():
                    pe.wait_ge(s["xs_ready"], 1)
                    for n in range(B * KEEP // P):
                        last = nc.tensor.transpose(pf[:, 1, n * P:(n + 1) * P], xs_tok[:, n * P:(n + 1) * P], ident)
                    last.then_inc(s["selT_ps"], 1)

                def body(j, last):
                    for par in range(2):
                        k = j * 2 + par
                        front = not (last and par)
                        f = k + 1
                        for e in range(E1):
                            up(k, e, par)
                            if e:
                                down(k, e - 1, par)
                            if not front:
                                choose(e)
                            if front and e == 1:
                                x_transposes(f)
                            if front and e == 3:
                                small(f)
                        if front:
                            n_transposes(f)
                        down(k, E1 - 1, par)
                        if not front:
                            choose_transposes()

                pe.sem_inc(s["y_ps"], 2)
                pe.wait_ge(const_in, 16)
                x_transposes(0)
                pe.wait_ge(s["wa_in"], 16 * 6)
                pe.wait_ge(s["wa_scaled"], 1)
                small(0)
                n_transposes(0)
                pe.wait_ge(s["w2_in"], 32)
                pe.wait_ge(s["xl_ready"], 1)
                with pe.Fori(0, NBLK // 2 - 1) as j:
                    body(j, False)
                body(NBLK // 2 - 1, True)


def load_grouped(eng, dst, rows, order, done):
    for g in range(G):
        for (at, width, src, first, per_head) in order:
            part = src.rearrange("p (h c) -> p h c", c=per_head)[:, g * HG:(g + 1) * HG, first:first + width]
            eng.dma_start(dst[rows, g, 0:QC].rearrange("p (i c) -> p i c", c=D)[:, :, at:at + width], part).then_inc(done, 16)


def attend(nc, a, sem, cst, gates, xsel, w, xt_d, nt_d, kr_d, res_d, ks_d, vs_d, out):
    ctx = ExitStack()
    with ctx:
        def sb(name, shape, dt=F32):
            return ctx.enter_context(nc.sbuf_tensor(name, shape, dt))

        def ps(name, shape, dt=F32):
            return ctx.enter_context(nc.psum_tensor(name, shape, dt))

        HT = HG * T
        EXPS = 2 * HG + 1
        TQ = T + P
        wq, wk, wn, wp, wsel = w["q"], w["k"], w["n"], w["proj"], w["sel"]
        NS = B * KEEP // P
        SQ = P // KEEP
        skcos = sb("s_kcos", [P, 2, HG, ROPE])
        sksin = sb("s_ksin", [P, 2, HG, ROPE])
        RING = 4
        sktok = sb("s_ktok", [P, RING, HG, D])
        svtok = sb("s_vtok", [P, RING, HG * VH])
        skt = sb("s_kt", [D, RING, SQ, HG, KEEP])
        xt = sb("a_xt", [P, 2, T], F32R)
        nt = sb("a_nt", [P, 2, T], F32R)
        nk = sb("a_nk", [P, 2, T], F32R)
        krt = sb("a_krt", [ROPE, T])
        res = sb("a_res", [P, NT, C])
        ot = sb("a_ot", [P, NT, C])
        gcur = sb("gcur", [P, 3])
        ks = [sb(f"ks{i}", [P, HG, KEEP]) for i in range(2)]
        vc = [sb(f"vc{i}", [P, VH]) for i in range(2)]
        ksb = sb("ksb", [D, HG, KEEP], BF16)
        vbd = [sb(f"vbd{i}", [P, HG, VH]) for i in range(2)]
        rcos = {x: sb(f"rcos_{x}", [P, NT, HG, ROPE]) for x in "qk"}
        rsin = {x: sb(f"rsin_{x}", [P, NT, HG, ROPE]) for x in "qk"}
        tok = {x: sb(f"tok_{x}", [P, NT, HG, ROPE]) for x in "qk"}
        qt = [sb(f"qt{i}", [P, HG, T]) for i in range(2)]
        kw = [sb(f"kw{i}", [P, HG, T]) for i in range(2)]
        k1 = [sb(f"k1{i}", [P, HG, T]) for i in range(2)]
        qb = sb("qb", [D, HG, T], BF16)
        kwb = sb("kwb", [D, HG, T], BF16)
        k1b = sb("k1b", [D, HG, T], BF16)
        v1 = [sb(f"v1{i}", [P, NT, HG * VH]) for i in range(G)]
        vw = [sb(f"vw{i}", [P, NT, HG * VH]) for i in range(2)]
        mtok = sb("mtok", [P, NT, P])
        junk = sb("junk", [P, 16, T], BF16)
        prob = [sb(f"prob{i}", [P, HG, 2, TQ]) for i in range(2)]
        prob2 = sb("prob2", [P, T])
        lden = sb("lden", [P, 3, T])
        rden = sb("rden", [P, 3, T])
        o1, o3, o2, o13 = (sb(n, [P, T]) for n in ("o1", "o3", "o2", "o13"))
        att = sb("att", [P, G, T])

        pj = ps("pj", [P, 2, 512])
        mx = [ps(f"mx{i}", [P, 512]) for i in range(2)]
        sc = ps("sc", [P, 2, 512])
        av = ps("av", [P, 2, T])
        dn = ps("dn", [P, 2, T])

        sel_bank = [x[:, :, :].rearrange("p a c -> p (a c)") for x in (av, dn)]

        names = ("sk_ps sk_used sk_nope sv_done sk_tok skT_ps skt_done mtok_zero rows_set xt_in nt_in nk_in kr_in res_in out_done "
                 "pq pkw kn_ps trq_ps trk_ps qn_ps kwn_ps mx_ps mT_ps sc_ps s2_ps av_ps av2_ps op_ps "
                 "rq rk q_copied k_copied q_add k_add kn_copied kr_copied k1b_ready ksb_ready qb_ready kwb_ready qt_ready kt_ready qn_rows kn_rows mrow "
                 "max_op exp_done masked vbd_ready g_ready log2 rec2 log13 rec13 n13 n2 att13 att_ready out_ready gate pgate").split()
        s = {n: sem("a_" + n) for n in names}
        ks_in = [sem(f"a_ks_in{i}") for i in range(2)]
        vc_in = [sem(f"a_vc_in{i}") for i in range(2)]
        sk_out = [sem(f"a_sk_out{i}") for i in range(RING)]
        sv_out = [sem(f"a_sv_out{i}") for i in range(RING)]
        ident = cst("ident")
        cos = cst("cos").rearrange("p (t c) -> p t c", c=ROPE)
        sin = cst("sin").rearrange("p (t a c) -> p t a c", a=2, c=HALF)
        out_v = out.rearrange("b (t p) c -> b p t c", p=P)
        res_v = res_d.rearrange("(b t p) c -> b p t c", t=NT, p=P)
        def nxt(b, g, d=1):
            return (b, g + d) if g + d < G else (b + 1, g + d - G)

        def stages(last, g):
            return not (last and g >= G - 1), not (last and g >= G - 2)

        def step(b, g):
            return b * G + g

        spread = {"start": (0, 1), "q": (2,), "k": (3, 4), "qt": (5, 6, 7), "kt": (8, 9), "next q": (10, 11),
                  "rough": (12,), "rough 3": (13,), "rough 5": (14, 15)}
        assert [u for us in spread.values() for u in us] == list(range(NS * G))

        def loop(eng, body):
            body(0, True, False)
            with eng.Fori(1, B - 1) as b:
                body(b, False, False)
            body(B - 1, False, True)

        with nc.Block() as block:
            @block.sync
            def _(sp):
                def load_latents(b):
                    sp.dma_start(nt[:, :, :].bitcast(F32), nt_d[b]).then_inc(s["nt_in"], 16)

                def load_plain_latents(b):
                    sp.dma_start(nk[:, :, :].bitcast(F32), nt_d[b]).then_inc(s["nk_in"], 16)

                def load_seq(b):
                    sp.dma_start(xt[:, :, :].bitcast(F32), xt_d[b]).then_inc(s["xt_in"], 16)
                    sp.dma_start(krt[:, :], kr_d[b]).then_inc(s["kr_in"], 16)

                def load_sel(b, g):
                    par = g % 2
                    sp.dma_start(ks[par][0:D, :, :].rearrange("p i c -> p (i c)"), ks_d[b][:, g * P:(g + 1) * P]).then_inc(ks_in[par], 16)
                    for i in range(HG):
                        at = (g * HG + i) * VH
                        sp.dma_start(vc[par][i * KEEP:(i + 1) * KEEP, :], vs_d[b][:, at:at + VH]).then_inc(vc_in[par], 16)

                def body(b, first, last):
                    for g in range(G):
                        n = nxt(b, g)
                        if g == 1:
                            if not first:
                                sp.wait_ge(s["out_ready"], b)
                                sp.dma_start(out_v[bass.ds(b - 1, 1)].rearrange("b p t c -> p (b t) c"), ot[:, :, :]).then_inc(s["out_done"], 16)
                            sp.dma_start(res[:, :, :], res_v[bass.ds(b, 1)].rearrange("b p t c -> p (b t) c")).then_inc(s["res_in"], 16)
                            if not last:
                                sp.wait_ge(s["pq"], step(b, G - 1) * NT + NT)
                                load_latents(b + 1)
                        if g == 2 and not last:
                            sp.wait_ge(s["qn_ps"], step(*n) + 1)
                            sp.wait_ge(s["kn_ps"], step(*n) + 1)
                            load_plain_latents(b + 1)
                            sp.wait_ge(s["kwn_ps"], step(*n) + 1)
                            sp.wait_ge(s["kr_copied"], b * 2 + 2)
                            load_seq(b + 1)
                        if not (last and g >= 2):
                            sp.wait_ge(s["s2_ps"], step(b, g) + 1)
                            sp.wait_ge(s["vbd_ready"], step(b, g) + 1)
                            load_sel(*nxt(b, g, 2))

                def store_selected(u):
                    n, g = divmod(u, G)
                    seqs, v = slice(n * SQ, (n + 1) * SQ), slice(g * HG * VH, (g + 1) * HG * VH)
                    sp.wait_ge(s["sv_done"], u + 1)
                    sp.dma_start(vs_d[seqs, :, v].rearrange("b k c -> (b k) c"), svtok[:, u % RING, :]).then_inc(sv_out[u % RING], 16)
                    sp.wait_ge(s["skt_done"], u + 1)
                    sp.dma_start(ks_d[seqs, :, g * P:(g + 1) * P].rearrange("b p c -> p b c"),
                                 skt[:, u % RING].rearrange("p q i c -> p q (i c)")).then_inc(sk_out[u % RING], 16)

                load_latents(0)
                load_plain_latents(0)
                load_seq(0)
                store_selected(0)
                sp.wait_ge(sv_out[0], 16)
                sp.wait_ge(sk_out[0], 16)
                load_sel(0, 0)
                for u in range(1, NS * G):
                    store_selected(u)
                for n in range(RING):
                    sp.wait_ge(sv_out[n], 16 * NS * G // RING)
                    sp.wait_ge(sk_out[n], 16 * NS * G // RING)
                load_sel(0, 1)
                loop(sp, body)
                sp.wait_ge(s["out_ready"], B)
                sp.dma_start(out_v[B - 1], ot[:, :, :]).then_inc(s["out_done"], 16)
                sp.wait_ge(s["out_done"], 16 * B)

            @block.tensor
            def _(pe):
                def project(w, x, g, t):
                    for n, (i, j) in enumerate([(0, 0), (1, 0), (0, 1)]):
                        last = nc.tensor.matmul(pj[:, t, 0:RC], x[:, j, t * P:(t + 1) * P], w[:, i, g, :], start=(n == 0), stop=(n == 2))
                    return last

                def plain(dst, which, x, g):
                    for n, (i, j) in enumerate([(0, 0), (0, 1), (1, 0)]):
                        last = nc.tensor.matmul(dst, wn[:, i, which, g * P:(g + 1) * P], x[:, j, :], start=(n == 0), stop=(n == 2))
                    return last

                def q_project(b, g, t):
                    if g == 0 and t == 0:
                        pe.wait_ge(s["nt_in"], 16 * (b + 1))
                    if t == 0:
                        pe.wait_ge(s["kt_ready"], (step(b, g) + 1) * 2)
                    else:
                        pe.wait_ge(s["kn_rows"], (step(b, g) + 1) * HG)
                    project(wq, nt, g, t).then_inc(s["pq"], 1)

                def k_nope(b, g):
                    if g == 0:
                        pe.wait_ge(s["nk_in"], 16 * (b + 1))
                    plain(sc[:, 1, 0:T], 1, nk, g).then_inc(s["kn_ps"], 1)

                def kw_project(b, g, tiles=range(NT)):
                    if g == 0:
                        pe.wait_ge(s["xt_in"], 16 * (b + 1))
                    for t in tiles:
                        done = step(b, g) * NT + t + 1
                        pe.wait_ge(s["rq"], done * 2)
                        pe.wait_ge(s["q_copied"], done)
                        project(wk, xt, g, t).then_inc(s["pkw"], 1)

                def transposes(x):
                    for i in range(HG // 2):
                        for t in range(NT):
                            last = nc.tensor.transpose(pj[:, 0, i * T + t * P:i * T + (t + 1) * P],
                                                       tok[x][:, t, 2 * i:2 * i + 2, :].rearrange("p i c -> p (i c)"), ident)
                    return last

                def q_transposes(b, g):
                    done = step(b, g) * NT
                    pe.wait_ge(s["q_add"], done + 2 * NT)
                    for t in range(NT):
                        pe.wait_ge(s["rk"], (done + t + 1) * 2)
                        pe.wait_ge(s["k_copied"], done + t + 1)
                        if t == 0:
                            transposes("q").then_inc(s["trq_ps"], 1)
                    plain(pj[:, 1, 0:T], 0, nk, g).then_inc(s["qn_ps"], 1)

                def kw_transposes(b, g):
                    st = step(b, g)
                    pe.wait_ge(s["k_add"], (st + 2) * NT)
                    pe.wait_ge(s["qt_ready"], st * 2 + 2)
                    transposes("k").then_inc(s["trk_ps"], 1)
                    pe.wait_ge(s["qn_rows"], st * HG + HG)
                    plain(pj[:, 1, 0:T], 2, xt, g).then_inc(s["kwn_ps"], 1)

                def rough(b, g, u):
                    st = step(b, g)
                    done = st * 17 + 4
                    if u == 0:
                        pe.wait_ge(s["qb_ready"], st + 1)
                        pe.wait_ge(s["ksb_ready"], st + 1)
                        pe.wait_ge(s["mrow"], st * HG + HG)
                    if u == 1:
                        pe.wait_ge(s["k1b_ready"], st + 1)
                        pe.wait_ge(s["kwb_ready"], st + 1)

                    def late(i, bank):
                        nc.tensor.matmul(bank[:, 0:T], qb[:, i, P:T], k1b[:, i, :], start=True, stop=True)
                        return nc.tensor.matmul(bank[:, T:2 * T], qb[:, i, P:T], kwb[:, i, :], start=True, stop=True)

                    def early(i, bank):
                        for j in range(2):
                            nc.tensor.matmul(bank[:, j * T:j * T + P], qb[:, i + j, 0:P], k1b[:, i + j, 0:P], start=True, stop=True)
                            last = nc.tensor.matmul(bank[:, j * T + P:j * T + T], qb[:, i + j, 0:P], kwb[:, i + j, 0:P], start=True, stop=True)
                        return last

                    if u == 0:
                        for t in range(NT):
                            for i in range(HG):
                                at = (t * HG + i) * KEEP
                                last = nc.tensor.matmul(mx[0][:, at:at + KEEP], qb[:, i, t * P:(t + 1) * P], ksb[:, i, :], start=True, stop=True)
                    if u == 1:
                        last = late(0, mx[1])
                    if u == 2:
                        pe.wait_ge(s["max_op"], done + 1)
                        last = early(0, mx[0])
                    if u == 3:
                        pe.wait_ge(s["max_op"], done + 3)
                        last = late(1, mx[1])
                    if u == 4:
                        pe.wait_ge(s["max_op"], done + 7)
                        last = late(2, mx[0])
                    if u == 5:
                        pe.wait_ge(s["max_op"], done + 9)
                        last = early(2, mx[1])
                    if u == 6:
                        pe.wait_ge(s["max_op"], done + 11)
                        last = late(3, mx[0])
                    last.then_inc(s["mx_ps"], 1)

                def max_transposes(b, g):
                    pe.wait_ge(s["max_op"], step(b, g) * 17 + 17 + 4)
                    for t in range(NT):
                        last = nc.tensor.transpose(mx[0][:, t * P:(t + 1) * P], mtok[:, t, :], ident)
                    last.then_inc(s["mT_ps"], 1)

                def scores(b, g, i, branches, next_copied=False):
                    st, par = step(b, g), g % 2
                    for j in branches:
                        if j == 0:
                            pe.wait_ge(s["mrow"], st * HG + HG + i + 1)
                        if i or j == 0:
                            pe.wait_ge(s["exp_done"], (st + 1) * EXPS + (2 * i + j - 1 if i else 0))
                        elif next_copied:
                            pe.wait_ge(s["kn_copied"], (st + 2) * HG)
                        k = (k1, kw)[j][par]
                        nc.tensor.matmul(sc[:, j, 0:T], k[:, i, 0:P], qt[par][:, i, :], start=True, stop=True)
                        nc.tensor.matmul(sc[:, j, T:TQ], k[:, i, P:T], qt[par][:, i, P:T], start=True, stop=True).then_inc(s["sc_ps"], 1)

                def selected_scores(b, g):
                    st, par = step(b, g), g % 2
                    pe.wait_ge(s["exp_done"], (st + 1) * EXPS + 2 * HG - 1)
                    pe.wait_ge(ks_in[par], (b * 2 + g // 2 + 1) * 16)
                    for i in range(HG):
                        last = nc.tensor.matmul(sc[i * KEEP:(i + 1) * KEEP, 0, 0:T], ks[par][:, i, :], qt[par][:, i, :], start=True, stop=True)
                    last.then_inc(s["s2_ps"], 1)

                def weigh(b, g, j, what):
                    st, par = step(b, g), g % 2
                    if what:
                        pe.wait_ge(s["n13"], st * 2 + 2)
                    else:
                        pe.wait_ge(s["log13"], st + 1)
                    v = vw[par] if j else v1[g]
                    for kt in range(NT):
                        for i in range(HG):
                            if kt == 0 and j == 0 and not what:
                                pe.wait_ge(s["masked"], st * 4 + i + 1)
                            left = v[:, kt, i * VH:(i + 1) * VH] if what else cst("ones")
                            dst = (av if what else dn)[i * VH:(i + 1) * VH, j, kt * P:T]
                            right = prob[par][:, i, j, 0:T] if kt == 0 else prob[par][:, i, j, T:TQ]
                            last = nc.tensor.matmul(dst, left, right, start=(kt == 0), stop=(kt == NT - 1))
                    return last

                def weigh_selected(b, g, prep):
                    st, par = step(b, g), g % 2
                    if prep:
                        pe.wait_ge(s["max_op"], (st + 1) * 17 + 15 + 4)
                    pe.wait_ge(s["exp_done"], (st + 2) * EXPS)
                    pe.wait_ge(s["vbd_ready"], st + 1)
                    nc.tensor.matmul(mx[1][:, 0:T], vbd[par][:, :, :].rearrange("p i c -> p (i c)"), prob2[:, :], start=True, stop=True)
                    nc.tensor.matmul(mx[1][:, T:2 * T], cst("block"), prob2[:, :], start=True, stop=True).then_inc(s["av2_ps"], 1)

                def out_project(b):
                    pe.wait_ge(s["att_ready"], b * G + G + 1)
                    for t in range(NT):
                        for g in range(G):
                            last = nc.tensor.matmul(mx[1][:, t * C:(t + 1) * C], att[:, g, t * P:(t + 1) * P], wp[:, g, :],
                                                    start=(g == 0), stop=(g == G - 1))
                    last.then_inc(s["op_ps"], 1)

                def body(b, first, last):
                    for g in range(G):
                        n, m = nxt(b, g), nxt(b, g, 2)
                        prep, ahead = stages(last, g)
                        scores(b, g, 0, range(2), prep)
                        if prep:
                            q_transposes(*n)
                        scores(b, g, 1, range(2))
                        if prep:
                            kw_transposes(*n)
                        if not (first and g == 0):
                            pe.wait_ge(s["n2"], step(b, g))
                        if g == 1 and not first:
                            out_project(b - 1)
                        scores(b, g, 2, range(2))
                        if ahead:
                            q_project(*m, 0)
                        if prep:
                            rough(*n, 0)
                        scores(b, g, 3, [0])
                        if g == 1 and not first:
                            pe.wait_ge(s["out_ready"], b)
                        if prep:
                            rough(*n, 1)
                            rough(*n, 2)
                        scores(b, g, 3, [1])
                        if ahead:
                            q_project(*m, 1)
                        if prep:
                            rough(*n, 3)
                        selected_scores(b, g)
                        if prep:
                            rough(*n, 4)
                        if ahead:
                            pe.wait_ge(s["exp_done"], (step(b, g) + 1) * EXPS + 2 * HG)
                            k_nope(*m)
                        weigh(b, g, 0, False)
                        if prep:
                            rough(*n, 5)
                        weigh(b, g, 0, True)
                        weigh(b, g, 1, True)
                        if prep:
                            rough(*n, 6)
                        if ahead:
                            kw_project(*m)
                        weigh(b, g, 1, False).then_inc(s["av_ps"], 1)
                        if prep:
                            max_transposes(*n)
                        weigh_selected(b, g, prep)

                def select_project(u):
                    n, g = divmod(u, G)
                    if u >= 2:
                        pe.wait_ge(s["sk_used"], 2 * (u - 1))
                        pe.wait_ge(s["sk_nope"], u - 1)
                        pe.wait_ge(s["sv_done"], u - 1)
                    nc.tensor.matmul(sel_bank[u % 2], xsel[:, n * P:(n + 1) * P], wsel[:, g, :], start=True, stop=True).then_inc(s["sk_ps"], 1)

                def select_transposes(u):
                    pe.wait_ge(s["sk_tok"], u + 1)
                    pe.wait_ge(s["sk_nope"], u + 1)
                    if u:
                        pe.wait_ge(s["skt_done"], u)
                    for i in range(HG):
                        last = nc.tensor.transpose(sc[0:D, 0, i * P:(i + 1) * P], sktok[:, u % RING, i, :], ident)
                    last.then_inc(s["skT_ps"], 1)

                def selected(stage):
                    for u in spread[stage]:
                        select_project(u)
                        if u >= 2:
                            select_transposes(u - 2)

                selected("start")
                for t in range(NT):
                    q_project(0, 0, t)
                selected("q")
                kw_project(0, 0)
                k_nope(0, 0)
                selected("k")
                q_transposes(0, 0)
                pe.wait_ge(s["kn_copied"], HG)
                k_nope(0, 1)
                selected("qt")
                kw_transposes(0, 0)
                selected("kt")
                for t in range(NT):
                    q_project(0, 1, t)
                selected("next q")
                kw_project(0, 1)
                for u in range(7):
                    rough(0, 0, u)
                    if u == 2:
                        selected("rough")
                    if u == 4:
                        selected("rough 3")
                selected("rough 5")
                select_transposes(NS * G - 2)
                max_transposes(0, 0)
                select_transposes(NS * G - 1)
                pe.wait_ge(s["sk_used"], 2 * NS * G)
                pe.wait_ge(s["sv_done"], NS * G)
                pe.wait_ge(s["skt_done"], NS * G)
                pe.wait_ge(s["rows_set"], 6)
                loop(pe, body)
                out_project(B - 1)

            @block.scalar
            def _(act):
                def copies(b, g, t, rotated, done, v):
                    act.wait_ge(s[rotated], (step(b, g) * NT + t + 1) * 2)
                    nc.scalar.copy(v[:, t, :], pj[:, t, QR:RC]).then_inc(s[done], 1)

                def q_copies(b, g, t):
                    copies(b, g, t, "rq", "q_copied", v1[g])

                def k_copies(b, g):
                    for t in range(NT):
                        copies(b, g, t, "rk", "k_copied", vw[g % 2])

                def transposed(b, g, ready, done, exact):
                    act.wait_ge(s[ready], step(b, g) + 1)
                    heads = exact[g % 2][0:ROPE].rearrange("p (a two) c -> p two a c", two=2)
                    for odd in range(2):
                        nc.scalar.copy(heads[:, odd], pj[odd * ROPE:(odd + 1) * ROPE, 0, :].rearrange("p (a c) -> p a c", c=T)).then_inc(s[done], 1)

                def logarithm2(b, g):
                    act.wait_ge(s["av2_ps"], step(b, g) + 1)
                    nc.scalar.activation(lden[:, 2, :], mx[1][:, T:2 * T], ACT.Ln).then_inc(s["log2"], 1)

                def reciprocal2(b, g):
                    act.wait_ge(s["log2"], step(b, g) + 1)
                    nc.scalar.activation(rden[:, 2, :], lden[:, 2, :], ACT.Exp, scale=-1.0).then_inc(s["rec2"], 1)

                def reciprocals13(b, g):
                    act.wait_ge(s["av_ps"], step(b, g) + 1)
                    nc.scalar.activation(lden[:, 0:2, :], dn[:, :, :], ACT.Ln).then_inc(s["log13"], 1)
                    act.wait_ge(s["log13"], step(b, g) + 2)
                    nc.scalar.activation(rden[:, 0:2, :], lden[:, 0:2, :], ACT.Exp, scale=-1.0).then_inc(s["rec13"], 1)

                def latent_rows(b, g):
                    act.wait_ge(s["kn_ps"], step(b, g) + 1)
                    for i in range(HG):
                        nc.scalar.copy(k1[g % 2][ROPE:D, i, :], sc[i * NOPE:(i + 1) * NOPE, 1, 0:T]).then_inc(s["kn_copied"], 1)

                def max_rows(b, g):
                    act.wait_ge(s["mT_ps"], step(b, g) + 1)
                    for i in range(HG):
                        nc.scalar.copy(qt[g % 2][D:P, i, :], mx[0][i * 32:(i + 1) * 32, 0:T]).then_inc(s["mrow"], 1)

                def exps(b, g, i):
                    for j in range(2):
                        act.wait_ge(s["sc_ps"], step(b, g) * 2 * HG + 2 * i + j + 1)
                        nc.scalar.activation(prob[g % 2][:, i, j, :], sc[:, j, 0:TQ], ACT.Exp, scale=SCALE).then_inc(s["exp_done"], 1)

                def exp_selected(b, g):
                    act.wait_ge(s["s2_ps"], step(b, g) + 1)
                    nc.scalar.activation(prob2[:, :], sc[:, 0, 0:T], ACT.Exp, scale=SCALE).then_inc(s["exp_done"], 1)

                def body(b, first, last):
                    for g in range(G):
                        n, m = nxt(b, g), nxt(b, g, 2)
                        before = (b, g - 1) if g else (b - 1, G - 1)
                        prep, ahead = stages(last, g)
                        if not (first and g == 0):
                            logarithm2(*before)
                            reciprocal2(*before)
                        exps(b, g, 0)
                        if prep:
                            transposed(*n, "trq_ps", "qt_ready", qt)
                        exps(b, g, 1)
                        if prep:
                            transposed(*n, "trk_ps", "kt_ready", kw)
                        exps(b, g, 2)
                        if not (first and g == 0):
                            reciprocals13(*before)
                        exps(b, g, 3)
                        if ahead:
                            q_copies(*m, 0)
                        exp_selected(b, g)
                        if ahead:
                            latent_rows(*m)
                            q_copies(*m, 1)
                        if prep:
                            max_rows(*n)
                        if ahead:
                            k_copies(*m)

                nc.scalar.preload_act_table_set("natural_log_exp_and_others")
                act.sem_inc(s["kt_ready"], 2)
                act.sem_inc(s["mrow"], 4)
                act.sem_inc(s["exp_done"], EXPS)
                act.sem_inc(s["log13"], 1)
                def select_copies(u):
                    par = u % 2
                    act.wait_ge(s["sk_used"], 2 * (u + 1))
                    if u >= RING:
                        act.wait_ge(s["skT_ps"], u - RING + 1)
                        act.wait_ge(sv_out[u % RING], 16 * (u // RING))
                    nc.scalar.copy(sktok[:, u % RING, :, ROPE:D], sel_bank[par][:, 0:QC].rearrange("p (i c) -> p i c", c=D)[:, :, ROPE:D]).then_inc(s["sk_nope"], 1)
                    nc.scalar.copy(svtok[:, u % RING, :], sel_bank[par][:, QC:GC]).then_inc(s["sv_done"], 1)

                def select_transposed(u):
                    act.wait_ge(s["skT_ps"], u + 1)
                    if u >= RING:
                        act.wait_ge(sk_out[u % RING], 16 * (u // RING))
                    src = sc[0:D, 0, :].rearrange("p (i q c) -> p q i c", i=HG, c=KEEP)
                    nc.scalar.copy(skt[:, u % RING], src).then_inc(s["skt_done"], 1)

                def selected(stage):
                    for u in spread[stage]:
                        select_copies(u)
                        if u >= 2:
                            select_transposed(u - 2)

                selected("start")
                for t in range(NT):
                    q_copies(0, 0, t)
                selected("q")
                k_copies(0, 0)
                latent_rows(0, 0)
                selected("k")
                transposed(0, 0, "trq_ps", "qt_ready", qt)
                latent_rows(0, 1)
                selected("qt")
                transposed(0, 0, "trk_ps", "kt_ready", kw)
                selected("kt")
                for t in range(NT):
                    q_copies(0, 1, t)
                selected("next q")
                k_copies(0, 1)
                for stage in ("rough", "rough 3", "rough 5"):
                    selected(stage)
                select_transposed(NS * G - 2)
                max_rows(0, 0)
                select_transposed(NS * G - 1)
                loop(act, body)
                logarithm2(B - 1, G - 1)
                reciprocal2(B - 1, G - 1)
                reciprocals13(B - 1, G - 1)

            @block.vector
            def _(dve):
                def rotate(b, g, t, x, ready, done, added):
                    tile = step(b, g) * NT + t
                    dve.wait_ge(s[ready], tile + 1)
                    dve.wait_ge(s[added], tile + 1)
                    src = pj[:, t, 0:QR].rearrange("p (i c) -> p i c", c=ROPE)
                    nc.vector.tensor_tensor(rcos[x][:, t], src, cos[:, t].unsqueeze(1).to_broadcast([P, HG, ROPE]), ALU.mult).then_inc(s[done], 1)
                    nc.vector.tensor_tensor(rsin[x][:, t].rearrange("p i (a c) -> p i a c", a=2),
                                            src.rearrange("p i (a c) -> p i a c", a=2)[:, :, ::-1, :],
                                            sin[:, t].unsqueeze(1).to_broadcast([P, HG, 2, HALF]), ALU.mult).then_inc(s[done], 1)

                def rotate_q(b, g, tiles=range(NT)):
                    for t in tiles:
                        rotate(b, g, t, "q", "pq", "rq", "q_add")

                def rotate_k(b, g):
                    for t in range(NT):
                        rotate(b, g, t, "k", "pkw", "rk", "k_add")

                def cast(b, g, exact, rounded, done):
                    nc.vector.tensor_copy(rounded[:, :, :], exact[g % 2][0:D]).then_inc(s[done], 1)

                def q_plain_rows(b, g):
                    dve.wait_ge(s["qn_ps"], step(b, g) + 1)
                    for i in range(HG):
                        nc.vector.tensor_copy(qt[g % 2][ROPE:D, i, :], pj[i * NOPE:(i + 1) * NOPE, 1, 0:T]).then_inc(s["qn_rows"], 1)

                def kw_plain_rows(b, g):
                    dve.wait_ge(s["kwn_ps"], step(b, g) + 1)
                    for i in range(HG):
                        nc.vector.tensor_copy(kw[g % 2][ROPE:D, i, :], pj[i * NOPE:(i + 1) * NOPE, 1, 0:T]).then_inc(s["kn_rows"], 1)

                def q_cast(b, g):
                    dve.wait_ge(s["qt_ready"], step(b, g) * 2 + 2)
                    dve.wait_ge(s["qn_rows"], step(b, g) * HG + HG)
                    cast(b, g, qt, qb, "qb_ready")

                def kw_cast(b, g):
                    dve.wait_ge(s["kt_ready"], step(b, g) * 2 + 4)
                    dve.wait_ge(s["kn_rows"], (step(b, g) + 2) * HG)
                    cast(b, g, kw, kwb, "kwb_ready")

                def latent_keys(b, g):
                    st = step(b, g)
                    dve.wait_ge(s["kn_ps"], st + 1)
                    if g < 2:
                        dve.wait_ge(s["kr_in"], 16 * (b + 1))
                        nc.vector.tensor_copy(k1[g][0:ROPE, :, :], krt[:, :].unsqueeze(1).to_broadcast([ROPE, HG, T])).then_inc(s["kr_copied"], 1)
                        dve.wait_ge(s["kr_copied"], b * 2 + g + 1)
                    dve.wait_ge(s["kn_copied"], st * HG + HG)
                    nc.vector.tensor_copy(k1b[:, :, :], k1[g % 2][0:D]).then_inc(s["k1b_ready"], 1)

                def selected_cast(b, g):
                    dve.wait_ge(ks_in[g % 2], (b * 2 + g // 2 + 1) * 16)
                    nc.vector.tensor_copy(ksb[:, :, :], ks[g % 2][0:D]).then_inc(s["ksb_ready"], 1)

                def maxima(b, g, part):
                    st = step(b, g)
                    done = [(0, 1, 7, 11)[part]]

                    def row_max(bank, at, width, t, i, branch):
                        n = done[0] - 1
                        nc.vector.tensor_tensor_reduce(out=junk[:, n, 0:width], in0=bank[:, at:at + width],
                                                       in1=cst("mask")[:, T - width:T], scale=1.0, scalar=-3e38, op0=ALU.add, op1=ALU.max,
                                                       accum_out=mtok[:, t, 32 * i + branch:32 * i + branch + 1]).then_inc(s["max_op"], 1)
                        done[0] += 1

                    def late(u, i, bank):
                        wait_alone(dve, s["mx_ps"], st * 7 + u + 1, s["gate"])
                        row_max(bank, 0, T, 1, i, BR1)
                        row_max(bank, T, T, 1, i, BR3)

                    def early(u, i, bank):
                        wait_alone(dve, s["mx_ps"], st * 7 + u + 1, s["gate"])
                        for j in range(2):
                            row_max(bank, j * T, P, 0, i + j, BR1)
                            row_max(bank, j * T + P, P, 0, i + j, BR3)

                    if part == 0:
                        dve.wait_ge(s["max_op"], st * 17 + 4)
                        dve.wait_ge(s["mx_ps"], st * 7 + 1)
                        nc.vector.tensor_reduce(mtok[:, :, :].rearrange("p t (i c) -> p t i c", c=32)[:, :, :, BR2],
                                                mx[0][:, 0:NT * HG * KEEP].rearrange("p (t i c) -> p t i c", i=HG, c=KEEP), X, ALU.max).then_inc(s["max_op"], 1)
                    if part == 1:
                        late(1, 0, mx[1])
                        early(2, 0, mx[0])
                    if part == 2:
                        late(3, 1, mx[1])
                        late(4, 2, mx[0])
                    if part == 3:
                        early(5, 2, mx[1])
                        late(6, 3, mx[0])

                def normalise2(b, g):
                    if g == 0:
                        nc.vector.tensor_copy(gcur[:, :], gates[:, bass.ds(b, 1), :].rearrange("p b c -> p (b c)")).then_inc(s["g_ready"], 1)
                        dve.wait_ge(s["g_ready"], b + 1)
                    dve.wait_ge(s["rec2"], step(b, g) + 1)
                    dve.wait_ge(s["att_ready"], step(b, g) + 1)
                    nc.vector.scalar_tensor_tensor(o2[:, :], mx[1][:, 0:T], gcur[:, 1:2], rden[:, 2, :], ALU.mult, ALU.mult).then_inc(s["n2"], 1)

                def normalise13(b, g):
                    dve.wait_ge(s["rec13"], step(b, g) + 1)
                    nc.vector.scalar_tensor_tensor(o1[:, :], av[:, 0, :], gcur[:, 0:1], rden[:, 0, :], ALU.mult, ALU.mult).then_inc(s["n13"], 1)
                    nc.vector.scalar_tensor_tensor(o3[:, :], av[:, 1, :], gcur[:, 2:3], rden[:, 1, :], ALU.mult, ALU.mult).then_inc(s["n13"], 1)

                def finish(b, first_out):
                    dve.wait_ge(s["op_ps"], b + 1)
                    dve.wait_ge(s["res_in"], 16 * (b + 1))
                    if not first_out:
                        dve.wait_ge(s["out_done"], 16 * b)
                    nc.vector.tensor_tensor(ot[:, :, :], mx[1][:, 0:NT * C].rearrange("p (t c) -> p t c", c=C), res[:, :, :], ALU.add).then_inc(s["out_ready"], 1)

                def body(b, first, last):
                    for g in range(G):
                        n, m = nxt(b, g), nxt(b, g, 2)
                        before = (b, g - 1) if g else (b - 1, G - 1)
                        prep, ahead = stages(last, g)
                        if not (first and g == 0):
                            normalise2(*before)
                        if prep:
                            q_plain_rows(*n)
                            selected_cast(*n)
                            q_cast(*n)
                            kw_plain_rows(*n)
                            kw_cast(*n)
                        if g == 1 and not first:
                            finish_at(b)
                        if prep:
                            maxima(*n, 0)
                        if ahead:
                            rotate_q(*m, [0])
                        if prep:
                            maxima(*n, 1)
                        if not (first and g == 0):
                            normalise13(*before)
                        if prep:
                            maxima(*n, 2)
                        if ahead:
                            rotate_q(*m, [1])
                        if prep:
                            maxima(*n, 3)
                        if ahead:
                            rotate_k(*m)
                            latent_keys(*m)

                def finish_at(b):
                    finish(b - 1, isinstance(b, int) and b == 1)

                dve.sem_inc(s["max_op"], 4)
                dve.sem_inc(s["kn_rows"], HG)
                dve.sem_inc(s["n13"], 2)

                def select_rotate(u):
                    par = u % 2
                    dve.wait_ge(s["sk_ps"], u + 1)
                    if u >= 2:
                        dve.wait_ge(s["sk_tok"], u - 1)
                    src = sel_bank[par][:, 0:QC].rearrange("p (i c) -> p i c", c=D)[:, :, 0:ROPE]
                    nc.vector.tensor_tensor(skcos[:, par], src, cst("scos").unsqueeze(1).to_broadcast([P, HG, ROPE]), ALU.mult).then_inc(s["sk_used"], 1)
                    nc.vector.tensor_tensor(sksin[:, par].rearrange("p i (a c) -> p i a c", a=2),
                                            src.rearrange("p i (a c) -> p i a c", a=2)[:, :, ::-1, :],
                                            cst("ssin").rearrange("p (a c) -> p a c", a=2).unsqueeze(1).to_broadcast([P, HG, 2, HALF]),
                                            ALU.mult).then_inc(s["sk_used"], 1)

                def minus_ones(i):
                    for j, k in enumerate((k1, kw)):
                        nc.vector.tensor_copy(k[i][D:P].rearrange("p i c -> p (i c)"),
                                              cst("mrow")[D:P, j:j + 1].to_broadcast([P - D, HT])).then_inc(s["rows_set"], 1)
                    nc.vector.tensor_copy(ks[i][D:P].rearrange("p i c -> p (i c)"),
                                          cst("mrow")[D:P, BR2:BR2 + 1].to_broadcast([P - D, HG * KEEP])).then_inc(s["rows_set"], 1)

                def selected(stage):
                    for u in spread[stage]:
                        select_rotate(u)

                selected("start")
                rotate_q(0, 0)
                nc.vector.memset(mtok[:, :, :], 0.0).then_inc(s["mtok_zero"], 1)
                selected("q")
                rotate_k(0, 0)
                selected("k")
                latent_keys(0, 0)
                q_plain_rows(0, 0)
                selected("qt")
                q_cast(0, 0)
                kw_plain_rows(0, 0)
                selected("kt")
                kw_cast(0, 0)
                rotate_q(0, 1)
                selected("next q")
                minus_ones(0)
                selected_cast(0, 0)
                rotate_k(0, 1)
                dve.wait_ge(s["mtok_zero"], 1)
                maxima(0, 0, 0)
                maxima(0, 0, 1)
                selected("rough")
                maxima(0, 0, 2)
                selected("rough 3")
                maxima(0, 0, 3)
                selected("rough 5")
                minus_ones(1)
                latent_keys(0, 1)
                loop(dve, body)
                normalise2(B - 1, G - 1)
                normalise13(B - 1, G - 1)
                finish(B - 1, False)

            @block.gpsimd
            def _(pool):
                def add(b, g, x, parts, done):
                    for t in range(NT):
                        pool.wait_ge(s[parts], (step(b, g) * NT + t + 1) * 2)
                        nc.gpsimd.tensor_tensor(tok[x][:, t], rcos[x][:, t], rsin[x][:, t], ALU.add).then_inc(s[done], 1)

                def mask(b, g, i):
                    wait_alone(pool, s["exp_done"], (step(b, g) + 1) * EXPS + 2 * i + 2, s["pgate"])
                    blocks = prob[g % 2][:, i, :, :]
                    at = [blocks[:, :, 0:P], blocks[:, :, T:TQ]]
                    for j in range(2):
                        ins = nc.gpsimd.affine_select(out=at[j], in_=at[j], compare_op=ALU.is_ge, fill=0.0, base=0,
                                                      pattern=[[0, 2], [1, P]], channel_multiplier=-1)
                    ins.then_inc(s["masked"], 1)

                def blocks(b, g):
                    pool.wait_ge(vc_in[g % 2], (b * 2 + g // 2 + 1) * 64)
                    nc.gpsimd.tensor_tensor(vbd[g % 2][:, :, :], vc[g % 2][:, :].unsqueeze(1).to_broadcast([P, HG, VH]),
                                            cst("block").rearrange("p (i c) -> p i c", c=VH), ALU.mult).then_inc(s["vbd_ready"], 1)

                def branches(b, g):
                    st = step(b, g)
                    pool.wait_ge(s["n13"], st * 2 + 4)
                    nc.gpsimd.tensor_tensor(o13[:, :], o1[:, :], o3[:, :], ALU.add).then_inc(s["att13"], 1)
                    pool.wait_ge(s["att13"], st + 1)
                    pool.wait_ge(s["n2"], st + 1)
                    if g == 0 and not (isinstance(b, int) and b == 0):
                        pool.wait_ge(s["op_ps"], b)
                    nc.gpsimd.tensor_tensor(att[:, g, :], o13[:, :], o2[:, :], ALU.add).then_inc(s["att_ready"], 1)

                def body(b, first, last):
                    for g in range(G):
                        n, m = nxt(b, g), nxt(b, g, 2)
                        before = (b, g - 1) if g else (b - 1, G - 1)
                        prep, ahead = stages(last, g)
                        mask(b, g, 0)
                        mask(b, g, 1)
                        mask(b, g, 2)
                        blocks(b, g)
                        mask(b, g, 3)
                        if not (first and g == 0):
                            branches(*before)
                        if ahead:
                            add(*m, "q", "rq", "q_add")
                            add(*m, "k", "rk", "k_add")

                pool.sem_inc(s["q_add"], NT)
                pool.sem_inc(s["k_add"], NT)
                pool.sem_inc(s["att_ready"], 1)

                def selected(stage):
                    for u in spread[stage]:
                        pool.wait_ge(s["sk_used"], 2 * (u + 1))
                        if u >= RING:
                            pool.wait_ge(s["skT_ps"], u - RING + 1)
                        nc.gpsimd.tensor_tensor(sktok[:, u % RING, :, 0:ROPE], skcos[:, u % 2], sksin[:, u % 2], ALU.add).then_inc(s["sk_tok"], 1)

                selected("start")
                add(0, 0, "q", "rq", "q_add")
                selected("q")
                add(0, 0, "k", "rk", "k_add")
                for stage in ("k", "qt", "kt"):
                    selected(stage)
                add(0, 1, "q", "rq", "q_add")
                selected("next q")
                add(0, 1, "k", "rk", "k_add")
                for stage in ("rough", "rough 3", "rough 5"):
                    selected(stage)
                loop(pool, body)
                branches(B - 1, G - 1)


_INS = ["L0_attn_x", "L0_attn_w_cq", "L0_attn_g_qnorm", "L0_attn_w_dq_nope", "L0_attn_w_dq_rope", "L0_attn_w_ckv", "L0_attn_g_kvnorm",
        "L0_attn_w_dk_nope", "L0_attn_w_dv", "L0_attn_w_krope", "L0_attn_w_imp", "L0_attn_w_selk", "L0_attn_w_selv", "L0_attn_w_wink",
        "L0_attn_w_winv", "L0_attn_w_gate", "L0_attn_w_proj", "L0_ffn_w_router", "L0_ffn_w1", "L0_ffn_w3", "L0_ffn_w2", "L0_ffn_sw1",
        "L0_ffn_sw3", "L0_ffn_sw2"]


def kernel(**inputs):
    import numpy as _np
    import concourse.bacc as _bacc
    from concourse import mybir as _mybir
    from concourse.bass_utils import run_bass_kernel_spmd as _run

    nc = _bacc.Bacc("TRN2", target_bir_lowering=False, num_devices=1)
    arrays, args = {}, {}
    for name in _INS:
        x = _np.ascontiguousarray(inputs[name])
        arrays[f"in_{name}"] = x
        args[name] = nc.dram_tensor(f"in_{name}", x.shape, _mybir.dt.from_np(x.dtype), kind="ExternalInput").ap()
    arrays["in_constants"] = constants(_np)
    args["constants"] = nc.dram_tensor("in_constants", (P, NCONST), F32, kind="ExternalInput").ap()
    out = nc.dram_tensor("out_0", (B, T, C), F32, kind="ExternalOutput").ap()
    layer_kernel(nc, args, out)
    r = _run(nc, [arrays], core_ids=[0])
    return r.results[0]["out_0"]
```
